# Optimizing a Trainium2 kernel written in Bass

```python
import numpy as np
import jax
import jax.numpy as jnp

def _softmax(x, axis=-1):
    return jax.nn.softmax(x, axis=axis)

def _gelu(x):
    return jax.nn.gelu(x, approximate=True)

def _silu(x):
    return jax.nn.silu(x)

def _sigmoid(x):
    return jax.nn.sigmoid(x)

def _layernorm(x, axis=-1, eps=1e-05):
    m = jnp.mean(x, axis=axis, keepdims=True)
    v = jnp.var(x, axis=axis, keepdims=True)
    return (x - m) / jnp.sqrt(v + eps)

def _scatter_add(tgt, idx, src, axis=0):
    return tgt.at[idx].add(src)

def _segment_sum(src, seg, n):
    return jax.ops.segment_sum(src, seg, n)
kernel_name = 'mk_audio_tower_d1_tok_audfeat512_r4_d1e34b'

def setup_inputs(seed: int=0):
    np.random.seed(seed)
    _w = jnp.asarray

    def _rec_inputs():
        import jax
        import jax.numpy as jnp
        _rk = jax.random.key(seed)
        x = -0.000548836 + 1.0005 * jax.random.normal(jax.random.fold_in(_rk, 1), (32, 256, 23), jnp.float32)
        return x
    x = _rec_inputs()

    def _L0_tok_setup():
        import jax, jax.numpy as jnp
        import numpy as np
        INPUT_DIM = 23
        OUTPUT_DIM = 128
        CONTEXT = 5
        DILATION = 1
        BN_EPS = 1e-05
        key = jax.random.key(seed)
        k1, k2, k3 = jax.random.split(key, 3)
        B, T = (32, 1024)
        x = jax.random.normal(k1, (B, T, INPUT_DIM), dtype=jnp.float32)
        fan_in = INPUT_DIM * CONTEXT
        bound = 1.0 / np.sqrt(fan_in)
        W = jax.random.uniform(k2, (OUTPUT_DIM, fan_in), minval=-bound, maxval=bound, dtype=jnp.float32)
        b = jax.random.uniform(k3, (OUTPUT_DIM,), minval=-bound, maxval=bound, dtype=jnp.float32)
        gamma = jnp.ones((OUTPUT_DIM,), dtype=jnp.float32)
        beta = jnp.zeros((OUTPUT_DIM,), dtype=jnp.float32)
        return {'x': x, 'W': W, 'b': b, 'gamma': gamma, 'beta': beta}
    _L0_tok_all = _L0_tok_setup()
    _L0_tok_in = {k: v for k, v in _L0_tok_all.items() if k in ('W', 'b', 'gamma', 'beta')}
    del _L0_tok_all

    def _L0_attn_setup():
        import jax, jax.numpy as jnp
        import numpy as np
        D_MODEL = 128
        N_HEADS = 8
        DH = D_MODEL // N_HEADS
        Q_PROJ = D_MODEL // 2
        KV_PROJ = 2 * D_MODEL // 3
        ROPE_DIM = D_MODEL // 8
        R = ROPE_DIM // N_HEADS
        THETA = 10000.0
        EPS = 1e-05
        B, S = (2, 512)

        def layernorm(x, g, b):
            m = jnp.mean(x, axis=-1, keepdims=True)
            v = jnp.var(x, axis=-1, keepdims=True)
            return (x - m) * jax.lax.rsqrt(v + EPS) * g + b

        def rope_cos_sin(seq_len, dtype):
            inv_freq = THETA ** (-jnp.arange(0, R, 2, dtype=jnp.float32) / R)
            ang = jnp.arange(seq_len, dtype=jnp.float32)[:, None] * inv_freq
            cos = jnp.concatenate([jnp.cos(ang), jnp.cos(ang)], axis=-1)
            sin = jnp.concatenate([jnp.sin(ang), jnp.sin(ang)], axis=-1)
            return (cos.astype(dtype), sin.astype(dtype))

        def apply_rope(x, cos, sin):
            x1, x2 = jnp.split(x, 2, axis=-1)
            rot = jnp.concatenate([-x2, x1], axis=-1)
            return x * cos + rot * sin

        def _reference_tuple_inner(x, W_dq, W_uq, W_qr, W_dkv, W_ukv, W_kr, W_o, q_ln_g, q_ln_b, kv_ln_g, kv_ln_b):
            b, s, d = x.shape
            cq = layernorm(x @ W_dq, q_ln_g, q_ln_b)
            Q = (cq @ W_uq).reshape(b, s, N_HEADS, DH).transpose(0, 2, 1, 3)
            Qr = (cq @ W_qr).reshape(b, s, N_HEADS, R).transpose(0, 2, 1, 3)
            cos, sin = rope_cos_sin(s, x.dtype)
            Qr = apply_rope(Qr, cos, sin)
            q = jnp.concatenate([Q, Qr], axis=-1)
            ckv = layernorm(x @ W_dkv, kv_ln_g, kv_ln_b)
            KV = ckv @ W_ukv
            K, V = (KV[..., :D_MODEL], KV[..., D_MODEL:])
            K = K.reshape(b, s, N_HEADS, DH).transpose(0, 2, 1, 3)
            Kr = (x @ W_kr).reshape(b, s, N_HEADS, R).transpose(0, 2, 1, 3)
            Kr = apply_rope(Kr, cos, sin)
            k = jnp.concatenate([K, Kr], axis=-1)
            v = V.reshape(b, s, N_HEADS, DH).transpose(0, 2, 1, 3)
            scale = 1.0 / jnp.sqrt(jnp.asarray(DH + R, x.dtype))
            scores = jnp.einsum('bhqd,bhkd->bhqk', q, k) * scale
            mask = jnp.tril(jnp.ones((s, s), dtype=bool))
            scores = jnp.where(mask, scores, jnp.finfo(scores.dtype).min)
            attn = jax.nn.softmax(scores, axis=-1)
            out = jnp.einsum('bhqk,bhkd->bhqd', attn, v)
            out = out.transpose(0, 2, 1, 3).reshape(b, s, d)
            return (out @ W_o.T, ckv)
        key = jax.random.key(seed)
        ks = jax.random.split(key, 9)
        p = lambda k, shape: 0.01 * jax.random.normal(k, shape, jnp.float32)
        return {'x': jax.random.normal(ks[0], (B, S, D_MODEL), jnp.float32), 'W_dq': p(ks[1], (D_MODEL, Q_PROJ)), 'W_uq': p(ks[2], (Q_PROJ, D_MODEL)), 'W_qr': p(ks[3], (Q_PROJ, ROPE_DIM)), 'W_dkv': p(ks[4], (D_MODEL, KV_PROJ)), 'W_ukv': p(ks[5], (KV_PROJ, 2 * D_MODEL)), 'W_kr': p(ks[6], (D_MODEL, ROPE_DIM)), 'W_o': p(ks[7], (D_MODEL, D_MODEL)), 'q_ln_g': jnp.ones((Q_PROJ,), jnp.float32), 'q_ln_b': jnp.zeros((Q_PROJ,), jnp.float32), 'kv_ln_g': jnp.ones((KV_PROJ,), jnp.float32), 'kv_ln_b': jnp.zeros((KV_PROJ,), jnp.float32)}
    _L0_attn_all = _L0_attn_setup()
    _L0_attn_in = {k: v for k, v in _L0_attn_all.items() if k in ('W_dq', 'W_uq', 'W_qr', 'W_dkv', 'W_ukv', 'W_kr', 'W_o', 'q_ln_g', 'q_ln_b', 'kv_ln_g', 'kv_ln_b')}
    del _L0_attn_all

    def _L0_ffn_setup():
        import jax, jax.numpy as jnp
        import numpy as np
        E = 8
        TOP_K = 2
        D = 128
        H = 256
        B, S = (16, 1024)
        key = jax.random.key(seed)
        ks = jax.random.split(key, 10)
        sd = lambda fan_in: 1.0 / np.sqrt(fan_in)
        x = jax.random.normal(ks[0], (B, S, D), dtype=jnp.float32)
        gw1 = jax.random.uniform(ks[1], (D, D // 2), jnp.float32, -sd(D), sd(D))
        gb1 = jnp.zeros((D // 2,), jnp.float32)
        gw2 = jax.random.uniform(ks[2], (D // 2, E), jnp.float32, -sd(D // 2), sd(D // 2))
        gb2 = jnp.zeros((E,), jnp.float32)
        we1 = jax.random.uniform(ks[3], (E, D, H), jnp.float32, -sd(D), sd(D))
        be1 = jnp.zeros((E, H), jnp.float32)
        we2 = jax.random.uniform(ks[4], (E, H, D), jnp.float32, -sd(H), sd(H))
        be2 = jnp.zeros((E, D), jnp.float32)
        return {'x': x, 'gw1': gw1, 'gb1': gb1, 'gw2': gw2, 'gb2': gb2, 'we1': we1, 'be1': be1, 'we2': we2, 'be2': be2}
    _L0_ffn_all = _L0_ffn_setup()
    _L0_ffn_in = {k: v for k, v in _L0_ffn_all.items() if k in ('gw1', 'gb1', 'gw2', 'gb2', 'we1', 'be1', 'we2', 'be2')}
    del _L0_ffn_all
    return {'x': x, 'L0_tok_W': _L0_tok_in['W'], 'L0_tok_b': _L0_tok_in['b'], 'L0_tok_gamma': _L0_tok_in['gamma'], 'L0_tok_beta': _L0_tok_in['beta'], 'L0_attn_W_dq': _L0_attn_in['W_dq'], 'L0_attn_W_uq': _L0_attn_in['W_uq'], 'L0_attn_W_qr': _L0_attn_in['W_qr'], 'L0_attn_W_dkv': _L0_attn_in['W_dkv'], 'L0_attn_W_ukv': _L0_attn_in['W_ukv'], 'L0_attn_W_kr': _L0_attn_in['W_kr'], 'L0_attn_W_o': _L0_attn_in['W_o'], 'L0_attn_q_ln_g': _L0_attn_in['q_ln_g'], 'L0_attn_q_ln_b': _L0_attn_in['q_ln_b'], 'L0_attn_kv_ln_g': _L0_attn_in['kv_ln_g'], 'L0_attn_kv_ln_b': _L0_attn_in['kv_ln_b'], 'L0_ffn_gw1': _L0_ffn_in['gw1'], 'L0_ffn_gb1': _L0_ffn_in['gb1'], 'L0_ffn_gw2': _L0_ffn_in['gw2'], 'L0_ffn_gb2': _L0_ffn_in['gb2'], 'L0_ffn_we1': _L0_ffn_in['we1'], 'L0_ffn_be1': _L0_ffn_in['be1'], 'L0_ffn_we2': _L0_ffn_in['we2'], 'L0_ffn_be2': _L0_ffn_in['be2']}

def reference(x, L0_tok_W, L0_tok_b, L0_tok_gamma, L0_tok_beta, L0_attn_W_dq, L0_attn_W_uq, L0_attn_W_qr, L0_attn_W_dkv, L0_attn_W_ukv, L0_attn_W_kr, L0_attn_W_o, L0_attn_q_ln_g, L0_attn_q_ln_b, L0_attn_kv_ln_g, L0_attn_kv_ln_b, L0_ffn_gw1, L0_ffn_gb1, L0_ffn_gw2, L0_ffn_gb2, L0_ffn_we1, L0_ffn_be1, L0_ffn_we2, L0_ffn_be2):
    import jax
    import jax.numpy as jnp

    def _L0_tok_ref(x, W, b, gamma, beta):
        import jax, jax.numpy as jnp
        import numpy as np
        INPUT_DIM = 23
        OUTPUT_DIM = 128
        CONTEXT = 5
        DILATION = 1
        BN_EPS = 1e-05
        B, T, D = x.shape
        T_out = T - DILATION * (CONTEXT - 1)
        xc = jnp.concatenate([x[:, i * DILATION:i * DILATION + T_out, :] for i in range(CONTEXT)], axis=-1)
        h = jnp.einsum('btf,of->bto', xc, W) + b
        h = jax.nn.relu(h)
        mean = jnp.mean(h, axis=(0, 1))
        var = jnp.mean(jnp.square(h - mean), axis=(0, 1))
        h = (h - mean) * jax.lax.rsqrt(var + BN_EPS) * gamma + beta
        return h

    def _L0_attn_ref(x, W_dq, W_uq, W_qr, W_dkv, W_ukv, W_kr, W_o, q_ln_g, q_ln_b, kv_ln_g, kv_ln_b):
        import jax, jax.numpy as jnp
        import numpy as np
        D_MODEL = 128
        N_HEADS = 8
        DH = D_MODEL // N_HEADS
        Q_PROJ = D_MODEL // 2
        KV_PROJ = 2 * D_MODEL // 3
        ROPE_DIM = D_MODEL // 8
        R = ROPE_DIM // N_HEADS
        THETA = 10000.0
        EPS = 1e-05
        B, S = (2, 512)

        def layernorm(x, g, b):
            m = jnp.mean(x, axis=-1, keepdims=True)
            v = jnp.var(x, axis=-1, keepdims=True)
            return (x - m) * jax.lax.rsqrt(v + EPS) * g + b

        def rope_cos_sin(seq_len, dtype):
            inv_freq = THETA ** (-jnp.arange(0, R, 2, dtype=jnp.float32) / R)
            ang = jnp.arange(seq_len, dtype=jnp.float32)[:, None] * inv_freq
            cos = jnp.concatenate([jnp.cos(ang), jnp.cos(ang)], axis=-1)
            sin = jnp.concatenate([jnp.sin(ang), jnp.sin(ang)], axis=-1)
            return (cos.astype(dtype), sin.astype(dtype))

        def apply_rope(x, cos, sin):
            x1, x2 = jnp.split(x, 2, axis=-1)
            rot = jnp.concatenate([-x2, x1], axis=-1)
            return x * cos + rot * sin

        def _reference_tuple_inner(x, W_dq, W_uq, W_qr, W_dkv, W_ukv, W_kr, W_o, q_ln_g, q_ln_b, kv_ln_g, kv_ln_b):
            b, s, d = x.shape
            cq = layernorm(x @ W_dq, q_ln_g, q_ln_b)
            Q = (cq @ W_uq).reshape(b, s, N_HEADS, DH).transpose(0, 2, 1, 3)
            Qr = (cq @ W_qr).reshape(b, s, N_HEADS, R).transpose(0, 2, 1, 3)
            cos, sin = rope_cos_sin(s, x.dtype)
            Qr = apply_rope(Qr, cos, sin)
            q = jnp.concatenate([Q, Qr], axis=-1)
            ckv = layernorm(x @ W_dkv, kv_ln_g, kv_ln_b)
            KV = ckv @ W_ukv
            K, V = (KV[..., :D_MODEL], KV[..., D_MODEL:])
            K = K.reshape(b, s, N_HEADS, DH).transpose(0, 2, 1, 3)
            Kr = (x @ W_kr).reshape(b, s, N_HEADS, R).transpose(0, 2, 1, 3)
            Kr = apply_rope(Kr, cos, sin)
            k = jnp.concatenate([K, Kr], axis=-1)
            v = V.reshape(b, s, N_HEADS, DH).transpose(0, 2, 1, 3)
            scale = 1.0 / jnp.sqrt(jnp.asarray(DH + R, x.dtype))
            scores = jnp.einsum('bhqd,bhkd->bhqk', q, k) * scale
            mask = jnp.tril(jnp.ones((s, s), dtype=bool))
            scores = jnp.where(mask, scores, jnp.finfo(scores.dtype).min)
            attn = jax.nn.softmax(scores, axis=-1)
            out = jnp.einsum('bhqk,bhkd->bhqd', attn, v)
            out = out.transpose(0, 2, 1, 3).reshape(b, s, d)
            return (out @ W_o.T, ckv)
        return _reference_tuple_inner(x, W_dq, W_uq, W_qr, W_dkv, W_ukv, W_kr, W_o, q_ln_g, q_ln_b, kv_ln_g, kv_ln_b)[0]

    def _L0_ffn_ref(x, gw1, gb1, gw2, gb2, we1, be1, we2, be2):
        import jax, jax.numpy as jnp
        import numpy as np
        E = 8
        TOP_K = 2
        D = 128
        H = 256
        B, S = (16, 1024)
        b, s, d = x.shape
        xf = x.reshape(-1, d)
        T = xf.shape[0]
        gate_logits = jax.nn.relu(xf @ gw1 + gb1) @ gw2 + gb2
        gate_weights = jax.nn.softmax(gate_logits, axis=-1)
        top_w, top_idx = jax.lax.top_k(gate_weights, TOP_K)
        top_w = jax.nn.softmax(top_w, axis=-1)
        combine = jnp.zeros((T, E), dtype=xf.dtype)
        combine = combine.at[jnp.arange(T)[:, None], top_idx].add(top_w)
        out = jnp.zeros_like(xf)
        for e in range(E):
            h = jax.nn.gelu(xf @ we1[e] + be1[e], approximate=False)
            y = h @ we2[e] + be2[e]
            out = out + combine[:, e:e + 1] * y
        return out.reshape(b, s, d)
    h = _L0_tok_ref(x, L0_tok_W, L0_tok_b, L0_tok_gamma, L0_tok_beta)
    h = h + _L0_attn_ref(_layernorm(h, axis=-1), L0_attn_W_dq, L0_attn_W_uq, L0_attn_W_qr, L0_attn_W_dkv, L0_attn_W_ukv, L0_attn_W_kr, L0_attn_W_o, L0_attn_q_ln_g, L0_attn_q_ln_b, L0_attn_kv_ln_g, L0_attn_kv_ln_b)
    h = h + _L0_ffn_ref(_layernorm(h, axis=-1), L0_ffn_gw1, L0_ffn_gb1, L0_ffn_gw2, L0_ffn_gb2, L0_ffn_we1, L0_ffn_be1, L0_ffn_we2, L0_ffn_be2)
    return h

_drawn_inputs = setup_inputs


def setup_inputs(seed=0):
    import zlib

    import numpy as np

    out = dict(_drawn_inputs(seed))
    spreads = {'L0_tok_gamma': (1.0, 0.2),
     'L0_tok_beta': (0.0, 0.1),
     'L0_attn_q_ln_g': (1.0, 0.6),
     'L0_attn_q_ln_b': (0.0, 0.8),
     'L0_attn_kv_ln_g': (1.0, 0.6),
     'L0_attn_kv_ln_b': (0.0, 0.8),
     'L0_ffn_gb1': (0.0, 0.1),
     'L0_ffn_gb2': (0.0, 0.1),
     'L0_ffn_be1': (0.0, 0.351),
     'L0_ffn_be2': (0.0, 0.1)}
    factors = {'L0_attn_W_dq': 8.0,
     'L0_attn_W_uq': 8.0,
     'L0_attn_W_qr': 8.0,
     'L0_attn_W_dkv': 8.0,
     'L0_attn_W_ukv': 8.0,
     'L0_attn_W_kr': 8.0,
     'L0_attn_W_o': 8.0}
    for name, (base, spread) in spreads.items():
        noise = np.random.default_rng([zlib.crc32(name.encode()), seed]).standard_normal(out[name].shape)
        drawn = base * np.exp(spread * noise) if base else spread * noise
        out[name] = jnp.asarray(drawn.astype(out[name].dtype))
    for name, factor in factors.items():
        out[name] = (out[name] * factor).astype(out[name].dtype)
    return out
```

```python
from contextlib import ExitStack

import numpy as np
import concourse.bass as bass
from concourse import mybir

F32 = mybir.dt.float32
F32R = mybir.dt.float32r
BF16 = mybir.dt.bfloat16
ALU = mybir.AluOpType
ACT = mybir.ActivationFunctionType
AX = mybir.AxisListType

B, T_IN, D_IN = 32, 256, 23
CTX = 5
T = T_IN - (CTX - 1)
TILE = T // 2
K_IN = CTX * D_IN
D = 128
N_TOK = B * T
CH = 2 * T
N_CH = N_TOK // CH
N_TILES = N_TOK // TILE
HEADS, DH, R = 8, 16, 2
DQ = DH + R
Q_PROJ, KV_PROJ = D // 2, 2 * D // 3
ROT = HEADS * R
EXPERTS, HID = 8, 256
EPS = 1e-5
SCALE = float(1.0 / np.sqrt(np.float32(DQ)))
STACK = 3 * DQ
SLOT = 64
TW = SLOT + STACK + 2
PROJ_W = 3 * D + 4 * ROT
STAT_W = D + Q_PROJ + KV_PROJ + 1


N_PREP = 14
N_POOL_C = 10
R_DIFF, R_END = 17, 23
LAG_W = 3


def batches(n, top):
    return min(max(n, 0), top) if isinstance(n, int) else n


def before(b, parity):
    return (b - parity) // 2


def wait(eng, sem, value):
    if not isinstance(value, int) or value > 0:
        eng.wait_ge(sem, value)


def pipeline(eng, n, lag, step):
    head = lag + 2 - lag % 2
    for s in range(head):
        step(s, s % 2, lambda k, s=s: 0 <= s - k < n)
    with eng.Fori(head, n - 1, 2) as i:
        for p in range(2):
            step(i + p, p, lambda k: True)
    for s in range(n, n + lag):
        step(s, s % 2, lambda k, s=s: 0 <= s - k < n)


def build(nc, A, out):
    ctx = ExitStack()
    with ctx:
        def sb(name, shape, dt=F32, where=ctx):
            return where.enter_context(nc.sbuf_tensor(name, shape, dt))

        def sem(name):
            return ctx.enter_context(nc.semaphore(name))

        h = sb("h", [D, N_TOK])
        eye = sb("eye", [128, 128])
        centre = sb("centre", [D, D])
        w1_hi = sb("w1_hi", [D, EXPERTS, HID], F32R)
        w1_lo = sb("w1_lo", [D, EXPERTS, HID], F32R)
        w2_hi = sb("w2_hi", [D, EXPERTS, 2, D], F32R)
        w2_lo = sb("w2_lo", [D, EXPERTS, 2, D], F32R)
        be1 = sb("be1_sb", [D, EXPERTS, 2])
        be2 = sb("be2_sb", [D, EXPERTS])
        gw1 = sb("gw1_sb", [D, 64])
        gw1_hi = sb("gw1_hi", [D, 64], F32R)
        gw1_lo = sb("gw1_lo", [D, 64], F32R)
        gb1 = sb("gb1_sb", [64, 1])
        gw2 = sb("gw2_sb", [65, EXPERTS])
        rank = sb("rank_sb", [TILE, EXPERTS])
        scratch = nc.dram_tensor("combine_scratch", [4, 16, EXPERTS, TILE], F32).ap()

        early = ExitStack()
        with early:
            def eb(name, shape, dt=F32):
                return sb(name, shape, dt, early)
            vecs = eb("vecs", [D, 16])
            bn = eb("bn", [D, N_CH, 6])
            bn_mv = eb("bn_mv", [D, 2])
            wdq = eb("wdq", [D, Q_PROJ])
            wdkv = eb("wdkv", [D, KV_PROJ + 1])
            wq_raw = eb("wq_raw", [Q_PROJ, D + 2 * ROT])
            wk_raw = eb("wk_raw", [KV_PROJ, 2 * D])
            wkr = eb("wkr", [D, 2 * ROT])
            wo_t = eb("wo_t", [D, D])
            q_gb = eb("q_gb", [Q_PROJ, 2])
            kv_gb = eb("kv_gb", [KV_PROJ, 2])
            cell = eb("cell", [1, 2])
            v_bias = eb("v_bias", [D, 1])
            o_bias = eb("o_bias", [D, 1])
            stat_hi = eb("stat_hi", [D, STAT_W], F32R)
            stat_lo = eb("stat_lo", [D, STAT_W], F32R)
            proj_hi = eb("proj_hi", [D, PROJ_W], F32R)
            proj_lo = eb("proj_lo", [D, PROJ_W], F32R)
            bias_row = eb("bias_row", [TILE, 2 * D + 2 * ROT])
            trig = eb("trig_sb", [TILE, 2, 4 * ROT])
            eye_bf = eb("eye_bf", [TILE, TILE], BF16)
            mask = eb("mask_sb", [TILE, 4, TILE], BF16)
            hs_hi = [eb(f"hs_hi{i}", [D, CH], F32R) for i in range(2)]
            hs_lo = [eb(f"hs_lo{i}", [D, CH], F32R) for i in range(2)]
            squares = [eb(f"squares{i}", [TILE, 4, STAT_W]) for i in range(2)]
            sums = eb("sums", [TILE, 3, N_TILES])
            varis = eb("varis", [TILE, 3, N_TILES])
            rstd = eb("rstd", [TILE, 3, N_TILES])
            rwork = eb("rwork", [TILE, 3, N_TILES])
            v_all = eb("v_all", [128, B, 2, D])
            slots = [eb(f"slots{i}", [TILE, 2, 2, HEADS, SLOT]) for i in range(2)]
            v_ones = [eb(f"v_ones{i}", [TILE, 2, HEADS, 32]) for i in range(2)]
            with ExitStack() as conv_mem:
                def cb(name, shape, dt=F32):
                    return sb(name, shape, dt, conv_mem)
                frames = cb("frames", [K_IN, B * T_IN])
                conv_w = cb("conv_w", [K_IN, D])
                ones = cb("ones", [128, TILE])
                bq_wide = cb("bq_wide", [Q_PROJ, TILE])
                bkv_wide = cb("bkv_wide", [KV_PROJ, TILE])
                yq_t = cb("yq_t", [Q_PROJ, D])
                yk_t = cb("yk_t", [KV_PROJ, D])
                wq_g = cb("wq_g", [Q_PROJ, D + 2 * ROT])
                wk_g = cb("wk_g", [KV_PROJ, 2 * D])
            with ExitStack() as att_mem:
                def ab(name, shape, dt=F32):
                    return sb(name, shape, dt, att_mem)
                x_tok = [ab(f"x_tok{i}", [TILE, 2, 2, HEADS, DQ]) for i in range(2)]
                rope = [ab(f"rope{i}", [TILE, 2, 2, 2, ROT]) for i in range(2)]
                stack = [ab(f"stack{i}", [128, 2, 4, T], F32R) for i in range(2)]
                neg_max = [ab(f"neg_max{i}", [TILE, 2, 2, 4]) for i in range(2)]
                neg_max_t = [ab(f"neg_max_t{i}", [HEADS, T], F32R) for i in range(2)]
                p0 = [ab(f"p0_{i}", [TILE, 2, 4, T]) for i in range(2)]
                p1 = [ab(f"p1_{i}", [TILE, 2, 4, TILE]) for i in range(2)]
                o_sb = [ab(f"o_sb{i}", [D, 2, T]) for i in range(2)]
                o_rec = [ab(f"o_rec{i}", [TILE, 16, 1]) for i in range(2)]
                o_tok = [ab(f"o_tok{i}", [TILE, 2, D]) for i in range(2)]
                o_feat = [ab(f"o_feat{i}", [D, T]) for i in range(2)]

        xh = sb("xh", [D, N_TOK], F32R)
        xl = sb("xl", [D, N_TOK], F32R)
        comb_t = sb("comb_t", [128, 4, TILE])
        act_f = [sb(f"act_f{i}", [D, 2, CH]) for i in range(2)]
        act_hi = [sb(f"act_hi{i}", [D, 2, CH], F32R) for i in range(2)]
        act_lo = [sb(f"act_lo{i}", [D, 2, CH], F32R) for i in range(2)]
        part = [sb(f"part{i}", [D, CH]) for i in range(2)]
        total = [sb(f"total{i}", [D, CH]) for i in range(2)]
        with ExitStack() as gate_mem:
            def gb(name, shape, dt=F32):
                return sb(name, shape, dt, gate_mem)
            hn = [gb(f"hn{i}", [D, CH]) for i in range(2)]
            sq2 = [gb(f"sq2_{i}", [TILE, 4, D]) for i in range(2)]
            st2 = [gb(f"st2_{i}", [TILE, 8, 4]) for i in range(2)]
            xn = [gb(f"xn{i}", [TILE, 4, D]) for i in range(2)]
            gh = [gb(f"gh{i}", [65, CH]) for i in range(2)]
            rt = [gb(f"rt{i}", [TILE, N_TILES, EXPERTS]) for i in range(6)]
            rs = gb("rs", [TILE, 6, N_TILES])
        comb = [sb(f"comb{i}", [D, 4, EXPERTS, TILE]) for i in range(2)]

        ps = ctx.enter_context(nc.psum_tensor("ps", [128, 8, 512], F32))

        def bank(k, rows, cols, at=0):
            return ps[0:rows, k, at:at + cols]

        (s_conv_in, s_consts, s_weights, s_ffn_in, s_raw, s_pool_c, s_prep, s_fold, s_fold_hi, s_fold_lo,
         s_conv, s_relu, s_bn, s_bn_sqrt, s_normed, s_hs_hi, s_hs_lo, s_stat, s_square, s_sums, s_root,
         s_rstd, s_hi, s_lo, s_proj, s_scaled, s_pool, s_rope, s_slot_hi, s_slot_lo, s_tr, s_tr_act,
         s_tr_dve, s_score, s_max, s_mt, s_mt_out, s_m_dma0, s_m_dma1, s_st, s_exp, s_masked, s_v_ones,
         s_pv, s_o_out, s_ot, s_rec, s_o_norm, s_nt, s_nt_out, s_wo, s_resid, s_hn, s_cen, s_sq2, s_chain2,
         s_var2, s_root2, s_xn, s_xt, s_xh, s_xl, s_gate, s_gh, s_logit, s_router, s_rexp, s_ct, s_ct_out,
         s_scratch, s_comb_in0, s_comb_in1, s_up, s_gelu, s_act_hi, s_split, s_down, s_part, s_total,
         s_out0, s_out1, s_wsplit) = (sem(n) for n in (
            "s_conv_in s_consts s_weights s_ffn_in s_raw s_pool_c s_prep s_fold s_fold_hi s_fold_lo "
            "s_conv s_relu s_bn s_bn_sqrt s_normed s_hs_hi s_hs_lo s_stat s_square s_sums s_root "
            "s_rstd s_hi s_lo s_proj s_scaled s_pool s_rope s_slot_hi s_slot_lo s_tr s_tr_act s_tr_dve "
            "s_score s_max s_mt s_mt_out s_m_dma0 s_m_dma1 s_st s_exp s_masked s_v_ones s_pv s_o_out "
            "s_ot s_rec s_o_norm s_nt s_nt_out s_wo s_resid s_hn s_cen s_sq2 s_chain2 s_var2 s_root2 "
            "s_xn s_xt s_xh s_xl s_gate s_gh s_logit s_router s_rexp s_ct s_ct_out s_scratch "
            "s_comb_in0 s_comb_in1 s_up s_gelu s_act_hi s_split s_down s_part s_total s_out0 s_out1 "
            "s_wsplit").split())
        s_m_dma, s_comb_in, s_out = (s_m_dma0, s_m_dma1), (s_comb_in0, s_comb_in1), (s_out0, s_out1)

        Y, S, P, M0, M1 = 0, 2, 4, 6, 7
        CEN, XT, GATE, LOGIT, CT, UP, DOWN = 0, 2, 4, 6, 7, 0, 4

        WEIGHTS = [(wdq[:, :], A["wdq"]), (wdkv[:, 0:KV_PROJ], A["wdkv"]), (wq_raw[:, 0:D], A["wuq"]),
                   (wq_raw[:, D:D + ROT], A["wqr"]), (wk_raw[:, :], A["wukv"]), (wkr[:, 0:ROT], A["wkr"]),
                   (wo_t[:, :], A["wo_t"]), (q_gb[:, :], A["q_gb"]), (kv_gb[:, :], A["kv_gb"])]
        CONSTS = [(eye[:, :], A["eye"]), (centre[:, :], A["centre"]), (trig[:, :, :], A["trig"]),
                  (eye_bf[:, :], A["eye_bf"]), (mask[:, :, :], A["mask"]), (rank[:, :], A["rank"])]
        FFN_IN = [(be1[:, :, :], A["be1"]), (be2[:, :], A["be2"]), (gw1[:, :], A["gw1"]),
                  (gb1[:, :], A["gb1"]), (gw2[:, :], A["gw2"])]
        v_flat = v_all[:, :, :, :].rearrange("p b t d -> p (b t d)")
        w1_raw, w2_raw = v_flat[:, 0:EXPERTS * HID], v_flat[:, EXPERTS * HID:2 * EXPERTS * HID]
        W1_HI, W1_LO = (w[:, :, :].rearrange("p e n -> p (e n)") for w in (w1_hi, w1_lo))
        W2_HI, W2_LO = (w[:, :, :, :].rearrange("p e a n -> p (e a n)") for w in (w2_hi, w2_lo))

        block = ctx.enter_context(nc.Block())

        @block.sync
        def _(sp):
            sp.dma_start(conv_w[:, :], A["conv_w"]).then_inc(s_conv_in, 16)
            sp.dma_start(vecs[:, 0:3], A["vecs"]).then_inc(s_conv_in, 16)
            for i in range(CTX):
                n = B * T_IN - (CTX - 1)
                sp.dma_start(frames[i * D_IN:(i + 1) * D_IN, 0:n], A["x_t"][:, i:i + n]).then_inc(s_conv_in, 16)
            for dst, src in WEIGHTS:
                sp.dma_start(dst, src).then_inc(s_weights, 16)
            for dst, src in CONSTS:
                sp.dma_start(dst, src).then_inc(s_consts, 16)
            sp.dma_start(w1_raw, A["we1"]).then_inc(s_raw, 16)
            sp.dma_start(w2_raw, A["we2"]).then_inc(s_raw, 16)
            for dst, src in FFN_IN:
                sp.dma_start(dst, src).then_inc(s_ffn_in, 16)

            def move_max(s, p, live):
                if live(2):
                    b = s - 2
                    wait(sp, s_mt_out, b + 1)
                    for half in range(2):
                        row = SLOT * half + STACK
                        sp.dma_start(stack[p][row:row + 1, 0, :, :].bitcast(F32),
                                     neg_max_t[p][4 * half:4 * half + 4, :].bitcast(F32)).then_inc(s_m_dma[p], 16)

            pipeline(sp, B, 4, move_max)

            sp.wait_ge(s_ct_out, 1)
            sp.dma_start(scratch.rearrange("k t e i -> (t e) k i"), comb_t[:, :, :]).then_inc(s_scratch, 16)
            sp.wait_ge(s_scratch, 16)
            n_comb = 4 * EXPERTS * TILE
            flat = scratch.rearrange("k t e i -> (k t e i)").rearrange("(a n) -> a n", a=1)

            def load_comb(c, p):
                sp.dma_start(comb[p][:, :, :, :].rearrange("p j e i -> p (j e i)"),
                             flat[:, bass.ds(c * n_comb, n_comb)].to_broadcast([D, n_comb]))\
                  .then_inc(s_comb_in[p], 16)

            def store(c, p):
                sp.wait_ge(s_total, EXPERTS * c + EXPERTS)
                sp.dma_start(out[:, bass.ds(c * CH, CH)], total[p][:, :]).then_inc(s_out[p], 16)

            for c in range(2):
                load_comb(c, c)
            with sp.Fori(0, N_CH - 3, 2) as i:
                for p in range(2):
                    store(i + p, p)
                    load_comb(i + p + 2, p)
            for c in range(N_CH - 2, N_CH):
                store(c, c % 2)
            for p in range(2):
                sp.wait_ge(s_out[p], 16 * (N_CH // 2))

        @block.gpsimd
        def _(pool):
            pool.memset(cell[:, :], 0.0)
            pool.memset(ones[:, :], 1.0).then_inc(s_pool_c, 1)
            pool.memset(wdkv[:, KV_PROJ:KV_PROJ + 1], 0.0).then_inc(s_pool_c, 1)
            for p in range(2):
                pool.memset(slots[p][:, :, 0, :, :], 0.0).then_inc(s_pool_c, 1)
                pool.memset(slots[p][:, :, 1, :, :], 1.0).then_inc(s_pool_c, 1)
                pool.memset(v_ones[p][:, :, :, DH:], 1.0).then_inc(s_pool_c, 1)
            pool.wait_ge(s_fold_lo, 4)
            pool.wait_ge(s_consts, 16 * len(CONSTS))

            def step(s, p, live):
                q = 1 - p
                if live(1):
                    b = s - 1
                    pool.wait_ge(s_scaled, 2 * b + 2)
                    x16 = x_tok[q][:, :, :, :, 0:DH].rearrange("p t s h d -> p t (s h) d")
                    qk_bias = bias_row[:, 0:2 * D].rearrange("p (a h d) -> p a h d", a=1, d=DH)\
                        .to_broadcast([TILE, 2, 2 * HEADS, DH])
                    pool.tensor_tensor(x16, x16, qk_bias, ALU.add).then_inc(s_pool, 1)
                    rq = rope[q][:, :, 0, :, :].rearrange("p t a r -> p t (a r)")
                    r_bias = bias_row[:, 2 * D:].rearrange("p (a r) -> p a r", a=1)\
                        .to_broadcast([TILE, 2, 2 * ROT])
                    pool.tensor_tensor(rq, rq, r_bias, ALU.add).then_inc(s_pool, 1)
                    pool.wait_ge(s_pool, 3 * b + 2)
                    ra = rope[q][:, :, :, :, :].rearrange("p t s a r -> p (t s a r)")
                    pool.tensor_tensor(ra, ra, trig[:, :, :].rearrange("p t r -> p (t r)"), ALU.mult)\
                        .then_inc(s_pool, 1)
                    pool.wait_ge(s_pool, 3 * b + 3)
                    rr = rope[q][:, :, :, :, :].rearrange("p t s a (h r) -> p (t s) a h r", r=R)
                    pool.tensor_tensor(x_tok[q][:, :, :, :, DH:].rearrange("p t s h r -> p (t s) h r"),
                                       rr[:, :, 0], rr[:, :, 1], ALU.add).then_inc(s_rope, 1)
                if live(3):
                    b = s - 3
                    for i, (units, t) in enumerate(((2, p1[q][:, :, :, :]), (6, p0[q][:, :, :, 0:TILE]))):
                        wait(pool, s_masked, 2 * b + i)
                        pool.wait_ge(s_exp, 6 * b + units)
                        pool.tensor_tensor(cell[:, 0:1], cell[:, 1:2], cell[:, 1:2], ALU.mult)
                        v = t.rearrange("p a b q -> p (a b) q")
                        pool.affine_select(out=v, in_=v, compare_op=ALU.is_ge, fill=0.0, base=0,
                                           pattern=[[0, HEADS], [1, TILE]], channel_multiplier=-1)\
                            .then_inc(s_masked, 1)

            pipeline(pool, B, 4, step)

            pool.wait_ge(s_resid, B)
            for p in range(2):
                pool.memset(gh[p][64:65, :], 1.0).then_inc(s_pool_c, 1)

            def add(c, p):
                for e in range(EXPERTS):
                    pool.wait_ge(s_part, EXPERTS * c + e + 1)
                    if e == 0:
                        wait(pool, s_out[p], 16 * before(c, p))
                    else:
                        pool.wait_ge(s_total, EXPERTS * c + e)
                    acc = h[:, bass.ds(c * CH, CH)] if e == 0 else total[p][:, :]
                    pool.tensor_tensor(total[p][:, :], acc, part[e % 2][:, :], ALU.add).then_inc(s_total, 1)

            for c in range(2):
                add(c, c)
            with pool.Fori(2, N_CH - 1, 2) as i:
                for p in range(2):
                    add(i + p, p)

        @block.scalar
        def _(act):
            act.wait_ge(s_conv_in, 16 * (2 + CTX))
            with act.Fori(0, N_CH - 3, 4) as i:
                for k in range(4):
                    act.wait_ge(s_conv, i + k + 1)
                    act.activation(h[:, bass.ds((i + k) * CH, CH)], bank(k, D, CH), ACT.Relu,
                                   bias=vecs[:, 0:1]).then_inc(s_relu, 1)
            act.wait_ge(s_fold, 2)
            act.activation(stat_hi[:, :], bank(4, D, STAT_W), ACT.Identity).then_inc(s_fold_hi, 1)
            act.activation(proj_hi[:, :], bank(5, D, PROJ_W), ACT.Identity).then_inc(s_fold_hi, 1)
            act.wait_ge(s_bn, N_CH + 2)
            act.activation(vecs[:, 4:5], vecs[:, 3:4], ACT.Sqrt).then_inc(s_bn_sqrt, 1)

            def stats(s, p, live):
                if live(0):
                    act.wait_ge(s_normed, s + 1)
                    wait(act, s_stat, s - 1)
                    act.activation(hs_hi[p][:, :], h[:, bass.ds(s * CH, CH)], ACT.Identity).then_inc(s_hs_hi, 1)
                if live(2):
                    c = s - 2
                    act.wait_ge(s_stat, c + 1)
                    wait(act, s_sums, c - 1)
                    act.activation(squares[p][:, :, :], ps[0:TILE, 4 * p:4 * p + 4, 0:STAT_W], ACT.Square)\
                        .then_inc(s_square, 1)

            pipeline(act, N_CH, 2, stats)
            act.wait_ge(s_root, 1)
            act.activation(rstd[:, :, :], varis[:, :, :], ACT.Sqrt).then_inc(s_root, 1)

            def exp(b, u, q):
                half, k = u % 2, u // 2
                act.wait_ge(s_st, 6 * b + u + 1)
                if u == 0:
                    wait(act, s_pv, b - 1)
                if k == 0:
                    dst, src = p1[q][:, half, :, :], bank(P + half, TILE, 4 * TILE)
                else:
                    dst, src = p0[q][:, half, 2 * k - 2:2 * k, :], bank(P + half, TILE, 2 * T)
                src = src.rearrange("p (a b) -> p a b", a=4 if k == 0 else 2)
                act.activation(dst, src, ACT.Exp, scale=SCALE).then_inc(s_exp, 1)

            def attention(s, p, live):
                q = 1 - p
                if live(2):
                    b = s - 2
                    for side in range(2):
                        act.wait_ge(s_tr, 4 * b + 2 * side + 1)
                        if side == 0:
                            wait(act, s_st, 6 * (b - 1))
                        act.activation(stack[p][0:TW, side, :, 0:TILE],
                                       bank(M0, TW, 4 * TILE).rearrange("p (a b) -> p a b", a=4),
                                       ACT.Identity).then_inc(s_tr_act, 1)
                if live(4):
                    b = s - 4
                    act.wait_ge(s_pv, b + 1)
                    wait(act, s_ot, b - 1)
                    act.activation(o_sb[p][:, :, :], bank(M0, D, 2 * T).rearrange("p (a b) -> p a b", a=2),
                                   ACT.Identity).then_inc(s_o_out, 1)
                if live(3):
                    exp(s - 3, 0, q)
                    exp(s - 3, 1, q)
                if live(4):
                    b = s - 4
                    act.wait_ge(s_nt, b + 1)
                    wait(act, s_wo, b - 1)
                    act.activation(o_feat[p][:, :], bank(M0, D, T), ACT.Identity).then_inc(s_nt_out, 1)
                if live(3):
                    exp(s - 3, 2, q)
                if live(1):
                    b = s - 1
                    act.wait_ge(s_rope, b + 1)
                    wait(act, s_tr, 4 * (b - 1))
                    sl = slots[q][:, :, :, :, :].bitcast(F32R)
                    act.activation(sl[:, :, :, :, 0:DQ].rearrange("p t s h d -> p (t s h) d"),
                                   x_tok[q][:, :, :, :, :].rearrange("p t s h d -> p (t s h) d"),
                                   ACT.Identity).then_inc(s_slot_hi, 1)
                    for side in range(2):
                        at = DQ * (1 + side)
                        act.activation(sl[:, :, side, :, at:at + DQ], x_tok[q][:, :, side, :, :],
                                       ACT.Identity).then_inc(s_slot_hi, 1)
                if live(3):
                    for u in range(3, 6):
                        exp(s - 3, u, q)
                if live(0):
                    wait(act, s_proj, s - 1)
                    act.activation(hs_hi[p][:, 0:T], h[:, bass.ds(s * T, T)], ACT.Identity).then_inc(s_hi, 1)
                if live(2):
                    b = s - 2
                    act.wait_ge(s_mt, b + 1)
                    wait(act, s_m_dma[p], 32 * before(b, p))
                    act.activation(neg_max_t[p][:, :], bank(M0, HEADS, T), ACT.Identity).then_inc(s_mt_out, 1)

            pipeline(act, B, 4, attention)

            def gate(s, p, live):
                q = 1 - p
                if live(1):
                    act.wait_ge(s_cen, s)
                    wait(act, s_chain2, 6 * (s - 2))
                    act.activation(sq2[q][:, :, :], bank(CEN + q, TILE, 4 * D).rearrange("p (a b) -> p a b", a=4),
                                   ACT.Square).then_inc(s_sq2, 1)
                if live(2):
                    act.wait_ge(s_xt, s - 1)
                    act.activation(xh[:, bass.ds((s - 2) * CH, CH)], bank(XT + p, D, CH), ACT.Identity)\
                        .then_inc(s_xh, 1)
                if live(1):
                    act.wait_ge(s_var2, s)
                    act.activation(st2[q][:, 2, :], st2[q][:, 1, :], ACT.Sqrt).then_inc(s_root2, 1)
                if live(3):
                    act.wait_ge(s_gate, s - 2)
                    wait(act, s_logit, s - 4)
                    act.activation(gh[q][0:64, :], bank(GATE + q, 64, CH), ACT.Relu, bias=gb1[:, :])\
                        .then_inc(s_gh, 1)

            pipeline(act, N_CH, 4, gate)
            act.wait_ge(s_router, 2)
            act.activation(rt[0][:, :, :], rt[1][:, :, :], ACT.Exp).then_inc(s_rexp, 1)
            act.wait_ge(s_router, R_DIFF)
            act.activation(rs[:, 4, :], rs[:, 3, :], ACT.Exp).then_inc(s_rexp, 1)

            def gelu(c):
                for e in range(EXPERTS):
                    n = EXPERTS * c + e
                    for half in range(2):
                        act.wait_ge(s_up, 2 * n + half + 1)
                        wait(act, s_split, 2 * (n - 2) + half + 1)
                        act.activation(act_f[e % 2][:, half, :], bank(UP + 2 * (e % 2) + half, D, CH), ACT.Gelu,
                                       bias=be1[:, e, half:half + 1]).then_inc(s_gelu, 1)

            gelu(0)
            with act.Fori(1, N_CH, 1) as c:
                gelu(c)

        @block.vector
        def _(dve):
            V = nc.vector
            count = {}

            def link(ins, s=s_prep):
                count[s] = count.get(s, 0) + 1
                ins.then_inc(s, 1)
                dve.wait_ge(s, count[s])

            def rsqrt_from_root(v, root, r, w, s):
                link(V.reciprocal(r, root), s)
                link(V.tensor_tensor(w, r, r, ALU.mult), s)
                link(V.tensor_tensor(w, w, v, ALU.mult), s)
                link(V.tensor_scalar(w, w, -0.5, 1.5, ALU.mult, ALU.add), s)
                link(V.tensor_tensor(r, r, w, ALU.mult), s)

            dve.wait_ge(s_weights, 16 * len(WEIGHTS))
            dve.wait_ge(s_pool_c, 2)
            dve.wait_ge(s_conv_in, 16 * (2 + CTX))
            for w, n, c in ((wdq, Q_PROJ, 11), (wdkv, KV_PROJ, 13)):
                link(V.tensor_reduce(vecs[:, c:c + 1], w[:, 0:n], AX.X, ALU.add))
                link(V.tensor_scalar(vecs[:, c + 1:c + 2], vecs[:, c:c + 1], -1.0 / n, None, ALU.mult))
                link(V.tensor_scalar(w[:, 0:n], w[:, 0:n], vecs[:, c + 1:c + 2], None, ALU.add))
            for w, at in ((wq_raw, D), (wkr, 0)):
                a = w[:, at:at + ROT].rearrange("p (h r) -> p r h", r=R)
                r = w[:, at + ROT:at + 2 * ROT].rearrange("p (h r) -> p r h", r=R)
                link(V.tensor_scalar(r[:, 0], a[:, 1], -1.0, None, ALU.mult))
                link(V.tensor_copy(r[:, 1], a[:, 0]))
            link(V.tensor_scalar(wq_g[:, :], wq_raw[:, :], q_gb[:, 0:1], None, ALU.mult))
            link(V.tensor_scalar(wk_g[:, :], wk_raw[:, :], kv_gb[:, 0:1], None, ALU.mult))
            link(V.tensor_scalar(bq_wide[:, :], ones[0:Q_PROJ, :], q_gb[:, 1:2], None, ALU.mult))
            link(V.tensor_scalar(bkv_wide[:, :], ones[0:KV_PROJ, :], kv_gb[:, 1:2], None, ALU.mult))
            assert count[s_prep] == N_PREP
            dve.wait_ge(s_fold, 1)
            link(V.tensor_copy(yq_t[:, :], bank(6, Q_PROJ, D)))
            link(V.tensor_copy(yk_t[:, :], bank(6, KV_PROJ, D, D)))
            dve.wait_ge(s_fold, 2)
            V.tensor_copy(v_bias[:, :], bank(7, D, 1, 300)).then_inc(s_fold_lo, 1)
            V.tensor_copy(bias_row[:, :], bank(7, TILE, 2 * D + 2 * ROT)).then_inc(s_fold_lo, 1)
            dve.wait_ge(s_fold, 3)
            V.tensor_copy(o_bias[:, :], bank(6, D, 1, 300)).then_inc(s_fold_lo, 1)

            with dve.Fori(0, N_CH - 3, 4) as i:
                for k in range(4):
                    dve.wait_ge(s_relu, i + k + 1)
                    V.bn_stats(bn[:, bass.ds(i + k, 1), :].rearrange("p a b -> p (a b)"),
                               h[:, bass.ds((i + k) * CH, CH)]).then_inc(s_bn, 1)
            dve.wait_ge(s_fold_hi, 2)
            V.tensor_tensor(stat_lo[:, :], bank(4, D, STAT_W), stat_hi[:, :].bitcast(F32), ALU.subtract)\
                .then_inc(s_fold_lo, 1)
            V.tensor_tensor(proj_lo[:, :], bank(5, D, PROJ_W), proj_hi[:, :].bitcast(F32), ALU.subtract)\
                .then_inc(s_fold_lo, 1)
            dve.wait_ge(s_bn, N_CH)
            V.bn_aggr(bn_mv[:, :], bn[:, :, :].rearrange("p a b -> p (a b)")).then_inc(s_bn, 1)
            dve.wait_ge(s_bn, N_CH + 1)
            V.tensor_scalar(vecs[:, 3:4], bn_mv[:, 1:2], EPS, None, ALU.add).then_inc(s_bn, 1)
            dve.wait_ge(s_bn_sqrt, 1)
            rsqrt_from_root(vecs[:, 3:4], vecs[:, 4:5], vecs[:, 5:6], vecs[:, 6:7], s_prep)
            link(V.tensor_tensor(vecs[:, 8:9], vecs[:, 1:2], vecs[:, 5:6], ALU.mult))
            link(V.tensor_tensor(vecs[:, 9:10], bn_mv[:, 0:1], vecs[:, 8:9], ALU.mult))
            link(V.tensor_tensor(vecs[:, 10:11], vecs[:, 2:3], vecs[:, 9:10], ALU.subtract))

            def stats(s, p, live):
                q = 1 - p
                if live(0):
                    hc = h[:, bass.ds(s * CH, CH)]
                    V.tensor_scalar(hc, hc, vecs[:, 8:9], vecs[:, 10:11], ALU.mult, ALU.add).then_inc(s_normed, 1)
                if live(1):
                    c = s - 1
                    dve.wait_ge(s_hs_hi, c + 1)
                    wait(dve, s_stat, c - 1)
                    V.tensor_tensor(hs_lo[q][:, :], h[:, bass.ds(c * CH, CH)], hs_hi[q][:, :].bitcast(F32),
                                    ALU.subtract).then_inc(s_hs_lo, 1)
                if live(2):
                    c = s - 2
                    dve.wait_ge(s_square, c + 1)
                    for k, (at, n) in enumerate(((0, D), (D, Q_PROJ), (D + Q_PROJ, KV_PROJ))):
                        last = V.tensor_reduce(sums[:, k, bass.ds(4 * c, 4)], squares[p][:, :, at:at + n],
                                               AX.X, ALU.add)
                    last.then_inc(s_sums, 1)

            pipeline(dve, N_CH, 2, stats)
            dve.wait_ge(s_sums, N_CH)
            link(V.tensor_scalar(varis[:, 0, :], sums[:, 0, :], 1.0 / D, EPS, ALU.mult, ALU.add))
            link(V.tensor_scalar(rwork[:, 0, :], varis[:, 0, :], EPS, None, ALU.mult))
            link(V.scalar_tensor_tensor(varis[:, 1, :], sums[:, 1, :], 1.0 / Q_PROJ, rwork[:, 0, :],
                                        op0=ALU.mult, op1=ALU.add))
            V.scalar_tensor_tensor(varis[:, 2, :], sums[:, 2, :], 1.0 / KV_PROJ, rwork[:, 0, :],
                                   op0=ALU.mult, op1=ALU.add).then_inc(s_root, 1)
            dve.wait_ge(s_raw, 32)
            dve.wait_ge(s_ffn_in, 16 * len(FFN_IN))
            for hi, lo, raw in ((W1_HI, W1_LO, w1_raw), (W2_HI, W2_LO, w2_raw), (gw1_hi[:, :], gw1_lo[:, :], gw1[:, :])):
                link(V.tensor_copy(hi, raw), s_wsplit)
                link(V.tensor_tensor(lo, raw, hi.bitcast(F32), ALU.subtract), s_wsplit)
            dve.wait_ge(s_root, 2)
            rsqrt_from_root(varis[:, :, :], rstd[:, :, :], sums[:, :, :], rwork[:, :, :], s_prep)
            r_all = sums

            def per_token(k, b, shape):
                v = r_all[:, k, bass.ds(2 * b, 2)]
                return (v.rearrange("p (t a) -> p t a", a=1) if len(shape) == 3 else
                        v.rearrange("p (t a c) -> p t a c", a=1, c=1)).to_broadcast(shape)

            def attention(s, p, live):
                q = 1 - p
                if live(2):
                    b = s - 2
                    for side in range(2):
                        dve.wait_ge(s_tr, 4 * b + 2 * side + 2)
                        if side == 0:
                            wait(dve, s_st, 6 * (b - 1))
                        V.tensor_copy(stack[p][0:TW, side, :, TILE:],
                                      bank(M1, TW, 4 * TILE).rearrange("p (a b) -> p a b", a=4))\
                            .then_inc(s_tr_dve, 1)
                if live(1):
                    b = s - 1
                    dve.wait_ge(s_proj, b + 1)
                    wait(dve, s_slot_hi, 3 * (b - 1))
                    y = ps[0:TILE, Y:Y + 2, :]
                    wide = [TILE, 2, HEADS, DH]
                    for side in range(2):
                        V.tensor_tensor(x_tok[q][:, :, side, :, 0:DH],
                                        y[:, :, side * D:side * D + D].rearrange("p t (h d) -> p t h d", d=DH),
                                        per_token(1 + side, b, wide), ALU.mult)
                    V.tensor_tensor(v_all[0:TILE, bass.ds(b, 1), :, :].rearrange("p b t d -> p (b t) d"),
                                    y[:, :, 2 * D:3 * D], per_token(2, b, [TILE, 2, D]), ALU.mult)
                    for side in range(2):
                        at = 3 * D + 2 * ROT * side
                        V.tensor_tensor(rope[q][:, :, side, :, :].rearrange("p t a r -> p t (a r)"),
                                        y[:, :, at:at + 2 * ROT], per_token(1 - side, b, [TILE, 2, 2 * ROT]),
                                        ALU.mult).then_inc(s_scaled, 1)
                if live(4):
                    b = s - 4
                    dve.wait_ge(s_ot, b + 1)
                    o = bank(M1, TILE, 512).rearrange("p (a c) -> p a c", c=32)
                    V.reciprocal(o_rec[p][:, :, :], o[:, :, DH:DH + 1]).then_inc(s_rec, 1)
                    dve.wait_ge(s_rec, b + 1)
                    wait(dve, s_nt, b - 1)
                    V.tensor_tensor(o_tok[p][:, :, :].rearrange("p t (a d) -> p (t a) d", d=DH), o[:, :, 0:DH],
                                    o_rec[p][:, :, :].to_broadcast([TILE, 16, DH]), ALU.mult).then_inc(s_o_norm, 1)
                if live(3):
                    b = s - 3
                    dve.wait_ge(s_scaled, 2 * b + 2)
                    wait(dve, s_pv, b - 1)
                    V.tensor_copy(v_ones[q][:, :, :, 0:DH].rearrange("p t h d -> p (t h) d"),
                                  v_all[0:TILE, bass.ds(b, 1), :, :].rearrange("p b t (h d) -> p (b t h) d", d=DH))\
                        .then_inc(s_v_ones, 1)
                for u in range(6):
                    if live(2):
                        b, half, k = s - 2, u % 2, u // 2
                        dve.wait_ge(s_score, 6 * b + u + 1)
                        if u == 0:
                            wait(dve, s_mt, b - 1)
                        if k == 0:
                            dst, src = neg_max[p][:, 0, half, :], bank(S + half, TILE, 4 * TILE)
                        else:
                            dst, src = neg_max[p][:, 1, half, 2 * k - 2:2 * k], bank(S + half, TILE, 2 * T)
                        src = src.rearrange("p (a b) -> p a b", a=4 if k == 0 else 2)
                        V.tensor_reduce(dst, src, AX.X, ALU.max, negate=True).then_inc(s_max, 1)
                    if u == 4 and live(4):
                        b = s - 4
                        dve.wait_ge(s_wo, b + 1)
                        hb = h[:, bass.ds(b * T, T)]
                        V.scalar_tensor_tensor(hb, bank(M1, D, T), o_bias[:, :], hb, op0=ALU.add, op1=ALU.add)\
                            .then_inc(s_resid, 1)
                if live(1):
                    b = s - 1
                    dve.wait_ge(s_slot_hi, 3 * b + 1)
                    for side in range(2):
                        at = DQ * (2 - side)
                        V.tensor_tensor(slots[q][:, :, side, :, at:at + DQ], x_tok[q][:, :, side, :, :],
                                        slots[q][:, :, side, :, 0:DQ], ALU.subtract).then_inc(s_slot_lo, 1)
                if live(0):
                    dve.wait_ge(s_hi, s + 1)
                    wait(dve, s_proj, s - 1)
                    V.tensor_tensor(hs_lo[p][:, 0:T], h[:, bass.ds(s * T, T)], hs_hi[p][:, 0:T].bitcast(F32),
                                    ALU.subtract).then_inc(s_lo, 1)

            pipeline(dve, B, 4, attention)

            def norm(s, p, live):
                q = 1 - p
                if live(0):
                    wait(dve, s_cen, s - 1)
                    if not isinstance(s, int) or s < 2:
                        dve.wait_ge(s_resid, B)
                    V.tensor_copy(hn[p][:, :], h[:, bass.ds(s * CH, CH)]).then_inc(s_hn, 1)
                if live(1):
                    c = s - 1
                    dve.wait_ge(s_sq2, c + 1)
                    V.tensor_reduce(st2[q][:, 0, :], sq2[q][:, :, :], AX.X, ALU.add).then_inc(s_chain2, 1)
                    dve.wait_ge(s_chain2, 6 * c + 1)
                    V.tensor_scalar(st2[q][:, 1, :], st2[q][:, 0, :], 1.0 / D, EPS, ALU.mult, ALU.add)\
                        .then_inc(s_var2, 1)
                if live(2):
                    c = s - 2
                    dve.wait_ge(s_xh, c + 1)
                    V.tensor_tensor(xl[:, bass.ds(c * CH, CH)], bank(XT + p, D, CH),
                                    xh[:, bass.ds(c * CH, CH)].bitcast(F32), ALU.subtract).then_inc(s_xl, 1)
                if live(1):
                    c = s - 1
                    v, root, r, w = (st2[q][:, k, :] for k in (1, 2, 3, 4))
                    dve.wait_ge(s_root2, c + 1)
                    V.reciprocal(r, root).then_inc(s_chain2, 1)
                    dve.wait_ge(s_chain2, 6 * c + 2)
                    V.tensor_tensor(w, r, r, ALU.mult).then_inc(s_chain2, 1)
                    dve.wait_ge(s_chain2, 6 * c + 3)
                    V.tensor_tensor(w, w, v, ALU.mult).then_inc(s_chain2, 1)
                    dve.wait_ge(s_chain2, 6 * c + 4)
                    V.tensor_scalar(w, w, -0.5, 1.5, ALU.mult, ALU.add).then_inc(s_chain2, 1)
                    dve.wait_ge(s_chain2, 6 * c + 5)
                    V.tensor_tensor(r, r, w, ALU.mult).then_inc(s_chain2, 1)
                    dve.wait_ge(s_chain2, 6 * c + 6)
                    wait(dve, s_xt, c - 1)
                    V.tensor_tensor(xn[q][:, :, :], bank(CEN + q, TILE, 4 * D).rearrange("p (a b) -> p a b", a=4),
                                    r.rearrange("p (a b) -> p a b", b=1).to_broadcast([TILE, 4, D]), ALU.mult)\
                        .then_inc(s_xn, 1)

            pipeline(dve, N_CH, 4, norm)

            shape = [TILE, N_TILES, EXPERTS]

            def over(v):
                return v.rearrange("p (t a) -> p t a", a=1).to_broadcast(shape)

            def first_largest(v, top, sel, tmp):
                link(V.tensor_reduce(top, v, AX.X, ALU.max), s_router)
                link(V.tensor_tensor(sel, v, over(top), ALU.is_equal), s_router)
                link(V.tensor_tensor(sel, sel, rank[:, :].rearrange("p (a e) -> p a e", a=1).to_broadcast(shape),
                                     ALU.mult), s_router)
                link(V.tensor_reduce(tmp, sel, AX.X, ALU.max), s_router)
                link(V.tensor_tensor(sel, sel, over(tmp), ALU.is_equal), s_router)

            dve.wait_ge(s_logit, N_CH)
            logits = bank(LOGIT, TILE, 512).rearrange("p (t e) -> p t e", e=EXPERTS)
            t = [x[:, :, :] for x in rt]
            r = [rs[:, k, :] for k in range(6)]
            link(V.tensor_reduce(r[0], logits, AX.X, ALU.max), s_router)
            link(V.tensor_tensor(t[1], logits, over(r[0]), ALU.subtract), s_router)
            dve.wait_ge(s_rexp, 1)
            link(V.tensor_reduce(r[1], t[0], AX.X, ALU.add), s_router)
            link(V.reciprocal(r[2], r[1]), s_router)
            link(V.tensor_tensor(t[2], t[0], over(r[2]), ALU.mult), s_router)
            first_largest(t[2], r[0], t[3], r[1])
            link(V.scalar_tensor_tensor(t[4], t[3], -2.0, t[2], op0=ALU.mult, op1=ALU.add), s_router)
            first_largest(t[4], r[2], t[5], r[1])
            link(V.tensor_tensor(r[3], r[2], r[0], ALU.subtract), s_router)
            assert count[s_router] == R_DIFF
            dve.wait_ge(s_rexp, 2)
            link(V.tensor_scalar(r[5], r[4], 1.0, None, ALU.add), s_router)
            link(V.reciprocal(r[1], r[5]), s_router)
            link(V.tensor_tensor(r[2], r[4], r[1], ALU.mult), s_router)
            link(V.tensor_tensor(t[0], t[3], over(r[1]), ALU.mult), s_router)
            link(V.tensor_tensor(t[1], t[5], over(r[2]), ALU.mult), s_router)
            link(V.tensor_tensor(t[2], t[0], t[1], ALU.add), s_router)
            assert count[s_router] == R_END
            dve.wait_ge(s_ct, 1)
            V.tensor_copy(comb_t[:, :, :], bank(CT, 128, 4 * TILE).rearrange("p (a b) -> p a b", a=4))\
                .then_inc(s_ct_out, 1)

            def split(n, e):
                for half in range(2):
                    dve.wait_ge(s_gelu, 2 * n + half + 1)
                    if half == 0:
                        wait(dve, s_down, n - 1)
                    V.tensor_copy(act_hi[e % 2][:, half, :], act_f[e % 2][:, half, :]).then_inc(s_act_hi, 1)
                    dve.wait_ge(s_act_hi, 2 * n + half + 1)
                    V.tensor_tensor(act_lo[e % 2][:, half, :], act_f[e % 2][:, half, :],
                                    act_hi[e % 2][:, half, :].bitcast(F32), ALU.subtract).then_inc(s_split, 1)

            def weigh(n, e, c, p):
                dve.wait_ge(s_down, n + 1)
                wait(dve, s_total, n - 1)
                if e == 0:
                    dve.wait_ge(s_comb_in[p], 16 * (before(c, p) + 1))
                V.scalar_tensor_tensor(part[e % 2][:, :].rearrange("p (j i) -> p j i", j=4),
                                       bank(DOWN + e % 2, D, CH).rearrange("p (j i) -> p j i", j=4),
                                       be2[:, e:e + 1], comb[p][:, :, e, :], op0=ALU.add, op1=ALU.mult)\
                    .then_inc(s_part, 1)

            def unit(c, k, live):
                if live:
                    m = (k - LAG_W) % (2 * EXPERTS)
                    cc = c + (k - LAG_W) // EXPERTS
                    weigh(EXPERTS * c + k - LAG_W, m % EXPERTS, cc, m // EXPERTS)
                split(EXPERTS * c + k, k % EXPERTS)

            for k in range(2 * EXPERTS):
                unit(0, k, k >= LAG_W)
            with dve.Fori(2, N_CH - 1, 2) as c:
                for k in range(2 * EXPERTS):
                    unit(c, k, True)
            for k in range(2 * EXPERTS - LAG_W, 2 * EXPERTS):
                weigh(EXPERTS * (N_CH - 2) + k, k % EXPERTS, N_CH - 1, 1)

        @block.tensor
        def _(pe):
            mm = nc.tensor.matmul

            pe.wait_ge(s_consts, 16 * len(CONSTS))
            pe.wait_ge(s_prep, N_PREP)
            mm(bank(6, Q_PROJ, D), wdq[:, :], centre[:, :], start=True, stop=True)
            mm(bank(6, KV_PROJ, D, D), wdkv[:, 0:KV_PROJ], centre[:, :], start=True, stop=True).then_inc(s_fold, 1)
            pe.wait_ge(s_prep, N_PREP + 2)
            mm(bank(4, D, D), centre[:, :], eye[:, :], start=True, stop=True)
            mm(bank(4, D, Q_PROJ, D), centre[:, :], wdq[:, :], start=True, stop=True)
            mm(bank(4, D, KV_PROJ + 1, D + Q_PROJ), centre[:, :], wdkv[:, :], start=True, stop=True)
            mm(bank(5, D, D), yq_t[:, :], wq_g[:, 0:D], start=True, stop=True)
            mm(bank(5, D, 2 * D, D), yk_t[:, :], wk_g[:, :], start=True, stop=True)
            mm(bank(5, D, 2 * ROT, 3 * D), yq_t[:, :], wq_g[:, D:], start=True, stop=True)
            mm(bank(5, D, 2 * ROT, 3 * D + 2 * ROT), centre[:, :], wkr[:, :], start=True, stop=True)
            mm(bank(7, TILE, D), bq_wide[:, :], wq_raw[:, 0:D], start=True, stop=True)
            mm(bank(7, TILE, D, D), bkv_wide[:, :], wk_raw[:, 0:D], start=True, stop=True)
            mm(bank(7, TILE, 2 * ROT, 2 * D), bq_wide[:, :], wq_raw[:, D:], start=True, stop=True)
            mm(bank(7, D, 1, 300), wk_raw[:, D:], kv_gb[:, 1:2], start=True, stop=True).then_inc(s_fold, 1)
            pe.wait_ge(s_fold_lo, 1)
            mm(bank(6, D, 1, 300), wo_t[:, :], v_bias[:, :], start=True, stop=True).then_inc(s_fold, 1)

            pe.wait_ge(s_conv_in, 16 * (2 + CTX))
            def conv(c, k, wait_for):
                wait(pe, s_relu, wait_for)
                rhs = frames[:, bass.ds(c * 2 * T_IN, 2 * T_IN)].rearrange("p (b t) -> p b t", b=2)[:, :, 0:T]
                mm(bank(k, D, CH).rearrange("p (b t) -> p b t", b=2), conv_w[:, :], rhs, start=True, stop=True)\
                    .then_inc(s_conv, 1)

            for k in range(4):
                conv(k, k, 0)
            with pe.Fori(4, N_CH - 3, 4) as i:
                for k in range(4):
                    conv(i + k, k, i + k - 3)

            def three(dst, w_hi, w_lo, x_hi, x_lo, first=True, last=True):
                mm(dst, w_hi, x_hi, start=first, stop=False)
                mm(dst, w_hi, x_lo, start=False, stop=False)
                return mm(dst, w_lo, x_hi, start=False, stop=last)

            def stats(s, p, live):
                if live(1):
                    c, q = s - 1, 1 - p
                    pe.wait_ge(s_hs_lo, c + 1)
                    wait(pe, s_square, c - 1)
                    if not isinstance(s, int) or s < 4:
                        pe.wait_ge(s_fold_lo, 5)
                    for j in range(4):
                        t = slice(j * TILE, j * TILE + TILE)
                        last = three(bank(4 * q + j, TILE, STAT_W), hs_hi[q][:, t], hs_lo[q][:, t],
                                     stat_hi[:, :], stat_lo[:, :])
                    last.then_inc(s_stat, 1)

            pipeline(pe, N_CH, 2, stats)

            def score(b, u, p):
                half, k = u % 2, u // 2
                at, rows = SLOT * half, slice(SLOT * half, SLOT * half + STACK)
                wait(pe, s_max, 6 * b + u - 1)
                if k == 0:
                    dst = bank(S + half, TILE, 4 * TILE).rearrange("p (a b) -> p a b", a=4)
                    for j in range(4):
                        mm(dst[:, j], stack[p][rows, 0, j, 0:TILE], stack[p][rows, 1, j, 0:TILE],
                           start=j == 0, stop=False, skip_group_check=True)
                    mm(dst, eye_bf[:, :], mask[:, :, :], start=False, stop=True, skip_group_check=True)\
                        .then_inc(s_score, 1)
                else:
                    dst = bank(S + half, TILE, 2 * T).rearrange("p (a b) -> p a b", a=2)
                    for j in range(2):
                        m = 2 * k - 2 + j
                        mm(dst[:, j], stack[p][rows, 0, m, TILE:], stack[p][rows, 1, m, :],
                           start=j == 0, stop=False, skip_group_check=True)
                    mm(dst[:, :, TILE:], eye_bf[:, :], mask[:, 0:2, :], start=False, stop=True,
                       skip_group_check=True).then_inc(s_score, 1)

            def score_t(b, u, q):
                half, k = u % 2, u // 2
                rows = slice(SLOT * half, SLOT * half + STACK + 1)
                if u == 0:
                    pe.wait_ge(s_m_dma[q], 32 * (before(b, q) + 1))
                wait(pe, s_exp, 6 * b + u - 1)
                if k == 0:
                    dst = bank(P + half, TILE, 4 * TILE).rearrange("p (a b) -> p a b", a=4)
                    for j in range(4):
                        last = mm(dst[:, j], stack[q][rows, 1, j, TILE:], stack[q][rows, 0, j, TILE:],
                                  start=True, stop=True)
                else:
                    dst = bank(P + half, TILE, 2 * T).rearrange("p (a b) -> p a b", a=2)
                    for j in range(2):
                        m = 2 * k - 2 + j
                        last = mm(dst[:, j], stack[q][rows, 1, m, 0:TILE], stack[q][rows, 0, m, :],
                                  start=True, stop=True)
                last.then_inc(s_st, 1)

            def attention(s, p, live):
                q = 1 - p
                if live(2):
                    b = s - 2
                    pe.wait_ge(s_slot_hi, 3 * b + 3)
                    pe.wait_ge(s_slot_lo, 2 * b + 2)
                    for side in range(2):
                        for t in range(2):
                            if t == 0:
                                wait(pe, *((s_mt_out, b) if side == 0 else (s_tr_act, 2 * b + 1)))
                            else:
                                wait(pe, *((s_resid, b - 2) if side == 0 else (s_tr_dve, 2 * b + 1)))
                            for j in range(4):
                                src = slots[p][:, t, side, 2 * j:2 * j + 2, :].rearrange("p h d -> p (h d)")
                                last = nc.tensor.transpose(bank(M0 + t, TW, TILE, j * TILE), src[:, 0:TW],
                                                           eye[0:TILE, 0:TILE])
                            last.then_inc(s_tr, 1)
                if live(4):
                    b = s - 4
                    pe.wait_ge(s_masked, 2 * b + 2)
                    pe.wait_ge(s_v_ones, b + 1)
                    wait(pe, s_tr_act, 2 * batches(s - 1, B))
                    if not live(2):
                        wait(pe, s_mt_out, batches(s - 2, B))
                        wait(pe, s_nt_out, b)
                    o = bank(M0, D, 2 * T).rearrange("p (g t) -> p g t", g=2)
                    for g in range(2):
                        for j in range(4):
                            mm(o[32 * j:32 * j + 32, g], v_ones[p][:, 0, 4 * g + j, :], p0[p][:, g, j, :],
                               start=g == 0, stop=False, skip_group_check=True)
                        for j in range(4):
                            last = mm(o[32 * j:32 * j + 32, g, TILE:], v_ones[p][:, 1, 4 * g + j, :],
                                      p1[p][:, g, j, :], start=False, stop=True, skip_group_check=True)
                    last.then_inc(s_pv, 1)
                if live(1):
                    b = s - 1
                    pe.wait_ge(s_lo, b + 1)
                    wait(pe, s_scaled, 2 * b)
                    for t in range(2):
                        tt = slice(t * TILE, t * TILE + TILE)
                        last = three(bank(Y + t, TILE, PROJ_W), hs_hi[q][:, tt], hs_lo[q][:, tt],
                                     proj_hi[:, :], proj_lo[:, :])
                    last.then_inc(s_proj, 1)
                if live(4):
                    b = s - 4
                    pe.wait_ge(s_o_out, b + 1)
                    wait(pe, s_tr_dve, 2 * batches(s - 1, B))
                    if not live(2):
                        wait(pe, s_resid, b)
                    for t in range(2):
                        for g in range(2):
                            last = nc.tensor.transpose(bank(M1, TILE, D, (2 * t + g) * D),
                                                       o_sb[p][:, g, t * TILE:t * TILE + TILE], eye[:, :])
                    last.then_inc(s_ot, 1)
                for u in range(6):
                    if live(2):
                        if u == 0:
                            pe.wait_ge(s_tr_act, 2 * (s - 2) + 2)
                            pe.wait_ge(s_tr_dve, 2 * (s - 2) + 2)
                        score(s - 2, u, p)
                    if live(3):
                        score_t(s - 3, u, q)
                    if u == 1 and live(4):
                        b = s - 4
                        pe.wait_ge(s_o_norm, b + 1)
                        for t in range(2):
                            last = nc.tensor.transpose(bank(M0, D, TILE, t * TILE), o_tok[p][:, t, :],
                                                       eye[0:TILE, 0:TILE])
                        last.then_inc(s_nt, 1)
                    if u == 4 and live(4):
                        b = s - 4
                        pe.wait_ge(s_nt_out, b + 1)
                        mm(bank(M1, D, T), wo_t[:, :], o_feat[p][:, :], start=True, stop=True).then_inc(s_wo, 1)
                if live(2):
                    b = s - 2
                    pe.wait_ge(s_max, 6 * b + 6)
                    for t in range(2):
                        last = nc.tensor.transpose(bank(M0, HEADS, TILE, t * TILE),
                                                   neg_max[p][:, t, :, :].rearrange("p a b -> p (a b)"),
                                                   eye[0:TILE, 0:TILE])
                    last.then_inc(s_mt, 1)

            pipeline(pe, B, 4, attention)

            def gate(s, p, live):
                q = 1 - p
                if live(0):
                    pe.wait_ge(s_hn, s + 1)
                    wait(pe, s_xn, s - 1)
                    for j in range(4):
                        last = mm(bank(CEN + p, TILE, D, j * D), hn[p][:, j * TILE:j * TILE + TILE], centre[:, :],
                                  start=True, stop=True)
                    last.then_inc(s_cen, 1)
                if live(2):
                    c = s - 2
                    pe.wait_ge(s_xn, c + 1)
                    wait(pe, s_xl, c - 1)
                    for j in range(4):
                        last = nc.tensor.transpose(bank(XT + p, D, TILE, j * TILE), xn[p][:, j, :],
                                                   eye[0:TILE, 0:TILE])
                    last.then_inc(s_xt, 1)
                if live(3):
                    c = s - 3
                    pe.wait_ge(s_xl, c + 1)
                    wait(pe, s_gh, c - 1)
                    three(bank(GATE + q, 64, CH), gw1_hi[:, :], gw1_lo[:, :], xh[:, bass.ds(c * CH, CH)],
                          xl[:, bass.ds(c * CH, CH)]).then_inc(s_gate, 1)
                if live(4):
                    c = s - 4
                    pe.wait_ge(s_gh, c + 1)
                    if not isinstance(s, int) or c < 2:
                        pe.wait_ge(s_pool_c, N_POOL_C)
                    for j in range(4):
                        last = mm(ps[0:TILE, LOGIT, bass.ds(4 * EXPERTS * c + EXPERTS * j, EXPERTS)],
                                  gh[p][:, j * TILE:j * TILE + TILE], gw2[:, :], start=True, stop=True)
                    last.then_inc(s_logit, 1)

            pipeline(pe, N_CH, 4, gate)

            def up(n, e, c):
                for half in range(2):
                    wait(pe, s_gelu, 2 * (n - 2) + half + 1)
                    cols = slice(half * D, half * D + D)
                    three(bank(UP + 2 * (e % 2) + half, D, CH), w1_hi[:, e, cols], w1_lo[:, e, cols],
                          xh[:, bass.ds(c * CH, CH)], xl[:, bass.ds(c * CH, CH)]).then_inc(s_up, 1)

            def down(n, e):
                wait(pe, s_part, n - 1)
                for half in range(2):
                    pe.wait_ge(s_split, 2 * n + half + 1)
                    last = three(bank(DOWN + e % 2, D, CH), w2_hi[:, e, half, :], w2_lo[:, e, half, :],
                                 act_hi[e % 2][:, half, :], act_lo[e % 2][:, half, :], half == 0, half == 1)
                last.then_inc(s_down, 1)

            def unit(c, k, live):
                up(EXPERTS * c + k, k % EXPERTS, c + k // EXPERTS)
                if live:
                    down(EXPERTS * c + k - 2, (k - 2) % EXPERTS)

            for k in range(2 * EXPERTS):
                unit(0, k, k >= 2)
                if k == 1:
                    pe.wait_ge(s_router, R_END)
                    flat = rt[2][:, :, :].rearrange("p t e -> p (t e)")
                    for j in range(4):
                        last = nc.tensor.transpose(bank(CT, 128, TILE, j * TILE), flat[:, 128 * j:128 * j + 128],
                                                   eye[0:TILE, 0:TILE])
                    last.then_inc(s_ct, 1)
            with pe.Fori(2, N_CH - 1, 2) as c:
                for k in range(2 * EXPERTS):
                    unit(c, k, True)
            for k in (EXPERTS - 2, EXPERTS - 1):
                down(EXPERTS * (N_CH - 1) + k, k)


def kernel(**inputs):
    import ml_dtypes
    import concourse.bacc as bacc
    from concourse.bass_utils import run_bass_kernel_spmd as run

    a = {n: np.asarray(v) for n, v in inputs.items()}
    t = {n[len("L0_attn_"):]: v for n, v in a.items() if n.startswith("L0_attn_")}
    f = {n[len("L0_ffn_"):]: v for n, v in a.items() if n.startswith("L0_ffn_")}
    pos = np.arange(T, dtype=np.float64).reshape(2, TILE).T[:, :, None]
    cos, sin = (np.broadcast_to(x, (TILE, 2, ROT)) for x in (np.cos(pos), np.sin(pos)))
    tri = np.where(np.arange(TILE)[None, :] <= np.arange(TILE)[:, None], 0.0, -3.0e38)
    arrays = {
        "x_t": a["x"].transpose(2, 0, 1).reshape(D_IN, B * T_IN),
        "conv_w": a["L0_tok_W"].T,
        "vecs": np.stack([a["L0_tok_b"], a["L0_tok_gamma"], a["L0_tok_beta"]], 1),
        "wdq": t["W_dq"], "wdkv": t["W_dkv"], "wuq": t["W_uq"], "wqr": t["W_qr"],
        "wukv": np.concatenate([t["W_ukv"][:, :D], t["W_ukv"][:, D:].reshape(KV_PROJ, 4, 2, DH)
                                .transpose(0, 2, 1, 3).reshape(KV_PROJ, D)], 1),
        "wkr": t["W_kr"],
        "wo_t": t["W_o"].T.reshape(4, 2, DH, D).transpose(1, 0, 2, 3).reshape(D, D),
        "q_gb": np.stack([t["q_ln_g"], t["q_ln_b"]], 1), "kv_gb": np.stack([t["kv_ln_g"], t["kv_ln_b"]], 1),
        "we1": f["we1"].transpose(1, 0, 2).reshape(D, EXPERTS * HID),
        "we2": f["we2"].reshape(EXPERTS, 2, D, D).transpose(2, 0, 1, 3).reshape(D, EXPERTS * HID),
        "be1": f["be1"].reshape(EXPERTS, 2, D).transpose(2, 0, 1), "be2": f["be2"].T,
        "gw1": f["gw1"], "gb1": f["gb1"][:, None], "gw2": np.concatenate([f["gw2"], f["gb2"][None]], 0),
        "eye": np.eye(128, dtype=np.float32),
        "centre": (np.eye(D) - 1.0 / D).astype(np.float32),
        "trig": np.concatenate([cos, sin, cos, sin], 2).astype(np.float32),
        "eye_bf": np.eye(TILE).astype(ml_dtypes.bfloat16),
        "mask": np.broadcast_to(tri[:, None, :], (TILE, 4, TILE)).astype(ml_dtypes.bfloat16),
        "rank": np.broadcast_to(np.arange(EXPERTS, 0, -1), (TILE, EXPERTS)).astype(np.float32),
    }
    nc = bacc.Bacc("TRN2", target_bir_lowering=False, num_devices=1)
    arrays = {f"in_{n}_dram": np.ascontiguousarray(v) for n, v in arrays.items()}
    aps = {n[3:-5]: nc.dram_tensor(n, v.shape, mybir.dt.from_np(v.dtype), kind="ExternalInput").ap()
           for n, v in arrays.items()}
    out = nc.dram_tensor("out_dram", (D, N_TOK), F32, kind="ExternalOutput").ap()
    build(nc, aps, out)
    r = run(nc, [arrays], core_ids=[0])
    return np.ascontiguousarray(np.asarray(r.results[0]["out_dram"]).T).reshape(B, T, D)
```

```python
from contextlib import ExitStack

import numpy as np
import concourse.bass as bass
from concourse import mybir

F32 = mybir.dt.float32
F32R = mybir.dt.float32r
BF16 = mybir.dt.bfloat16
ALU = mybir.AluOpType
ACT = mybir.ActivationFunctionType
AX = mybir.AxisListType

B, T_IN, D_IN = 32, 256, 23
CTX = 5
T = T_IN - (CTX - 1)
TILE = T // 2
K_IN = CTX * D_IN
D = 128
N_TOK = B * T
CH = 2 * T
N_CH = N_TOK // CH
N_TILES = N_TOK // TILE
HEADS, DH, R = 8, 16, 2
DQ = DH + R
Q_PROJ, KV_PROJ = D // 2, 2 * D // 3
ROT = HEADS * R
EXPERTS, HID = 8, 256
EPS = 1e-5
SCALE = float(1.0 / np.sqrt(np.float32(DQ)))
STACK = 3 * DQ
SLOT = 64
TW = SLOT + STACK + 2
PROJ_W = 3 * D + 4 * ROT
STAT_W = D + Q_PROJ + KV_PROJ + 1


N_PREP = 14
N_POOL_C = 13
R_DIFF, R_END = 17, 23
N_CHAIN = 7
LAG_W = 3


def batches(n, top):
    return min(max(n, 0), top) if isinstance(n, int) else n


def before(b, parity):
    return (b - parity) // 2


def wait(eng, sem, value):
    if not isinstance(value, int) or value > 0:
        eng.wait_ge(sem, value)


def pipeline(eng, n, lag, step, unroll=2):
    head = lag + 1 + (n - lag - 1) % unroll
    for s in range(head):
        step(s, s % unroll, lambda k, s=s: 0 <= s - k < n)
    with eng.Fori(head, n - unroll + 1, unroll) as i:
        for p in range(unroll):
            step(i + p, p, lambda k: True)
    for s in range(n, n + lag):
        step(s, s % unroll, lambda k, s=s: 0 <= s - k < n)


def build(nc, A, out):
    ctx = ExitStack()
    with ctx:
        def sb(name, shape, dt=F32, where=ctx):
            return where.enter_context(nc.sbuf_tensor(name, shape, dt))

        def sem(name):
            return ctx.enter_context(nc.semaphore(name))

        h = sb("h", [D, N_TOK])
        eye = sb("eye", [128, 128])
        centre = sb("centre", [D, D])
        w1_hi = sb("w1_hi", [D, EXPERTS, HID], F32R)
        w1_lo = sb("w1_lo", [D, EXPERTS, HID], F32R)
        w2_hi = sb("w2_hi", [D, EXPERTS, 2, D], F32R)
        w2_lo = sb("w2_lo", [D, EXPERTS, 2, D], F32R)
        be1 = sb("be1_sb", [D, EXPERTS, 2])
        be2 = sb("be2_sb", [D, EXPERTS])
        gw1 = sb("gw1_sb", [D, 64])
        gw1_hi = sb("gw1_hi", [D, 64], F32R)
        gw1_lo = sb("gw1_lo", [D, 64], F32R)
        gb1 = sb("gb1_sb", [64, 1])
        gw2 = sb("gw2_sb", [65, EXPERTS])
        rank = sb("rank_sb", [TILE, EXPERTS])
        scratch = nc.dram_tensor("combine_scratch", [4, 16, EXPERTS, TILE], F32).ap()

        early = ExitStack()
        with early:
            def eb(name, shape, dt=F32):
                return sb(name, shape, dt, early)
            vecs = eb("vecs", [D, 16])
            bn = eb("bn", [D, N_CH, 6])
            bn_mv = eb("bn_mv", [D, 2])
            wdq = eb("wdq", [D, Q_PROJ])
            wdkv = eb("wdkv", [D, KV_PROJ + 1])
            wq_raw = eb("wq_raw", [Q_PROJ, D + 2 * ROT])
            wk_raw = eb("wk_raw", [KV_PROJ, 2 * D])
            wkr = eb("wkr", [D, 2 * ROT])
            wo_t = eb("wo_t", [D, D])
            q_gb = eb("q_gb", [Q_PROJ, 2])
            kv_gb = eb("kv_gb", [KV_PROJ, 2])
            cell = eb("cell", [TILE, 2])
            held = eb("held", [1, 2])
            eye_r = eb("eye_r", [TILE, TILE], F32R)
            v_bias = eb("v_bias", [D, 1])
            o_bias = eb("o_bias", [D, 1])
            stat_hi = eb("stat_hi", [D, STAT_W], F32R)
            stat_lo = eb("stat_lo", [D, STAT_W], F32R)
            proj_hi = eb("proj_hi", [D, PROJ_W], F32R)
            proj_lo = eb("proj_lo", [D, PROJ_W], F32R)
            bias_row = eb("bias_row", [TILE, 2 * D + 2 * ROT])
            trig = eb("trig_sb", [TILE, 2, 4 * ROT])
            eye_bf = eb("eye_bf", [TILE, TILE], BF16)
            mask = eb("mask_sb", [TILE, 4, TILE], BF16)
            hs_hi = [eb(f"hs_hi{i}", [D, CH], F32R) for i in range(2)]
            hs_lo = [eb(f"hs_lo{i}", [D, CH], F32R) for i in range(2)]
            squares = [eb(f"squares{i}", [TILE, 4, STAT_W]) for i in range(2)]
            sums = eb("sums", [TILE, 3, N_TILES])
            varis = eb("varis", [TILE, 3, N_TILES])
            rstd = eb("rstd", [TILE, 3, N_TILES])
            rwork = eb("rwork", [TILE, 3, N_TILES])
            v_all = eb("v_all", [128, B, 2, D])
            slots = [eb(f"slots{i}", [TILE, 2, 2, HEADS, SLOT], F32R) for i in range(2)]
            v_ones = [eb(f"v_ones{i}", [TILE, 2, HEADS, 32]) for i in range(2)]
            with ExitStack() as conv_mem:
                def cb(name, shape, dt=F32):
                    return sb(name, shape, dt, conv_mem)
                frames = cb("frames", [K_IN, B * T_IN])
                conv_w = cb("conv_w", [K_IN, D])
                ones = cb("ones", [128, TILE])
                bq_wide = cb("bq_wide", [Q_PROJ, TILE])
                bkv_wide = cb("bkv_wide", [KV_PROJ, TILE])
                yq_t = cb("yq_t", [Q_PROJ, D])
                yk_t = cb("yk_t", [KV_PROJ, D])
                wq_g = cb("wq_g", [Q_PROJ, D + 2 * ROT])
                wk_g = cb("wk_g", [KV_PROJ, 2 * D])
            with ExitStack() as att_mem:
                def ab(name, shape, dt=F32):
                    return sb(name, shape, dt, att_mem)
                x_tok = [ab(f"x_tok{i}", [TILE, 2, 2, HEADS, DQ]) for i in range(2)]
                rope = [ab(f"rope{i}", [TILE, 2, 2, 2, ROT]) for i in range(2)]
                stack = [ab(f"stack{i}", [128, 2, 4, T], F32R) for i in range(2)]
                neg_max = [ab(f"neg_max{i}", [TILE, 2, 2, 4]) for i in range(2)]
                neg_max_t = [ab(f"neg_max_t{i}", [HEADS, T], F32R) for i in range(2)]
                p0 = [ab(f"p0_{i}", [TILE, 2, 4, T]) for i in range(2)]
                p1 = [ab(f"p1_{i}", [TILE, 2, 4, TILE]) for i in range(2)]
                o_sb = [ab(f"o_sb{i}", [D, 2, T]) for i in range(2)]
                o_rec = [ab(f"o_rec{i}", [TILE, 16, 1]) for i in range(2)]
                o_tok = [ab(f"o_tok{i}", [TILE, 2, D]) for i in range(2)]
                o_feat = [ab(f"o_feat{i}", [D, T]) for i in range(2)]

        xh = sb("xh", [D, N_TOK], F32R)
        xl = sb("xl", [D, N_TOK], F32R)
        comb_t = sb("comb_t", [128, 4, TILE])
        act_f = [sb(f"act_f{i}", [D, 2, CH]) for i in range(2)]
        act_hi = [sb(f"act_hi{i}", [D, 2, CH], F32R) for i in range(2)]
        act_lo = [sb(f"act_lo{i}", [D, 2, CH], F32R) for i in range(2)]
        part = [sb(f"part{i}", [D, CH]) for i in range(2)]
        total = [sb(f"total{i}", [D, CH]) for i in range(2)]
        with ExitStack() as gate_mem:
            def gb(name, shape, dt=F32):
                return sb(name, shape, dt, gate_mem)
            hn = [gb(f"hn{i}", [D, CH]) for i in range(2)]
            sq2 = [gb(f"sq2_{i}", [TILE, 4, D]) for i in range(2)]
            st2 = [gb(f"st2_{i}", [TILE, 8, 4]) for i in range(2)]
            consts4 = gb("consts4", [TILE, 3, 4])
            xn = [gb(f"xn{i}", [TILE, 4, D]) for i in range(2)]
            gh = [gb(f"gh{i}", [65, CH]) for i in range(2)]
            rt = [gb(f"rt{i}", [TILE, N_TILES, EXPERTS]) for i in range(6)]
            rs = gb("rs", [TILE, 6, N_TILES])
        comb = [sb(f"comb{i}", [D, 4, EXPERTS, TILE]) for i in range(2)]

        ps = ctx.enter_context(nc.psum_tensor("ps", [128, 8, 512], F32))

        def bank(k, rows, cols, at=0):
            return ps[0:rows, k, at:at + cols]

        (s_conv_in, s_consts, s_weights, s_ffn_in, s_raw, s_pool_c, s_prep, s_fold, s_fold_hi, s_fold_lo,
         s_conv, s_relu, s_bn, s_bn_sqrt, s_normed, s_hs_hi, s_hs_lo, s_stat, s_square, s_sums, s_root,
         s_rstd, s_hi, s_lo, s_proj, s_scaled, s_pool, s_rope, s_slot_hi, s_slot_lo, s_tr, s_tr_act,
         s_tr_dve, s_score, s_max, s_mt, s_mt_out, s_m_dma0, s_m_dma1, s_st, s_exp, s_masked, s_v_ones, s_v,
         s_pv, s_o_out, s_ot, s_rec, s_o_norm, s_nt, s_nt_out, s_wo, s_resid, s_hn, s_cen, s_sq2, s_chain2,
         s_var2, s_root2, s_xn, s_xt, s_xh, s_xl, s_gate, s_gh, s_logit, s_router, s_rexp, s_ct, s_ct_out,
         s_scratch, s_comb_in0, s_comb_in1, s_up, s_gelu, s_act_hi, s_split, s_down, s_part, s_total,
         s_out0, s_out1, s_wsplit, s_cell) = (sem(n) for n in (
            "s_conv_in s_consts s_weights s_ffn_in s_raw s_pool_c s_prep s_fold s_fold_hi s_fold_lo "
            "s_conv s_relu s_bn s_bn_sqrt s_normed s_hs_hi s_hs_lo s_stat s_square s_sums s_root "
            "s_rstd s_hi s_lo s_proj s_scaled s_pool s_rope s_slot_hi s_slot_lo s_tr s_tr_act s_tr_dve "
            "s_score s_max s_mt s_mt_out s_m_dma0 s_m_dma1 s_st s_exp s_masked s_v_ones s_v s_pv s_o_out "
            "s_ot s_rec s_o_norm s_nt s_nt_out s_wo s_resid s_hn s_cen s_sq2 s_chain2 s_var2 s_root2 "
            "s_xn s_xt s_xh s_xl s_gate s_gh s_logit s_router s_rexp s_ct s_ct_out s_scratch "
            "s_comb_in0 s_comb_in1 s_up s_gelu s_act_hi s_split s_down s_part s_total s_out0 s_out1 "
            "s_wsplit s_cell").split())
        s_m_dma, s_comb_in, s_out = (s_m_dma0, s_m_dma1), (s_comb_in0, s_comb_in1), (s_out0, s_out1)

        Y, S, P, M0, M1 = 0, 2, 4, 6, 7
        TR = (M0, Y)
        CEN, XT, GATE, LOGIT, CT, UP, DOWN = (0, 1, 5, 7), 2, 4, 6, 7, 0, 4

        WEIGHTS = [(wdq[:, :], A["wdq"]), (wdkv[:, 0:KV_PROJ], A["wdkv"]), (wq_raw[:, 0:D], A["wuq"]),
                   (wq_raw[:, D:D + ROT], A["wqr"]), (wk_raw[:, :], A["wukv"]), (wkr[:, 0:ROT], A["wkr"]),
                   (wo_t[:, :], A["wo_t"]), (q_gb[:, :], A["q_gb"]), (kv_gb[:, :], A["kv_gb"])]
        CONSTS = [(eye[:, :], A["eye"]), (centre[:, :], A["centre"]), (trig[:, :, :], A["trig"]),
                  (eye_bf[:, :], A["eye_bf"]), (mask[:, :, :], A["mask"]), (rank[:, :], A["rank"])]
        FFN_IN = [(be1[:, :, :], A["be1"]), (be2[:, :], A["be2"]), (gw1[:, :], A["gw1"]),
                  (gb1[:, :], A["gb1"]), (gw2[:, :], A["gw2"])]
        v_flat = v_all[:, :, :, :].rearrange("p b t d -> p (b t d)")
        w1_raw, w2_raw = v_flat[:, 0:EXPERTS * HID], v_flat[:, EXPERTS * HID:2 * EXPERTS * HID]
        W1_HI, W1_LO = (w[:, :, :].rearrange("p e n -> p (e n)") for w in (w1_hi, w1_lo))
        W2_HI, W2_LO = (w[:, :, :, :].rearrange("p e a n -> p (e a n)") for w in (w2_hi, w2_lo))

        block = ctx.enter_context(nc.Block())

        @block.sync
        def _(sp):
            sp.dma_start(conv_w[:, :], A["conv_w"]).then_inc(s_conv_in, 16)
            sp.dma_start(vecs[:, 0:3], A["vecs"]).then_inc(s_conv_in, 16)
            for i in range(CTX):
                n = B * T_IN - (CTX - 1)
                sp.dma_start(frames[i * D_IN:(i + 1) * D_IN, 0:n], A["x_t"][:, i:i + n]).then_inc(s_conv_in, 16)
            for dst, src in WEIGHTS:
                sp.dma_start(dst, src).then_inc(s_weights, 16)
            for dst, src in CONSTS:
                sp.dma_start(dst, src).then_inc(s_consts, 16)
            sp.dma_start(w1_raw, A["we1"]).then_inc(s_raw, 16)
            sp.dma_start(w2_raw, A["we2"]).then_inc(s_raw, 16)
            for dst, src in FFN_IN:
                sp.dma_start(dst, src).then_inc(s_ffn_in, 16)

            def move_max(s, p, live):
                if live(4):
                    b = s - 4
                    wait(sp, s_mt_out, b + 1)
                    for half in range(2):
                        row = SLOT * half + STACK
                        sp.dma_start(stack[p][row:row + 1, 0, :, :].bitcast(F32),
                                     neg_max_t[p][4 * half:4 * half + 4, :].bitcast(F32)).then_inc(s_m_dma[p], 16)

            pipeline(sp, B, 6, move_max)

            sp.wait_ge(s_ct_out, 1)
            sp.dma_start(scratch.rearrange("k t e i -> (t e) k i"), comb_t[:, :, :]).then_inc(s_scratch, 16)
            sp.wait_ge(s_scratch, 16)
            n_comb = 4 * EXPERTS * TILE
            flat = scratch.rearrange("k t e i -> (k t e i)").rearrange("(a n) -> a n", a=1)

            def load_comb(c, p):
                sp.dma_start(comb[p][:, :, :, :].rearrange("p j e i -> p (j e i)"),
                             flat[:, bass.ds(c * n_comb, n_comb)].to_broadcast([D, n_comb]))\
                  .then_inc(s_comb_in[p], 16)

            def store(c, p):
                sp.wait_ge(s_total, EXPERTS * c + EXPERTS)
                sp.dma_start(out[:, bass.ds(c * CH, CH)], total[p][:, :]).then_inc(s_out[p], 16)

            for c in range(2):
                load_comb(c, c)
            with sp.Fori(0, N_CH - 3, 2) as i:
                for p in range(2):
                    store(i + p, p)
                    load_comb(i + p + 2, p)
            for c in range(N_CH - 2, N_CH):
                store(c, c % 2)
            for p in range(2):
                sp.wait_ge(s_out[p], 16 * (N_CH // 2))

        @block.gpsimd
        def _(pool):
            pool.memset(held[:, :], 0.0)
            pool.memset(cell[:, 0:1], 0.0).then_inc(s_cell, 1)
            pool.memset(cell[:, 1:2], 1.0).then_inc(s_cell, 1)
            pool.wait_ge(s_cell, 2)
            pool.memset(ones[:, :], 1.0).then_inc(s_pool_c, 1)
            pool.memset(wdkv[:, KV_PROJ:KV_PROJ + 1], 0.0).then_inc(s_pool_c, 1)
            for p in range(2):
                for side in range(2):
                    fill = cell[:, side:side + 1].rearrange("p (a b c) -> p a b c", a=1, b=1)
                    pool.tensor_copy(slots[p][:, :, side, :, STACK:],
                                     fill.to_broadcast([TILE, 2, HEADS, SLOT - STACK])).then_inc(s_pool_c, 1)
                pool.memset(v_ones[p][:, :, :, DH:], 1.0).then_inc(s_pool_c, 1)
            pool.wait_ge(s_fold_lo, 4)
            pool.wait_ge(s_consts, 16 * len(CONSTS))

            def step(s, p, live):
                q = 1 - p
                if live(1):
                    b = s - 1
                    pool.wait_ge(s_scaled, 2 * b + 2)
                    ra = rope[q][:, :, :, :, :].rearrange("p t s a r -> p (t s a r)")
                    pool.tensor_tensor(ra, ra, trig[:, :, :].rearrange("p t r -> p (t r)"), ALU.mult)\
                        .then_inc(s_pool, 1)
                    pool.wait_ge(s_pool, b + 1)
                    rr = rope[q][:, :, :, :, :].rearrange("p t s a (h r) -> p (t s) a h r", r=R)
                    pool.tensor_tensor(x_tok[q][:, :, :, :, DH:].rearrange("p t s h r -> p (t s) h r"),
                                       rr[:, :, 0], rr[:, :, 1], ALU.add).then_inc(s_rope, 1)
                if live(4):
                    b = s - 4
                    for i, (units, t) in enumerate(((2, p1[p][:, :, :, :]), (6, p0[p][:, :, :, 0:TILE]))):
                        wait(pool, s_masked, 2 * b + i)
                        pool.wait_ge(s_exp, 6 * b + units)
                        pool.tensor_tensor(held[:, 0:1], held[:, 1:2], held[:, 1:2], ALU.mult)
                        v = t.rearrange("p a b q -> p (a b) q")
                        pool.affine_select(out=v, in_=v, compare_op=ALU.is_ge, fill=0.0, base=0,
                                           pattern=[[0, HEADS], [1, TILE]], channel_multiplier=-1)\
                            .then_inc(s_masked, 1)

            pipeline(pool, B, 6, step)

            pool.wait_ge(s_resid, B)
            for p in range(2):
                pool.memset(gh[p][64:65, :], 1.0).then_inc(s_pool_c, 1)
            pool.wait_ge(s_pool_c, N_POOL_C - 3)
            for k, value in enumerate((EPS, -0.5, 1.5)):
                pool.memset(consts4[:, k, :], value).then_inc(s_pool_c, 1)
            pool.wait_ge(s_pool_c, N_POOL_C)
            eps4, half4, more4 = (consts4[:, k, :] for k in range(3))

            def norm(s, k4, live):
                p = k4 % 2
                if live(2):
                    c = s - 2
                    mean, v, r, w, r2 = (st2[p][:, k, :] for k in range(5))
                    pool.wait_ge(s_var2, c + 1)
                    wait(pool, s_xn, c - 1)
                    pool.tensor_tensor(v, mean, eps4, ALU.add).then_inc(s_chain2, 1)
                    for k, (o, a, b, op) in enumerate(((r, v, half4, ALU.pow), (w, r, r, ALU.mult), (w, w, v, ALU.mult),
                                                       (w, w, half4, ALU.mult), (w, w, more4, ALU.add),
                                                       (r2, r, w, ALU.mult))):
                        pool.wait_ge(s_chain2, N_CHAIN * c + k + 1)
                        pool.tensor_tensor(o, a, b, op).then_inc(s_chain2, 1)

            pipeline(pool, N_CH, 6, norm, 4)

            def add(c, p):
                for e in range(EXPERTS):
                    pool.wait_ge(s_part, EXPERTS * c + e + 1)
                    if e == 0:
                        wait(pool, s_out[p], 16 * before(c, p))
                    else:
                        pool.wait_ge(s_total, EXPERTS * c + e)
                    acc = h[:, bass.ds(c * CH, CH)] if e == 0 else total[p][:, :]
                    pool.tensor_tensor(total[p][:, :], acc, part[e % 2][:, :], ALU.add).then_inc(s_total, 1)

            for c in range(2):
                add(c, c)
            with pool.Fori(2, N_CH - 1, 2) as i:
                for p in range(2):
                    add(i + p, p)

        @block.scalar
        def _(act):
            act.wait_ge(s_conv_in, 16 * (2 + CTX))
            with act.Fori(0, N_CH - 3, 4) as i:
                for k in range(4):
                    act.wait_ge(s_conv, i + k + 1)
                    act.activation(h[:, bass.ds((i + k) * CH, CH)], bank(k, D, CH), ACT.Relu,
                                   bias=vecs[:, 0:1]).then_inc(s_relu, 1)
            act.wait_ge(s_fold, 2)
            act.activation(stat_hi[:, :], bank(4, D, STAT_W), ACT.Identity).then_inc(s_fold_hi, 1)
            act.activation(proj_hi[:, :], bank(5, D, PROJ_W), ACT.Identity).then_inc(s_fold_hi, 1)
            act.wait_ge(s_bn, N_CH + 2)
            act.activation(vecs[:, 4:5], vecs[:, 3:4], ACT.Sqrt).then_inc(s_bn_sqrt, 1)

            def stats(s, p, live):
                if live(0):
                    act.wait_ge(s_normed, s + 1)
                    wait(act, s_stat, s - 1)
                    act.activation(hs_hi[p][:, :], h[:, bass.ds(s * CH, CH)], ACT.Identity).then_inc(s_hs_hi, 1)
                if live(2):
                    c = s - 2
                    act.wait_ge(s_stat, c + 1)
                    wait(act, s_sums, c - 1)
                    act.activation(squares[p][:, :, :], ps[0:TILE, 4 * p:4 * p + 4, 0:STAT_W], ACT.Square)\
                        .then_inc(s_square, 1)

            pipeline(act, N_CH, 2, stats)
            act.wait_ge(s_root, 1)
            act.activation(rstd[:, :, :], varis[:, :, :], ACT.Sqrt).then_inc(s_root, 1)

            def exp(b, u, p):
                half, k = u % 2, u // 2
                act.wait_ge(s_st, 6 * b + u + 1)
                if u == 0:
                    wait(act, s_pv, b - 1)
                if k == 0:
                    dst, src = p1[p][:, half, :, :], bank(P + half, TILE, 4 * TILE)
                else:
                    dst, src = p0[p][:, half, 2 * k - 2:2 * k, :], bank(P + half, TILE, 2 * T)
                src = src.rearrange("p (a b) -> p a b", a=4 if k == 0 else 2)
                act.activation(dst, src, ACT.Exp, scale=SCALE).then_inc(s_exp, 1)

            def move_stack(b, side, q):
                act.wait_ge(s_tr, 4 * b + 2 * (1 - side) + 1)
                if side == 1:
                    wait(act, s_st, 6 * (b - 1))
                act.activation(stack[q][0:TW, side, :, 0:TILE],
                               bank(TR[side], TW, 4 * TILE).rearrange("p (a b) -> p a b", a=4),
                               ACT.Identity).then_inc(s_tr_act, 1)

            def attention(s, p, live):
                q = 1 - p
                if live(3):
                    move_stack(s - 3, 1, q)
                    move_stack(s - 3, 0, q)
                if live(4):
                    b = s - 4
                    act.wait_ge(s_mt, b + 1)
                    wait(act, s_m_dma[p], 16 * 2 * before(b, p))
                    act.activation(neg_max_t[p][:, :], bank(S, HEADS, T), ACT.Identity).then_inc(s_mt_out, 1)
                if live(6):
                    b = s - 6
                    act.wait_ge(s_nt, b + 1)
                    wait(act, s_wo, b - 1)
                    act.activation(o_feat[p][:, :], bank(S + 1, D, T), ACT.Identity).then_inc(s_nt_out, 1)
                if live(2):
                    b = s - 2
                    act.wait_ge(s_rope, b + 1)
                    act.wait_ge(s_v, b + 1)
                    wait(act, s_tr, 4 * (b - 1))
                    sl = slots[p]
                    act.activation(sl[:, :, :, :, 0:DQ].rearrange("p t s h d -> p (t s h) d"),
                                   x_tok[p][:, :, :, :, :].rearrange("p t s h d -> p (t s h) d"),
                                   ACT.Identity).then_inc(s_slot_hi, 1)
                    for side in range(2):
                        at = DQ * (1 + side)
                        act.activation(sl[:, :, side, :, at:at + DQ], x_tok[p][:, :, side, :, :],
                                       ACT.Identity).then_inc(s_slot_hi, 1)
                if live(0):
                    wait(act, s_proj, s - 1)
                    act.activation(hs_hi[p][:, 0:T], h[:, bass.ds(s * T, T)], ACT.Identity).then_inc(s_hi, 1)
                if live(5):
                    b = s - 5
                    act.wait_ge(s_pv, b + 1)
                    wait(act, s_ot, b - 1)
                    act.activation(o_sb[q][:, :, :], bank(M0, D, 2 * T).rearrange("p (a b) -> p a b", a=2),
                                   ACT.Identity).then_inc(s_o_out, 1)
                if live(4):
                    for u in range(6):
                        exp(s - 4, u, p)

            pipeline(act, B, 6, attention)

            def gate(s, k4, live):
                p, q = k4 % 2, 1 - k4 % 2
                if live(1):
                    act.wait_ge(s_cen, s)
                    wait(act, s_var2, s - 2)
                    act.activation(sq2[q][:, :, :], bank(CEN[(k4 - 1) % 4], TILE, 4 * D).rearrange("p (a b) -> p a b", a=4),
                                   ACT.Square, scale=float(D ** -0.5)).then_inc(s_sq2, 1)
                if live(4):
                    c = s - 4
                    act.wait_ge(s_xt, c + 1)
                    act.activation(xh[:, bass.ds(c * CH, CH)], bank(XT + p, D, CH), ACT.Identity)\
                        .then_inc(s_xh, 1)
                if live(5):
                    c = s - 5
                    act.wait_ge(s_gate, c + 1)
                    wait(act, s_logit, c - 1)
                    act.activation(gh[q][0:64, :], bank(GATE, 64, CH), ACT.Relu, bias=gb1[:, :])\
                        .then_inc(s_gh, 1)

            pipeline(act, N_CH, 6, gate, 4)
            act.wait_ge(s_router, 2)
            act.activation(rt[0][:, :, :], rt[1][:, :, :], ACT.Exp).then_inc(s_rexp, 1)
            act.wait_ge(s_router, R_DIFF)
            act.activation(rs[:, 4, :], rs[:, 3, :], ACT.Exp).then_inc(s_rexp, 1)

            def gelu(c):
                for e in range(EXPERTS):
                    n = EXPERTS * c + e
                    for half in range(2):
                        act.wait_ge(s_up, 2 * n + half + 1)
                        wait(act, s_split, 2 * (n - 2) + half + 1)
                        act.activation(act_f[e % 2][:, half, :], bank(UP + 2 * (e % 2) + half, D, CH), ACT.Gelu,
                                       bias=be1[:, e, half:half + 1]).then_inc(s_gelu, 1)

            gelu(0)
            with act.Fori(1, N_CH, 1) as c:
                gelu(c)

        @block.vector
        def _(dve):
            V = nc.vector
            count = {}

            def link(ins, s=s_prep):
                count[s] = count.get(s, 0) + 1
                ins.then_inc(s, 1)
                dve.wait_ge(s, count[s])

            def rsqrt_from_root(v, root, r, w, s):
                link(V.reciprocal(r, root), s)
                link(V.tensor_tensor(w, r, r, ALU.mult), s)
                link(V.tensor_tensor(w, w, v, ALU.mult), s)
                link(V.tensor_scalar(w, w, -0.5, 1.5, ALU.mult, ALU.add), s)
                link(V.tensor_tensor(r, r, w, ALU.mult), s)

            dve.wait_ge(s_weights, 16 * len(WEIGHTS))
            dve.wait_ge(s_pool_c, 2)
            dve.wait_ge(s_conv_in, 16 * (2 + CTX))
            for w, n, c in ((wdq, Q_PROJ, 11), (wdkv, KV_PROJ, 13)):
                link(V.tensor_reduce(vecs[:, c:c + 1], w[:, 0:n], AX.X, ALU.add))
                link(V.tensor_scalar(vecs[:, c + 1:c + 2], vecs[:, c:c + 1], -1.0 / n, None, ALU.mult))
                link(V.tensor_scalar(w[:, 0:n], w[:, 0:n], vecs[:, c + 1:c + 2], None, ALU.add))
            for w, at in ((wq_raw, D), (wkr, 0)):
                a = w[:, at:at + ROT].rearrange("p (h r) -> p r h", r=R)
                r = w[:, at + ROT:at + 2 * ROT].rearrange("p (h r) -> p r h", r=R)
                link(V.tensor_scalar(r[:, 0], a[:, 1], -1.0, None, ALU.mult))
                link(V.tensor_copy(r[:, 1], a[:, 0]))
            link(V.tensor_scalar(wq_g[:, :], wq_raw[:, :], q_gb[:, 0:1], None, ALU.mult))
            link(V.tensor_scalar(wk_g[:, :], wk_raw[:, :], kv_gb[:, 0:1], None, ALU.mult))
            link(V.tensor_scalar(bq_wide[:, :], ones[0:Q_PROJ, :], q_gb[:, 1:2], None, ALU.mult))
            link(V.tensor_scalar(bkv_wide[:, :], ones[0:KV_PROJ, :], kv_gb[:, 1:2], None, ALU.mult))
            assert count[s_prep] == N_PREP
            dve.wait_ge(s_fold, 1)
            link(V.tensor_copy(yq_t[:, :], bank(6, Q_PROJ, D)))
            link(V.tensor_copy(yk_t[:, :], bank(6, KV_PROJ, D, D)))
            dve.wait_ge(s_fold, 2)
            V.tensor_copy(v_bias[:, :], bank(7, D, 1, 300)).then_inc(s_fold_lo, 1)
            V.tensor_copy(bias_row[:, :], bank(7, TILE, 2 * D + 2 * ROT)).then_inc(s_fold_lo, 1)
            dve.wait_ge(s_fold, 3)
            V.tensor_copy(o_bias[:, :], bank(6, D, 1, 300)).then_inc(s_fold_lo, 1)

            dve.wait_ge(s_consts, 16 * len(CONSTS))
            V.tensor_copy(eye_r[:, :], eye[0:TILE, 0:TILE]).then_inc(s_fold_lo, 1)

            with dve.Fori(0, N_CH - 3, 4) as i:
                for k in range(4):
                    dve.wait_ge(s_relu, i + k + 1)
                    V.bn_stats(bn[:, bass.ds(i + k, 1), :].rearrange("p a b -> p (a b)"),
                               h[:, bass.ds((i + k) * CH, CH)]).then_inc(s_bn, 1)
            dve.wait_ge(s_fold_hi, 2)
            V.tensor_tensor(stat_lo[:, :], bank(4, D, STAT_W), stat_hi[:, :].bitcast(F32), ALU.subtract)\
                .then_inc(s_fold_lo, 1)
            V.tensor_tensor(proj_lo[:, :], bank(5, D, PROJ_W), proj_hi[:, :].bitcast(F32), ALU.subtract)\
                .then_inc(s_fold_lo, 1)
            dve.wait_ge(s_bn, N_CH)
            V.bn_aggr(bn_mv[:, :], bn[:, :, :].rearrange("p a b -> p (a b)")).then_inc(s_bn, 1)
            dve.wait_ge(s_bn, N_CH + 1)
            V.tensor_scalar(vecs[:, 3:4], bn_mv[:, 1:2], EPS, None, ALU.add).then_inc(s_bn, 1)
            dve.wait_ge(s_bn_sqrt, 1)
            rsqrt_from_root(vecs[:, 3:4], vecs[:, 4:5], vecs[:, 5:6], vecs[:, 6:7], s_prep)
            link(V.tensor_tensor(vecs[:, 8:9], vecs[:, 1:2], vecs[:, 5:6], ALU.mult))
            link(V.tensor_tensor(vecs[:, 9:10], bn_mv[:, 0:1], vecs[:, 8:9], ALU.mult))
            link(V.tensor_tensor(vecs[:, 10:11], vecs[:, 2:3], vecs[:, 9:10], ALU.subtract))

            def stats(s, p, live):
                q = 1 - p
                if live(0):
                    hc = h[:, bass.ds(s * CH, CH)]
                    V.tensor_scalar(hc, hc, vecs[:, 8:9], vecs[:, 10:11], ALU.mult, ALU.add).then_inc(s_normed, 1)
                if live(1):
                    c = s - 1
                    dve.wait_ge(s_hs_hi, c + 1)
                    wait(dve, s_stat, c - 1)
                    V.tensor_tensor(hs_lo[q][:, :], h[:, bass.ds(c * CH, CH)], hs_hi[q][:, :].bitcast(F32),
                                    ALU.subtract).then_inc(s_hs_lo, 1)
                if live(2):
                    c = s - 2
                    dve.wait_ge(s_square, c + 1)
                    for k, (at, n) in enumerate(((0, D), (D, Q_PROJ), (D + Q_PROJ, KV_PROJ))):
                        last = V.tensor_reduce(sums[:, k, bass.ds(4 * c, 4)], squares[p][:, :, at:at + n],
                                               AX.X, ALU.add)
                    last.then_inc(s_sums, 1)

            pipeline(dve, N_CH, 2, stats)
            dve.wait_ge(s_sums, N_CH)
            link(V.tensor_scalar(varis[:, 0, :], sums[:, 0, :], 1.0 / D, EPS, ALU.mult, ALU.add))
            link(V.tensor_scalar(rwork[:, 0, :], varis[:, 0, :], EPS, None, ALU.mult))
            link(V.scalar_tensor_tensor(varis[:, 1, :], sums[:, 1, :], 1.0 / Q_PROJ, rwork[:, 0, :],
                                        op0=ALU.mult, op1=ALU.add))
            V.scalar_tensor_tensor(varis[:, 2, :], sums[:, 2, :], 1.0 / KV_PROJ, rwork[:, 0, :],
                                   op0=ALU.mult, op1=ALU.add).then_inc(s_root, 1)
            dve.wait_ge(s_raw, 32)
            dve.wait_ge(s_ffn_in, 16 * len(FFN_IN))
            for hi, lo, raw in ((W1_HI, W1_LO, w1_raw), (W2_HI, W2_LO, w2_raw), (gw1_hi[:, :], gw1_lo[:, :], gw1[:, :])):
                link(V.tensor_copy(hi, raw), s_wsplit)
                link(V.tensor_tensor(lo, raw, hi.bitcast(F32), ALU.subtract), s_wsplit)
            dve.wait_ge(s_root, 2)
            rsqrt_from_root(varis[:, :, :], rstd[:, :, :], sums[:, :, :], rwork[:, :, :], s_prep)
            r_all = sums

            def per_token(k, b, shape):
                v = r_all[:, k, bass.ds(2 * b, 2)]
                return (v.rearrange("p (t a) -> p t a", a=1) if len(shape) == 3 else
                        v.rearrange("p (t a c) -> p t a c", a=1, c=1)).to_broadcast(shape)

            def scale(b, q):
                dve.wait_ge(s_proj, b + 1)
                wait(dve, s_slot_hi, 3 * (b - 1))
                y = ps[0:TILE, Y:Y + 2, :]
                V.tensor_tensor(rope[q][:, :, 1, :, :].rearrange("p t a r -> p t (a r)"), y[:, :, 3 * D + 2 * ROT:PROJ_W],
                                per_token(0, b, [TILE, 2, 2 * ROT]), ALU.mult)
                for t in range(2):
                    r_q, r_kv = (r_all[:, k, bass.ds(2 * b + t, 1)] for k in (1, 2))
                    V.scalar_tensor_tensor(rope[q][:, t, 0, :, :].rearrange("p a r -> p (a r)"),
                                           y[:, t, 3 * D:3 * D + 2 * ROT], r_q, bias_row[:, 2 * D:],
                                           op0=ALU.mult, op1=ALU.add).then_inc(s_scaled, 1)
                for t in range(2):
                    r_q, r_kv = (r_all[:, k, bass.ds(2 * b + t, 1)] for k in (1, 2))
                    for side, r in ((0, r_q), (1, r_kv)):
                        V.scalar_tensor_tensor(x_tok[q][:, t, side, :, 0:DH],
                                               y[:, t, side * D:side * D + D].rearrange("p (h d) -> p h d", d=DH), r,
                                               bias_row[:, side * D:side * D + D].rearrange("p (h d) -> p h d", d=DH),
                                               op0=ALU.mult, op1=ALU.add)
                V.tensor_tensor(v_all[0:TILE, bass.ds(b, 1), :, :].rearrange("p b t d -> p (b t) d"),
                                y[:, :, 2 * D:3 * D], per_token(2, b, [TILE, 2, D]), ALU.mult).then_inc(s_v, 1)

            def neg_maximum(b, u, q):
                half, k = u % 2, u // 2
                dve.wait_ge(s_score, 6 * b + u + 1)
                if u == 0:
                    wait(dve, s_mt, b - 1)
                if k == 0:
                    dst, src = neg_max[q][:, 0, half, :], bank(S + half, TILE, 4 * TILE)
                else:
                    dst, src = neg_max[q][:, 1, half, 2 * k - 2:2 * k], bank(S + half, TILE, 2 * T)
                src = src.rearrange("p (a b) -> p a b", a=4 if k == 0 else 2)
                V.tensor_reduce(dst, src, AX.X, ALU.max, negate=True).then_inc(s_max, 1)

            def attention(s, p, live):
                q = 1 - p
                if live(3):
                    b = s - 3
                    for side in (1, 0):
                        dve.wait_ge(s_tr, 4 * b + 2 * (1 - side) + 2)
                        if side == 1:
                            wait(dve, s_st, 6 * (b - 1))
                        V.tensor_copy(stack[q][0:TW, side, :, TILE:],
                                      bank(TR[side] + 1, TW, 4 * TILE).rearrange("p (a b) -> p a b", a=4))\
                            .then_inc(s_tr_dve, 1)
                if live(4):
                    b = s - 4
                    dve.wait_ge(s_v, b + 1)
                    wait(dve, s_pv, b - 1)
                    V.tensor_copy(v_ones[p][:, :, :, 0:DH].rearrange("p t h d -> p (t h) d"),
                                  v_all[0:TILE, bass.ds(b, 1), :, :].rearrange("p b t (h d) -> p (b t h) d", d=DH))\
                        .then_inc(s_v_ones, 1)
                if live(2):
                    b = s - 2
                    dve.wait_ge(s_slot_hi, 3 * b + 1)
                    for side in range(2):
                        at = DQ * (2 - side)
                        V.tensor_tensor(slots[p][:, :, side, :, at:at + DQ], x_tok[p][:, :, side, :, :],
                                        slots[p][:, :, side, :, 0:DQ].bitcast(F32), ALU.subtract).then_inc(s_slot_lo, 1)
                if live(1):
                    scale(s - 1, q)
                if live(6):
                    b = s - 6
                    dve.wait_ge(s_wo, b + 1)
                    hb = h[:, bass.ds(b * T, T)]
                    V.scalar_tensor_tensor(hb, bank(M1, D, T), o_bias[:, :], hb, op0=ALU.add, op1=ALU.add)\
                        .then_inc(s_resid, 1)
                if live(3):
                    neg_maximum(s - 3, 0, q)
                    neg_maximum(s - 3, 1, q)
                if live(5):
                    b = s - 5
                    dve.wait_ge(s_ot, b + 1)
                    o = bank(M1, TILE, 512).rearrange("p (a c) -> p a c", c=32)
                    V.reciprocal(o_rec[q][:, :, :], o[:, :, DH:DH + 1]).then_inc(s_rec, 1)
                    dve.wait_ge(s_rec, b + 1)
                    wait(dve, s_nt, b - 1)
                    V.tensor_tensor(o_tok[q][:, :, :].rearrange("p t (a d) -> p (t a) d", d=DH), o[:, :, 0:DH],
                                    o_rec[q][:, :, :].to_broadcast([TILE, 16, DH]), ALU.mult).then_inc(s_o_norm, 1)
                if live(0):
                    dve.wait_ge(s_hi, s + 1)
                    wait(dve, s_proj, s - 1)
                    V.tensor_tensor(hs_lo[p][:, 0:T], h[:, bass.ds(s * T, T)], hs_hi[p][:, 0:T].bitcast(F32),
                                    ALU.subtract).then_inc(s_lo, 1)
                if live(3):
                    neg_maximum(s - 3, 2, q)
                if live(3):
                    neg_maximum(s - 3, 3, q)
                if live(3):
                    neg_maximum(s - 3, 4, q)
                if live(3):
                    neg_maximum(s - 3, 5, q)

            pipeline(dve, B, 6, attention)

            def norm(s, k4, live):
                p, q = k4 % 2, 1 - k4 % 2
                if live(0):
                    if not isinstance(s, int) or s == 0:
                        dve.wait_ge(s_resid, B)
                    wait(dve, s_cen, s - 1)
                    V.tensor_copy(hn[p][:, :], h[:, bass.ds(s * CH, CH)]).then_inc(s_hn, 1)
                if live(3):
                    c = s - 3
                    dve.wait_ge(s_chain2, N_CHAIN * c + N_CHAIN)
                    wait(dve, s_xt, c - 1)
                    V.tensor_tensor(xn[q][:, :, :], bank(CEN[(k4 - 3) % 4], TILE, 4 * D).rearrange("p (a b) -> p a b", a=4),
                                    st2[q][:, 4, :].rearrange("p (a b) -> p a b", b=1).to_broadcast([TILE, 4, D]),
                                    ALU.mult).then_inc(s_xn, 1)
                if live(1):
                    c = s - 1
                    dve.wait_ge(s_sq2, c + 1)
                    V.tensor_reduce(st2[q][:, 0, :], sq2[q][:, :, :], AX.X, ALU.add).then_inc(s_var2, 1)
                if live(4):
                    c = s - 4
                    dve.wait_ge(s_xh, c + 1)
                    V.tensor_tensor(xl[:, bass.ds(c * CH, CH)], bank(XT + p, D, CH),
                                    xh[:, bass.ds(c * CH, CH)].bitcast(F32), ALU.subtract).then_inc(s_xl, 1)

            pipeline(dve, N_CH, 6, norm, 4)

            shape = [TILE, N_TILES, EXPERTS]

            def over(v):
                return v.rearrange("p (t a) -> p t a", a=1).to_broadcast(shape)

            def first_largest(v, top, sel, tmp):
                link(V.tensor_reduce(top, v, AX.X, ALU.max), s_router)
                link(V.tensor_tensor(sel, v, over(top), ALU.is_equal), s_router)
                link(V.tensor_tensor(sel, sel, rank[:, :].rearrange("p (a e) -> p a e", a=1).to_broadcast(shape),
                                     ALU.mult), s_router)
                link(V.tensor_reduce(tmp, sel, AX.X, ALU.max), s_router)
                link(V.tensor_tensor(sel, sel, over(tmp), ALU.is_equal), s_router)

            dve.wait_ge(s_logit, N_CH)
            logits = bank(LOGIT, TILE, 512).rearrange("p (t e) -> p t e", e=EXPERTS)
            t = [x[:, :, :] for x in rt]
            r = [rs[:, k, :] for k in range(6)]
            link(V.tensor_reduce(r[0], logits, AX.X, ALU.max), s_router)
            link(V.tensor_tensor(t[1], logits, over(r[0]), ALU.subtract), s_router)
            dve.wait_ge(s_rexp, 1)
            link(V.tensor_reduce(r[1], t[0], AX.X, ALU.add), s_router)
            link(V.reciprocal(r[2], r[1]), s_router)
            link(V.tensor_tensor(t[2], t[0], over(r[2]), ALU.mult), s_router)
            first_largest(t[2], r[0], t[3], r[1])
            link(V.scalar_tensor_tensor(t[4], t[3], -2.0, t[2], op0=ALU.mult, op1=ALU.add), s_router)
            first_largest(t[4], r[2], t[5], r[1])
            link(V.tensor_tensor(r[3], r[2], r[0], ALU.subtract), s_router)
            assert count[s_router] == R_DIFF
            dve.wait_ge(s_rexp, 2)
            link(V.tensor_scalar(r[5], r[4], 1.0, None, ALU.add), s_router)
            link(V.reciprocal(r[1], r[5]), s_router)
            link(V.tensor_tensor(r[2], r[4], r[1], ALU.mult), s_router)
            link(V.tensor_tensor(t[0], t[3], over(r[1]), ALU.mult), s_router)
            link(V.tensor_tensor(t[1], t[5], over(r[2]), ALU.mult), s_router)
            link(V.tensor_tensor(t[2], t[0], t[1], ALU.add), s_router)
            assert count[s_router] == R_END
            dve.wait_ge(s_ct, 1)
            V.tensor_copy(comb_t[:, :, :], bank(CT, 128, 4 * TILE).rearrange("p (a b) -> p a b", a=4))\
                .then_inc(s_ct_out, 1)

            def split(n, e):
                for half in range(2):
                    dve.wait_ge(s_gelu, 2 * n + half + 1)
                    if half == 0:
                        wait(dve, s_down, n - 1)
                    V.tensor_copy(act_hi[e % 2][:, half, :], act_f[e % 2][:, half, :]).then_inc(s_act_hi, 1)
                    dve.wait_ge(s_act_hi, 2 * n + half + 1)
                    V.tensor_tensor(act_lo[e % 2][:, half, :], act_f[e % 2][:, half, :],
                                    act_hi[e % 2][:, half, :].bitcast(F32), ALU.subtract).then_inc(s_split, 1)

            def weigh(n, e, c, p):
                dve.wait_ge(s_down, n + 1)
                wait(dve, s_total, n - 1)
                if e == 0:
                    dve.wait_ge(s_comb_in[p], 16 * (before(c, p) + 1))
                V.scalar_tensor_tensor(part[e % 2][:, :].rearrange("p (j i) -> p j i", j=4),
                                       bank(DOWN + e % 2, D, CH).rearrange("p (j i) -> p j i", j=4),
                                       be2[:, e:e + 1], comb[p][:, :, e, :], op0=ALU.add, op1=ALU.mult)\
                    .then_inc(s_part, 1)

            def unit(c, k, live):
                if live:
                    m = (k - LAG_W) % (2 * EXPERTS)
                    cc = c + (k - LAG_W) // EXPERTS
                    weigh(EXPERTS * c + k - LAG_W, m % EXPERTS, cc, m // EXPERTS)
                split(EXPERTS * c + k, k % EXPERTS)

            for k in range(2 * EXPERTS):
                unit(0, k, k >= LAG_W)
            with dve.Fori(2, N_CH - 1, 2) as c:
                for k in range(2 * EXPERTS):
                    unit(c, k, True)
            for k in range(2 * EXPERTS - LAG_W, 2 * EXPERTS):
                weigh(EXPERTS * (N_CH - 2) + k, k % EXPERTS, N_CH - 1, 1)

        @block.tensor
        def _(pe):
            mm = nc.tensor.matmul

            pe.wait_ge(s_consts, 16 * len(CONSTS))
            pe.wait_ge(s_prep, N_PREP)
            mm(bank(6, Q_PROJ, D), wdq[:, :], centre[:, :], start=True, stop=True)
            mm(bank(6, KV_PROJ, D, D), wdkv[:, 0:KV_PROJ], centre[:, :], start=True, stop=True).then_inc(s_fold, 1)
            pe.wait_ge(s_prep, N_PREP + 2)
            mm(bank(4, D, D), centre[:, :], eye[:, :], start=True, stop=True)
            mm(bank(4, D, Q_PROJ, D), centre[:, :], wdq[:, :], start=True, stop=True)
            mm(bank(4, D, KV_PROJ + 1, D + Q_PROJ), centre[:, :], wdkv[:, :], start=True, stop=True)
            mm(bank(5, D, D), yq_t[:, :], wq_g[:, 0:D], start=True, stop=True)
            mm(bank(5, D, 2 * D, D), yk_t[:, :], wk_g[:, :], start=True, stop=True)
            mm(bank(5, D, 2 * ROT, 3 * D), yq_t[:, :], wq_g[:, D:], start=True, stop=True)
            mm(bank(5, D, 2 * ROT, 3 * D + 2 * ROT), centre[:, :], wkr[:, :], start=True, stop=True)
            mm(bank(7, TILE, D), bq_wide[:, :], wq_raw[:, 0:D], start=True, stop=True)
            mm(bank(7, TILE, D, D), bkv_wide[:, :], wk_raw[:, 0:D], start=True, stop=True)
            mm(bank(7, TILE, 2 * ROT, 2 * D), bq_wide[:, :], wq_raw[:, D:], start=True, stop=True)
            mm(bank(7, D, 1, 300), wk_raw[:, D:], kv_gb[:, 1:2], start=True, stop=True).then_inc(s_fold, 1)
            pe.wait_ge(s_fold_lo, 1)
            mm(bank(6, D, 1, 300), wo_t[:, :], v_bias[:, :], start=True, stop=True).then_inc(s_fold, 1)

            pe.wait_ge(s_conv_in, 16 * (2 + CTX))
            def conv(c, k, wait_for):
                wait(pe, s_relu, wait_for)
                rhs = frames[:, bass.ds(c * 2 * T_IN, 2 * T_IN)].rearrange("p (b t) -> p b t", b=2)[:, :, 0:T]
                mm(bank(k, D, CH).rearrange("p (b t) -> p b t", b=2), conv_w[:, :], rhs, start=True, stop=True)\
                    .then_inc(s_conv, 1)

            for k in range(4):
                conv(k, k, 0)
            with pe.Fori(4, N_CH - 3, 4) as i:
                for k in range(4):
                    conv(i + k, k, i + k - 3)

            def three(dst, w_hi, w_lo, x_hi, x_lo, first=True, last=True):
                mm(dst, w_hi, x_hi, start=first, stop=False)
                mm(dst, w_hi, x_lo, start=False, stop=False)
                return mm(dst, w_lo, x_hi, start=False, stop=last)

            def stats(s, p, live):
                if live(1):
                    c, q = s - 1, 1 - p
                    pe.wait_ge(s_hs_lo, c + 1)
                    wait(pe, s_square, c - 1)
                    if not isinstance(s, int) or s < 4:
                        pe.wait_ge(s_fold_lo, 6)
                    for j in range(4):
                        t = slice(j * TILE, j * TILE + TILE)
                        last = three(bank(4 * q + j, TILE, STAT_W), hs_hi[q][:, t], hs_lo[q][:, t],
                                     stat_hi[:, :], stat_lo[:, :])
                    last.then_inc(s_stat, 1)

            pipeline(pe, N_CH, 2, stats)

            def score(b, u, p):
                half, k = u % 2, u // 2
                at, rows = SLOT * half, slice(SLOT * half, SLOT * half + STACK)
                wait(pe, s_max, 6 * b + u - 1)
                if k == 0:
                    dst = bank(S + half, TILE, 4 * TILE).rearrange("p (a b) -> p a b", a=4)
                    for j in range(4):
                        mm(dst[:, j], stack[p][rows, 0, j, 0:TILE], stack[p][rows, 1, j, 0:TILE],
                           start=j == 0, stop=False, skip_group_check=True)
                    mm(dst, eye_bf[:, :], mask[:, :, :], start=False, stop=True, skip_group_check=True)\
                        .then_inc(s_score, 1)
                else:
                    dst = bank(S + half, TILE, 2 * T).rearrange("p (a b) -> p a b", a=2)
                    for j in range(2):
                        m = 2 * k - 2 + j
                        mm(dst[:, j], stack[p][rows, 0, m, TILE:], stack[p][rows, 1, m, :],
                           start=j == 0, stop=False, skip_group_check=True)
                    mm(dst[:, :, TILE:], eye_bf[:, :], mask[:, 0:2, :], start=False, stop=True,
                       skip_group_check=True).then_inc(s_score, 1)

            def score_t(b, u, q):
                half, k = u % 2, u // 2
                rows = slice(SLOT * half, SLOT * half + STACK + 1)
                if u == 0:
                    pe.wait_ge(s_m_dma[q], 32 * (before(b, q) + 1))
                wait(pe, s_exp, 6 * b + u - 1)
                if k == 0:
                    dst = bank(P + half, TILE, 4 * TILE).rearrange("p (a b) -> p a b", a=4)
                    for j in range(4):
                        last = mm(dst[:, j], stack[q][rows, 1, j, TILE:], stack[q][rows, 0, j, TILE:],
                                  start=True, stop=True)
                else:
                    dst = bank(P + half, TILE, 2 * T).rearrange("p (a b) -> p a b", a=2)
                    for j in range(2):
                        m = 2 * k - 2 + j
                        last = mm(dst[:, j], stack[q][rows, 1, m, 0:TILE], stack[q][rows, 0, m, :],
                                  start=True, stop=True)
                last.then_inc(s_st, 1)

            def attention(s, p, live):
                q = 1 - p
                if live(3):
                    b = s - 3
                    pe.wait_ge(s_slot_hi, 3 * b + 3)
                    pe.wait_ge(s_slot_lo, 2 * b + 2)
                    wait(pe, s_o_out, b - 2)
                    wait(pe, s_o_norm, b - 2)
                    wait(pe, s_v, batches(b + 2, B))
                    for side in (1, 0):
                        for t in range(2):
                            for j in range(4):
                                src = slots[q][:, t, side, 2 * j:2 * j + 2, :].rearrange("p h d -> p (h d)")
                                last = mm(bank(TR[side] + t, D, TILE, j * TILE), src, eye_r[:, :], start=True, stop=True)
                            last.then_inc(s_tr, 1)
                if live(4):
                    b = s - 4
                    pe.wait_ge(s_max, 6 * b + 6)
                    for t in range(2):
                        last = nc.tensor.transpose(bank(S, HEADS, TILE, t * TILE),
                                                   neg_max[p][:, t, :, :].rearrange("p a b -> p (a b)"),
                                                   eye[0:TILE, 0:TILE])
                    last.then_inc(s_mt, 1)
                if live(6):
                    b = s - 6
                    pe.wait_ge(s_o_norm, b + 1)
                    for t in range(2):
                        last = nc.tensor.transpose(bank(S + 1, D, TILE, t * TILE), o_tok[p][:, t, :],
                                                   eye[0:TILE, 0:TILE])
                    last.then_inc(s_nt, 1)
                if live(1):
                    b = s - 1
                    pe.wait_ge(s_lo, b + 1)
                    if live(3):
                        pe.wait_ge(s_tr_act, 2 * (s - 3) + 1)
                        pe.wait_ge(s_tr_dve, 2 * (s - 3) + 1)
                    wait(pe, s_v, b)
                    for t in range(2):
                        tt = slice(t * TILE, t * TILE + TILE)
                        last = three(bank(Y + t, TILE, PROJ_W), hs_hi[q][:, tt], hs_lo[q][:, tt],
                                     proj_hi[:, :], proj_lo[:, :])
                    last.then_inc(s_proj, 1)
                if live(5):
                    b = s - 5
                    pe.wait_ge(s_masked, 2 * b + 2)
                    pe.wait_ge(s_v_ones, b + 1)
                    wait(pe, *((s_tr_act, 2 * (s - 3) + 2) if live(3) else (s_o_out, b)))
                    o = bank(M0, D, 2 * T).rearrange("p (g t) -> p g t", g=2)
                    for g in range(2):
                        for j in range(4):
                            mm(o[32 * j:32 * j + 32, g], v_ones[q][:, 0, 4 * g + j, :], p0[q][:, g, j, :],
                               start=g == 0, stop=False, skip_group_check=True)
                        for j in range(4):
                            last = mm(o[32 * j:32 * j + 32, g, TILE:], v_ones[q][:, 1, 4 * g + j, :],
                                      p1[q][:, g, j, :], start=False, stop=True, skip_group_check=True)
                    last.then_inc(s_pv, 1)
                if live(6):
                    b = s - 6
                    pe.wait_ge(s_nt_out, b + 1)
                    if live(3):
                        pe.wait_ge(s_tr_dve, 2 * (s - 3) + 2)
                    mm(bank(M1, D, T), wo_t[:, :], o_feat[p][:, :], start=True, stop=True).then_inc(s_wo, 1)
                if live(3):
                    pe.wait_ge(s_tr_act, 2 * (s - 3) + 2)
                    pe.wait_ge(s_tr_dve, 2 * (s - 3) + 2)
                    if live(4):
                        pe.wait_ge(s_mt_out, s - 3)
                    score(s - 3, 0, q)
                    if live(6):
                        pe.wait_ge(s_nt_out, s - 5)
                    score(s - 3, 1, q)
                for u in range(6):
                    if live(3) and u >= 2:
                        score(s - 3, u, q)
                    if live(4):
                        score_t(s - 4, u, p)
                    if u == 0 and live(5):
                        b = s - 5
                        pe.wait_ge(s_o_out, b + 1)
                        wait(pe, s_resid, b)
                        for t in range(2):
                            for g in range(2):
                                last = nc.tensor.transpose(bank(M1, TILE, D, (2 * t + g) * D),
                                                           o_sb[q][:, g, t * TILE:t * TILE + TILE], eye[:, :])
                        last.then_inc(s_ot, 1)

            pipeline(pe, B, 6, attention)

            def gate(s, k4, live):
                p, q = k4 % 2, 1 - k4 % 2
                if live(4):
                    c = s - 4
                    pe.wait_ge(s_xn, c + 1)
                    wait(pe, s_xl, c - 1)
                    for j in range(4):
                        last = nc.tensor.transpose(bank(XT + p, D, TILE, j * TILE), xn[p][:, j, :],
                                                   eye[0:TILE, 0:TILE])
                    last.then_inc(s_xt, 1)
                if live(5):
                    c = s - 5
                    pe.wait_ge(s_xl, c + 1)
                    wait(pe, s_gh, c)
                    three(bank(GATE, 64, CH), gw1_hi[:, :], gw1_lo[:, :], xh[:, bass.ds(c * CH, CH)],
                          xl[:, bass.ds(c * CH, CH)]).then_inc(s_gate, 1)
                if live(6):
                    c = s - 6
                    pe.wait_ge(s_gh, c + 1)
                    if not isinstance(s, int) or c < 2:
                        pe.wait_ge(s_pool_c, N_POOL_C)
                    for j in range(4):
                        last = mm(ps[0:TILE, LOGIT, bass.ds(4 * EXPERTS * c + EXPERTS * j, EXPERTS)],
                                  gh[p][:, j * TILE:j * TILE + TILE], gw2[:, :], start=True, stop=True)
                    last.then_inc(s_logit, 1)
                if live(0):
                    pe.wait_ge(s_hn, s + 1)
                    wait(pe, s_xn, s - 3)
                    for j in range(4):
                        last = mm(bank(CEN[k4], TILE, D, j * D), hn[p][:, j * TILE:j * TILE + TILE], centre[:, :],
                                  start=True, stop=True)
                    last.then_inc(s_cen, 1)

            pipeline(pe, N_CH, 6, gate, 4)

            def up(n, e, c):
                for half in range(2):
                    wait(pe, s_gelu, 2 * (n - 2) + half + 1)
                    cols = slice(half * D, half * D + D)
                    three(bank(UP + 2 * (e % 2) + half, D, CH), w1_hi[:, e, cols], w1_lo[:, e, cols],
                          xh[:, bass.ds(c * CH, CH)], xl[:, bass.ds(c * CH, CH)]).then_inc(s_up, 1)

            def down(n, e):
                wait(pe, s_part, n - 1)
                for half in range(2):
                    pe.wait_ge(s_split, 2 * n + half + 1)
                    last = three(bank(DOWN + e % 2, D, CH), w2_hi[:, e, half, :], w2_lo[:, e, half, :],
                                 act_hi[e % 2][:, half, :], act_lo[e % 2][:, half, :], half == 0, half == 1)
                last.then_inc(s_down, 1)

            def unit(c, k, live):
                up(EXPERTS * c + k, k % EXPERTS, c + k // EXPERTS)
                if live:
                    down(EXPERTS * c + k - 2, (k - 2) % EXPERTS)

            for k in range(2 * EXPERTS):
                unit(0, k, k >= 2)
                if k == 1:
                    pe.wait_ge(s_router, R_END)
                    flat = rt[2][:, :, :].rearrange("p t e -> p (t e)")
                    for j in range(4):
                        last = nc.tensor.transpose(bank(CT, 128, TILE, j * TILE), flat[:, 128 * j:128 * j + 128],
                                                   eye[0:TILE, 0:TILE])
                    last.then_inc(s_ct, 1)
            with pe.Fori(2, N_CH - 1, 2) as c:
                for k in range(2 * EXPERTS):
                    unit(c, k, True)
            for k in (EXPERTS - 2, EXPERTS - 1):
                down(EXPERTS * (N_CH - 1) + k, k)


def kernel(**inputs):
    import ml_dtypes
    import concourse.bacc as bacc
    from concourse.bass_utils import run_bass_kernel_spmd as run

    a = {n: np.asarray(v) for n, v in inputs.items()}
    t = {n[len("L0_attn_"):]: v for n, v in a.items() if n.startswith("L0_attn_")}
    f = {n[len("L0_ffn_"):]: v for n, v in a.items() if n.startswith("L0_ffn_")}
    pos = np.arange(T, dtype=np.float64).reshape(2, TILE).T[:, :, None]
    cos, sin = (np.broadcast_to(x, (TILE, 2, ROT)) for x in (np.cos(pos), np.sin(pos)))
    tri = np.where(np.arange(TILE)[None, :] <= np.arange(TILE)[:, None], 0.0, -3.0e38)
    arrays = {
        "x_t": a["x"].transpose(2, 0, 1).reshape(D_IN, B * T_IN),
        "conv_w": a["L0_tok_W"].T,
        "vecs": np.stack([a["L0_tok_b"], a["L0_tok_gamma"], a["L0_tok_beta"]], 1),
        "wdq": t["W_dq"], "wdkv": t["W_dkv"], "wuq": t["W_uq"], "wqr": t["W_qr"],
        "wukv": np.concatenate([t["W_ukv"][:, :D], t["W_ukv"][:, D:].reshape(KV_PROJ, 4, 2, DH)
                                .transpose(0, 2, 1, 3).reshape(KV_PROJ, D)], 1),
        "wkr": t["W_kr"],
        "wo_t": t["W_o"].T.reshape(4, 2, DH, D).transpose(1, 0, 2, 3).reshape(D, D),
        "q_gb": np.stack([t["q_ln_g"], t["q_ln_b"]], 1), "kv_gb": np.stack([t["kv_ln_g"], t["kv_ln_b"]], 1),
        "we1": f["we1"].transpose(1, 0, 2).reshape(D, EXPERTS * HID),
        "we2": f["we2"].reshape(EXPERTS, 2, D, D).transpose(2, 0, 1, 3).reshape(D, EXPERTS * HID),
        "be1": f["be1"].reshape(EXPERTS, 2, D).transpose(2, 0, 1), "be2": f["be2"].T,
        "gw1": f["gw1"], "gb1": f["gb1"][:, None], "gw2": np.concatenate([f["gw2"], f["gb2"][None]], 0),
        "eye": np.eye(128, dtype=np.float32),
        "centre": (np.eye(D) - 1.0 / D).astype(np.float32),
        "trig": np.concatenate([cos, sin, cos, sin], 2).astype(np.float32),
        "eye_bf": np.eye(TILE).astype(ml_dtypes.bfloat16),
        "mask": np.broadcast_to(tri[:, None, :], (TILE, 4, TILE)).astype(ml_dtypes.bfloat16),
        "rank": np.broadcast_to(np.arange(EXPERTS, 0, -1), (TILE, EXPERTS)).astype(np.float32),
    }
    nc = bacc.Bacc("TRN2", target_bir_lowering=False, num_devices=1)
    arrays = {f"in_{n}_dram": np.ascontiguousarray(v) for n, v in arrays.items()}
    aps = {n[3:-5]: nc.dram_tensor(n, v.shape, mybir.dt.from_np(v.dtype), kind="ExternalInput").ap()
           for n, v in arrays.items()}
    out = nc.dram_tensor("out_dram", (D, N_TOK), F32, kind="ExternalOutput").ap()
    build(nc, aps, out)
    r = run(nc, [arrays], core_ids=[0])
    return np.ascontiguousarray(np.asarray(r.results[0]["out_dram"]).T).reshape(B, T, D)
```

```python
from contextlib import ExitStack

import numpy as np
import concourse.bass as bass
from concourse import mybir

F32 = mybir.dt.float32
F32R = mybir.dt.float32r
BF16 = mybir.dt.bfloat16
ALU = mybir.AluOpType
ACT = mybir.ActivationFunctionType
AX = mybir.AxisListType

B, T_IN, D_IN = 32, 256, 23
CTX = 5
T = T_IN - (CTX - 1)
TILE = T // 2
K_IN = CTX * D_IN
D = 128
N_TOK = B * T
CH = 2 * T
N_CH = N_TOK // CH
N_TILES = N_TOK // TILE
HEADS, DH, R = 8, 16, 2
DQ = DH + R
Q_PROJ, KV_PROJ = D // 2, 2 * D // 3
ROT = HEADS * R
EXPERTS, HID = 8, 256
EPS = 1e-5
SCALE = float(1.0 / np.sqrt(np.float32(DQ)))
STACK = 3 * DQ
SLOT = 64
TW = SLOT + STACK + 2
PROJ_W = 3 * D + 4 * ROT
STAT_W = D + Q_PROJ + KV_PROJ + 1


FOLD_AT = (7, 11, 13)
N_PREP = 14
N_POOL_C = 13
R_EXP, R_DIFF, R_END = 2, 17, 22
FIRST_CHUNKS = 4
N_CHAIN = 7
LAG_W = 3


def batches(n, top):
    return min(max(n, 0), top) if isinstance(n, int) else n


def before(b, parity):
    return (b - parity) // 2


def wait(eng, sem, value):
    if not isinstance(value, int) or value > 0:
        eng.wait_ge(sem, value)


def pipeline(eng, n, lag, step, unroll=2):
    head = lag + 1 + (n - lag - 1) % unroll
    for s in range(head):
        step(s, s % unroll, lambda k, s=s: 0 <= s - k < n)
    with eng.Fori(head, n - unroll + 1, unroll) as i:
        for p in range(unroll):
            step(i + p, p, lambda k: True)
    for s in range(n, n + lag):
        step(s, s % unroll, lambda k, s=s: 0 <= s - k < n)


def build(nc, A, out):
    ctx = ExitStack()
    with ctx:
        def sb(name, shape, dt=F32, where=ctx):
            return where.enter_context(nc.sbuf_tensor(name, shape, dt))

        def sem(name):
            return ctx.enter_context(nc.semaphore(name))

        h = sb("h", [D, N_TOK])
        eye = sb("eye", [128, 128])
        centre = sb("centre", [D, D])
        w1_hi = sb("w1_hi", [D, EXPERTS, HID], F32R)
        w1_lo = sb("w1_lo", [D, EXPERTS, HID], F32R)
        w2_hi = sb("w2_hi", [D, EXPERTS, 2, D], F32R)
        w2_lo = sb("w2_lo", [D, EXPERTS, 2, D], F32R)
        be1 = sb("be1_sb", [D, EXPERTS, 2])
        be2 = sb("be2_sb", [D, EXPERTS])
        gw1 = sb("gw1_sb", [D, 64])
        gw1_hi = sb("gw1_hi", [D, 64], F32R)
        gw1_lo = sb("gw1_lo", [D, 64], F32R)
        gb1 = sb("gb1_sb", [64, 1])
        gw2 = sb("gw2_sb", [65, EXPERTS])
        rank = sb("rank_sb", [TILE, EXPERTS])
        scratch = nc.dram_tensor("combine_scratch", [4, 16, EXPERTS, TILE], F32).ap()

        early = ExitStack()
        with early:
            def eb(name, shape, dt=F32):
                return sb(name, shape, dt, early)
            vecs = eb("vecs", [D, 16])
            bn = eb("bn", [D, N_CH, 6])
            bn_mv = eb("bn_mv", [D, 2])
            wdq = eb("wdq", [D, Q_PROJ])
            wdkv = eb("wdkv", [D, KV_PROJ + 1])
            wq_raw = eb("wq_raw", [Q_PROJ, D + 2 * ROT])
            wk_raw = eb("wk_raw", [KV_PROJ, 2 * D])
            wkr = eb("wkr", [D, 2 * ROT])
            wo_t = eb("wo_t", [D, D])
            q_gb = eb("q_gb", [Q_PROJ, 2])
            kv_gb = eb("kv_gb", [KV_PROJ, 2])
            cell = eb("cell", [TILE, 2])
            held = eb("held", [1, 2])
            eye_r = eb("eye_r", [TILE, TILE], F32R)
            v_bias = eb("v_bias", [D, 1])
            o_bias = eb("o_bias", [D, 1])
            stat_hi = eb("stat_hi", [D, STAT_W], F32R)
            stat_lo = eb("stat_lo", [D, STAT_W], F32R)
            proj_hi = eb("proj_hi", [D, PROJ_W], F32R)
            proj_lo = eb("proj_lo", [D, PROJ_W], F32R)
            bias_row = eb("bias_row", [TILE, 2 * D + 2 * ROT])
            trig = eb("trig_sb", [TILE, 2, 4 * ROT])
            eye_bf = eb("eye_bf", [TILE, TILE], BF16)
            mask = eb("mask_sb", [TILE, 4, TILE], BF16)
            hs_hi = [eb(f"hs_hi{i}", [D, CH], F32R) for i in range(2)]
            hs_lo = [eb(f"hs_lo{i}", [D, CH], F32R) for i in range(2)]
            squares = [eb(f"squares{i}", [TILE, 4, STAT_W]) for i in range(2)]
            sums = eb("sums", [TILE, 3, N_TILES])
            varis = eb("varis", [TILE, 3, N_TILES])
            rstd = eb("rstd", [TILE, 3, N_TILES])
            rwork = eb("rwork", [TILE, 3, N_TILES])
            v_all = eb("v_all", [128, B, 2, D])
            slots = [eb(f"slots{i}", [TILE, 2, 2, HEADS, SLOT], F32R) for i in range(2)]
            v_ones = [eb(f"v_ones{i}", [TILE, 2, HEADS, 32]) for i in range(2)]
            with ExitStack() as conv_mem:
                def cb(name, shape, dt=F32):
                    return sb(name, shape, dt, conv_mem)
                frames = cb("frames", [K_IN, B * T_IN])
                conv_w = cb("conv_w", [K_IN, D])
                ones = cb("ones", [128, TILE])
                bq_wide = cb("bq_wide", [Q_PROJ, TILE])
                bkv_wide = cb("bkv_wide", [KV_PROJ, TILE])
                yq_t = cb("yq_t", [Q_PROJ, D])
                yk_t = cb("yk_t", [KV_PROJ, D])
                wq_g = cb("wq_g", [Q_PROJ, D + 2 * ROT])
                wk_g = cb("wk_g", [KV_PROJ, 2 * D])
            with ExitStack() as att_mem:
                def ab(name, shape, dt=F32):
                    return sb(name, shape, dt, att_mem)
                x_tok = [ab(f"x_tok{i}", [TILE, 2, 2, HEADS, DQ]) for i in range(2)]
                rope = [ab(f"rope{i}", [TILE, 2, 2, 2, ROT]) for i in range(2)]
                stack = [ab(f"stack{i}", [128, 2, 4, T], F32R) for i in range(2)]
                neg_max = [ab(f"neg_max{i}", [TILE, 2, 2, 4]) for i in range(2)]
                neg_max_t = [ab(f"neg_max_t{i}", [HEADS, T], F32R) for i in range(2)]
                p0 = [ab(f"p0_{i}", [TILE, 2, 4, T]) for i in range(2)]
                p1 = [ab(f"p1_{i}", [TILE, 2, 4, TILE]) for i in range(2)]
                o_sb = [ab(f"o_sb{i}", [D, 2, T]) for i in range(2)]
                o_rec = [ab(f"o_rec{i}", [TILE, 16, 1]) for i in range(2)]
                o_tok = [ab(f"o_tok{i}", [TILE, 2, D]) for i in range(2)]
                o_feat = [ab(f"o_feat{i}", [D, T]) for i in range(2)]

        xh = sb("xh", [D, N_TOK], F32R)
        xl = sb("xl", [D, N_TOK], F32R)
        rt = [sb(f"rt{i}", [TILE, N_TILES, EXPERTS]) for i in range(6)]
        rs = sb("rs", [TILE, 6, N_TILES])
        comb_t = sb("comb_t", [128, 4, TILE])
        act_f = [sb(f"act_f{i}", [D, 2, CH]) for i in range(2)]
        act_hi = [sb(f"act_hi{i}", [D, 2, CH], F32R) for i in range(2)]
        act_lo = [sb(f"act_lo{i}", [D, 2, CH], F32R) for i in range(2)]
        part = [sb(f"part{i}", [D, CH]) for i in range(2)]
        total = [sb(f"total{i}", [D, CH]) for i in range(2)]
        with ExitStack() as gate_mem:
            def gb(name, shape, dt=F32):
                return sb(name, shape, dt, gate_mem)
            hn = [gb(f"hn{i}", [D, CH]) for i in range(2)]
            sq2 = [gb(f"sq2_{i}", [TILE, 4, D]) for i in range(2)]
            st2 = [gb(f"st2_{i}", [TILE, 8, 4]) for i in range(2)]
            consts4 = gb("consts4", [TILE, 3, 4])
            xn = [gb(f"xn{i}", [TILE, 4, D]) for i in range(2)]
            gh = [gb(f"gh{i}", [65, CH]) for i in range(2)]
        comb = [sb(f"comb{i}", [D, 4, EXPERTS, TILE]) for i in range(2)]

        ps = ctx.enter_context(nc.psum_tensor("ps", [128, 8, 512], F32))

        def bank(k, rows, cols, at=0):
            return ps[0:rows, k, at:at + cols]

        (s_conv_in, s_frames0, s_frames1, s_frames2, s_frames3, s_consts, s_weights, s_ffn_in, s_raw,
         s_pool_c, s_prep, s_fold, s_fold_hi, s_fold_lo,
         s_conv, s_relu, s_bn, s_bn_sqrt, s_normed, s_hs_hi, s_hs_lo, s_stat, s_square, s_sums, s_root,
         s_hi, s_lo, s_proj, s_scaled, s_pool, s_rope, s_slot_hi, s_slot_lo, s_tr, s_tr_act,
         s_tr_dve, s_score, s_max, s_mt, s_mt_out, s_m_dma0, s_m_dma1, s_st, s_exp, s_masked, s_v_ones, s_v,
         s_pv, s_o_out, s_ot, s_rec, s_o_norm, s_nt, s_nt_out, s_wo, s_resid, s_hn, s_cen, s_sq2, s_chain2,
         s_var2, s_xn, s_xt, s_xh, s_xl, s_gate, s_gh, s_logit, s_router, s_rexp, s_ct, s_ct_out,
         s_scratch, s_comb_in0, s_comb_in1, s_up, s_gelu, s_act_hi, s_split, s_down, s_part, s_total,
         s_out0, s_out1, s_wsplit, s_cell) = (sem(n) for n in (
            "s_conv_in s_frames0 s_frames1 s_frames2 s_frames3 s_consts s_weights s_ffn_in s_raw "
            "s_pool_c s_prep s_fold s_fold_hi s_fold_lo "
            "s_conv s_relu s_bn s_bn_sqrt s_normed s_hs_hi s_hs_lo s_stat s_square s_sums s_root "
            "s_hi s_lo s_proj s_scaled s_pool s_rope s_slot_hi s_slot_lo s_tr s_tr_act s_tr_dve "
            "s_score s_max s_mt s_mt_out s_m_dma0 s_m_dma1 s_st s_exp s_masked s_v_ones s_v s_pv s_o_out "
            "s_ot s_rec s_o_norm s_nt s_nt_out s_wo s_resid s_hn s_cen s_sq2 s_chain2 s_var2 "
            "s_xn s_xt s_xh s_xl s_gate s_gh s_logit s_router s_rexp s_ct s_ct_out s_scratch "
            "s_comb_in0 s_comb_in1 s_up s_gelu s_act_hi s_split s_down s_part s_total s_out0 s_out1 "
            "s_wsplit s_cell").split())
        s_frames = (s_frames0, s_frames1, s_frames2, s_frames3)
        s_m_dma, s_comb_in, s_out = (s_m_dma0, s_m_dma1), (s_comb_in0, s_comb_in1), (s_out0, s_out1)

        Y, S, P, M0, M1 = 0, 2, 4, 6, 7
        TR = (M0, Y)
        CEN, XT, GATE, LOGIT, CT, UP, DOWN = (0, 1, 5, 7), 2, 4, 6, 7, 0, 4

        WEIGHTS = [(wdq[:, :], A["wdq"]), (wdkv[:, 0:KV_PROJ], A["wdkv"]), (wq_raw[:, 0:D], A["wuq"]),
                   (wq_raw[:, D:D + ROT], A["wqr"]), (wk_raw[:, :], A["wukv"]), (wkr[:, 0:ROT], A["wkr"]),
                   (wo_t[:, :], A["wo_t"]), (q_gb[:, :], A["q_gb"]), (kv_gb[:, :], A["kv_gb"]),
                   (eye[:, :], A["eye"]), (centre[:, :], A["centre"])]
        CONSTS = [(trig[:, :, :], A["trig"]),
                  (eye_bf[:, :], A["eye_bf"]), (mask[:, :, :], A["mask"]), (rank[:, :], A["rank"])]
        FFN_IN = [(be1[:, :, :], A["be1"]), (be2[:, :], A["be2"]), (gw1[:, :], A["gw1"]),
                  (gb1[:, :], A["gb1"]), (gw2[:, :], A["gw2"])]
        v_flat = v_all[:, :, :, :].rearrange("p b t d -> p (b t d)")
        w1_raw, w2_raw = v_flat[:, 0:EXPERTS * HID], v_flat[:, EXPERTS * HID:2 * EXPERTS * HID]
        W1_HI, W1_LO = (w[:, :, :].rearrange("p e n -> p (e n)") for w in (w1_hi, w1_lo))
        W2_HI, W2_LO = (w[:, :, :, :].rearrange("p e a n -> p (e a n)") for w in (w2_hi, w2_lo))

        block = ctx.enter_context(nc.Block())

        @block.sync
        def _(sp):
            sp.dma_start(conv_w[:, :], A["conv_w"]).then_inc(s_conv_in, 16)
            sp.dma_start(vecs[:, 0:3], A["vecs"]).then_inc(s_conv_in, 16)
            n = B * T_IN // len(s_frames)
            for k, s_part in enumerate(s_frames):
                for i in range(CTX):
                    end = min((k + 1) * n, B * T_IN - (CTX - 1))
                    sp.dma_start(frames[i * D_IN:(i + 1) * D_IN, k * n:end], A["x_t"][:, k * n + i:end + i])\
                      .then_inc(s_part, 16)
                if k == 0:
                    for dst, src in WEIGHTS:
                        sp.dma_start(dst, src).then_inc(s_weights, 16)
            for dst, src in CONSTS:
                sp.dma_start(dst, src).then_inc(s_consts, 16)
            sp.dma_start(w1_raw, A["we1"]).then_inc(s_raw, 16)
            sp.dma_start(w2_raw, A["we2"]).then_inc(s_raw, 16)
            for dst, src in FFN_IN:
                sp.dma_start(dst, src).then_inc(s_ffn_in, 16)

            def move_max(s, p, live):
                if live(4):
                    b = s - 4
                    wait(sp, s_mt_out, b + 1)
                    for half in range(2):
                        row = SLOT * half + STACK
                        sp.dma_start(stack[p][row:row + 1, 0, :, :].bitcast(F32),
                                     neg_max_t[p][4 * half:4 * half + 4, :].bitcast(F32)).then_inc(s_m_dma[p], 16)

            pipeline(sp, B, 6, move_max)

            def store_weights(part, blocks):
                sp.wait_ge(s_ct_out, part + 1)
                sp.dma_start(scratch[blocks].rearrange("k t e i -> (t e) k i"), comb_t[:, blocks, :])\
                  .then_inc(s_scratch, 16)
                sp.wait_ge(s_scratch, 16 * (part + 1))

            n_comb = 4 * EXPERTS * TILE
            flat = scratch.rearrange("k t e i -> (k t e i)").rearrange("(a n) -> a n", a=1)

            def load_comb(c, p):
                sp.dma_start(comb[p][:, :, :, :].rearrange("p j e i -> p (j e i)"),
                             flat[:, bass.ds(c * n_comb, n_comb)].to_broadcast([D, n_comb]))\
                  .then_inc(s_comb_in[p], 16)

            def store(c, p):
                sp.wait_ge(s_total, EXPERTS * c + EXPERTS)
                sp.dma_start(out[:, bass.ds(c * CH, CH)], total[p][:, :]).then_inc(s_out[p], 16)

            store_weights(0, slice(0, 1))
            for c in range(2):
                load_comb(c, c)
            store(0, 0)
            load_comb(2, 0)
            store_weights(1, slice(1, 4))
            store(1, 1)
            load_comb(3, 1)
            with sp.Fori(2, N_CH - 3, 2) as i:
                for p in range(2):
                    store(i + p, p)
                    load_comb(i + p + 2, p)
            for c in range(N_CH - 2, N_CH):
                store(c, c % 2)
            for p in range(2):
                sp.wait_ge(s_out[p], 16 * (N_CH // 2))

        @block.gpsimd
        def _(pool):
            pool.memset(held[:, :], 0.0)
            pool.memset(cell[:, 0:1], 0.0).then_inc(s_cell, 1)
            pool.memset(cell[:, 1:2], 1.0).then_inc(s_cell, 1)
            pool.wait_ge(s_cell, 2)
            pool.memset(ones[:, :], 1.0).then_inc(s_pool_c, 1)
            pool.memset(wdkv[:, KV_PROJ:KV_PROJ + 1], 0.0).then_inc(s_pool_c, 1)
            for p in range(2):
                for side in range(2):
                    fill = cell[:, side:side + 1].rearrange("p (a b c) -> p a b c", a=1, b=1)
                    pool.tensor_copy(slots[p][:, :, side, :, STACK:],
                                     fill.to_broadcast([TILE, 2, HEADS, SLOT - STACK])).then_inc(s_pool_c, 1)
                pool.memset(v_ones[p][:, :, :, DH:], 1.0).then_inc(s_pool_c, 1)
            pool.wait_ge(s_raw, 32)
            pool.wait_ge(s_ffn_in, 16 * len(FFN_IN))
            for k, (hi, lo, raw) in enumerate(((W1_HI, W1_LO, w1_raw), (W2_HI, W2_LO, w2_raw),
                                               (gw1_hi[:, :], gw1_lo[:, :], gw1[:, :]))):
                pool.tensor_copy(hi, raw).then_inc(s_wsplit, 1)
                pool.wait_ge(s_wsplit, 2 * k + 1)
                pool.tensor_tensor(lo, raw, hi.bitcast(F32), ALU.subtract).then_inc(s_wsplit, 1)
                pool.wait_ge(s_wsplit, 2 * k + 2)
            pool.wait_ge(s_fold_lo, 4)
            pool.wait_ge(s_consts, 16 * len(CONSTS))

            def step(s, p, live):
                q = 1 - p
                if live(1):
                    b = s - 1
                    pool.wait_ge(s_scaled, 2 * b + 2)
                    ra = rope[q][:, :, :, :, :].rearrange("p t s a r -> p (t s a r)")
                    pool.tensor_tensor(ra, ra, trig[:, :, :].rearrange("p t r -> p (t r)"), ALU.mult)\
                        .then_inc(s_pool, 1)
                    pool.wait_ge(s_pool, b + 1)
                    rr = rope[q][:, :, :, :, :].rearrange("p t s a (h r) -> p (t s) a h r", r=R)
                    pool.tensor_tensor(x_tok[q][:, :, :, :, DH:].rearrange("p t s h r -> p (t s) h r"),
                                       rr[:, :, 0], rr[:, :, 1], ALU.add).then_inc(s_rope, 1)
                if live(4):
                    b = s - 4
                    for i, (units, t) in enumerate(((2, p1[p][:, :, :, :]), (6, p0[p][:, :, :, 0:TILE]))):
                        wait(pool, s_masked, 2 * b + i)
                        pool.wait_ge(s_exp, 6 * b + units)
                        pool.tensor_tensor(held[:, 0:1], held[:, 1:2], held[:, 1:2], ALU.mult)
                        v = t.rearrange("p a b q -> p (a b) q")
                        pool.affine_select(out=v, in_=v, compare_op=ALU.is_ge, fill=0.0, base=0,
                                           pattern=[[0, HEADS], [1, TILE]], channel_multiplier=-1)\
                            .then_inc(s_masked, 1)

            pipeline(pool, B, 6, step)

            pool.wait_ge(s_resid, B)
            for p in range(2):
                pool.memset(gh[p][64:65, :], 1.0).then_inc(s_pool_c, 1)
            pool.wait_ge(s_pool_c, N_POOL_C - 3)
            for k, value in enumerate((EPS, -0.5, 1.5)):
                pool.memset(consts4[:, k, :], value).then_inc(s_pool_c, 1)
            pool.wait_ge(s_pool_c, N_POOL_C)
            eps4, half4, more4 = (consts4[:, k, :] for k in range(3))

            def norm(s, k4, live):
                p = k4 % 2
                if live(2):
                    c = s - 2
                    mean, v, r, w, r2 = (st2[p][:, k, :] for k in range(5))
                    pool.wait_ge(s_var2, c + 1)
                    wait(pool, s_xn, c - 1)
                    pool.tensor_tensor(v, mean, eps4, ALU.add).then_inc(s_chain2, 1)
                    for k, (o, a, b, op) in enumerate(((r, v, half4, ALU.pow), (w, r, r, ALU.mult), (w, w, v, ALU.mult),
                                                       (w, w, half4, ALU.mult), (w, w, more4, ALU.add),
                                                       (r2, r, w, ALU.mult))):
                        pool.wait_ge(s_chain2, N_CHAIN * c + k + 1)
                        pool.tensor_tensor(o, a, b, op).then_inc(s_chain2, 1)

            pipeline(pool, N_CH, 6, norm, 4)

            def add(c, p):
                for e in range(EXPERTS):
                    pool.wait_ge(s_part, EXPERTS * c + e + 1)
                    if e == 0:
                        wait(pool, s_out[p], 16 * before(c, p))
                    else:
                        pool.wait_ge(s_total, EXPERTS * c + e)
                    acc = h[:, bass.ds(c * CH, CH)] if e == 0 else total[p][:, :]
                    pool.tensor_tensor(total[p][:, :], acc, part[e % 2][:, :], ALU.add).then_inc(s_total, 1)

            for c in range(2):
                add(c, c)
            with pool.Fori(2, N_CH - 1, 2) as i:
                for p in range(2):
                    add(i + p, p)

        @block.scalar
        def _(act):
            act.wait_ge(s_conv_in, 16 * 2)
            for c in range(N_CH):
                act.wait_ge(s_conv, c + 1)
                act.activation(h[:, c * CH:c * CH + CH], bank(c % 4, D, CH), ACT.Relu, bias=vecs[:, 0:1])\
                    .then_inc(s_relu, 1)
            act.wait_ge(s_fold, 2)
            act.activation(stat_hi[:, :], bank(4, D, STAT_W), ACT.Identity).then_inc(s_fold_hi, 1)
            act.activation(proj_hi[:, :], bank(5, D, PROJ_W), ACT.Identity).then_inc(s_fold_hi, 1)
            act.wait_ge(s_bn, N_CH + 2)
            act.activation(vecs[:, 4:5], vecs[:, 3:4], ACT.Sqrt).then_inc(s_bn_sqrt, 1)

            act.wait_ge(s_bn, N_CH + 3)

            def stats(s, p, live):
                q = 1 - p
                if live(1):
                    c = s - 1
                    act.wait_ge(s_normed, c + 1)
                    wait(act, s_stat, c - 1)
                    act.activation(hs_hi[q][:, :], h[:, bass.ds(c * CH, CH)], ACT.Identity).then_inc(s_hs_hi, 1)
                if live(0):
                    hc = h[:, bass.ds(2 * s * T, CH)]
                    act.activation(hc, hc, ACT.Identity, scale=vecs[:, 8:9], bias=vecs[:, 10:11]).then_inc(s_normed, 1)
                if live(3):
                    c = s - 3
                    act.wait_ge(s_stat, c + 1)
                    wait(act, s_sums, c - 1)
                    act.activation(squares[q][:, :, :], ps[0:TILE, 4 * q:4 * q + 4, 0:STAT_W], ACT.Square)\
                        .then_inc(s_square, 1)

            pipeline(act, N_CH, 4, stats)
            def split_high(s, p):
                wait(act, s_proj, s - 1)
                act.activation(hs_hi[p][:, 0:T], h[:, bass.ds(s * T, T)], ACT.Identity).then_inc(s_hi, 1)

            act.wait_ge(s_stat, N_CH)
            for b in range(2):
                split_high(b, b)
            act.wait_ge(s_root, 1)
            act.activation(rstd[:, :, :], varis[:, :, :], ACT.Sqrt).then_inc(s_root, 1)

            def exp(b, u, p):
                half, k = u % 2, u // 2
                act.wait_ge(s_st, 6 * b + u + 1)
                if u == 0:
                    wait(act, s_pv, b - 1)
                if k == 0:
                    dst, src = p1[p][:, half, :, :], bank(P + half, TILE, 4 * TILE)
                else:
                    dst, src = p0[p][:, half, 2 * k - 2:2 * k, :], bank(P + half, TILE, 2 * T)
                src = src.rearrange("p (a b) -> p a b", a=4 if k == 0 else 2)
                act.activation(dst, src, ACT.Exp, scale=SCALE).then_inc(s_exp, 1)

            def move_stack(b, side, q):
                act.wait_ge(s_tr, 4 * b + 2 * (1 - side) + 1)
                if side == 1:
                    wait(act, s_st, 6 * (b - 1))
                act.activation(stack[q][0:TW, side, :, 0:TILE],
                               bank(TR[side], TW, 4 * TILE).rearrange("p (a b) -> p a b", a=4),
                               ACT.Identity).then_inc(s_tr_act, 1)

            def attention(s, p, live):
                q = 1 - p
                if live(3):
                    move_stack(s - 3, 1, q)
                    move_stack(s - 3, 0, q)
                if live(4):
                    b = s - 4
                    act.wait_ge(s_mt, b + 1)
                    wait(act, s_m_dma[p], 16 * 2 * before(b, p))
                    act.activation(neg_max_t[p][:, :], bank(S, HEADS, T), ACT.Identity).then_inc(s_mt_out, 1)
                if live(6):
                    b = s - 6
                    act.wait_ge(s_nt, b + 1)
                    wait(act, s_wo, b - 1)
                    act.activation(o_feat[p][:, :], bank(S + 1, D, T), ACT.Identity).then_inc(s_nt_out, 1)
                if live(2):
                    b = s - 2
                    act.wait_ge(s_rope, b + 1)
                    act.wait_ge(s_v, b + 1)
                    wait(act, s_tr, 4 * (b - 1))
                    sl = slots[p]
                    act.activation(sl[:, :, :, :, 0:DQ].rearrange("p t s h d -> p (t s h) d"),
                                   x_tok[p][:, :, :, :, :].rearrange("p t s h d -> p (t s h) d"),
                                   ACT.Identity).then_inc(s_slot_hi, 1)
                    for side in range(2):
                        at = DQ * (1 + side)
                        act.activation(sl[:, :, side, :, at:at + DQ], x_tok[p][:, :, side, :, :],
                                       ACT.Identity).then_inc(s_slot_hi, 1)
                if live(0) and not (isinstance(s, int) and s < 2):
                    split_high(s, p)
                if live(5):
                    b = s - 5
                    act.wait_ge(s_pv, b + 1)
                    wait(act, s_ot, b - 1)
                    act.activation(o_sb[q][:, :, :], bank(M0, D, 2 * T).rearrange("p (a b) -> p a b", a=2),
                                   ACT.Identity).then_inc(s_o_out, 1)
                if live(4):
                    for u in range(6):
                        exp(s - 4, u, p)

            pipeline(act, B, 6, attention)

            def gate(s, k4, live):
                p, q = k4 % 2, 1 - k4 % 2
                if live(1):
                    act.wait_ge(s_cen, s)
                    wait(act, s_var2, s - 2)
                    act.activation(sq2[q][:, :, :], bank(CEN[(k4 - 1) % 4], TILE, 4 * D).rearrange("p (a b) -> p a b", a=4),
                                   ACT.Square, scale=float(D ** -0.5)).then_inc(s_sq2, 1)
                if live(4):
                    c = s - 4
                    act.wait_ge(s_xt, c + 1)
                    act.activation(xh[:, bass.ds(c * CH, CH)], bank(XT + p, D, CH), ACT.Identity)\
                        .then_inc(s_xh, 1)
                if live(5):
                    c = s - 5
                    act.wait_ge(s_gate, c + 1)
                    wait(act, s_logit, c - 1)
                    act.activation(gh[q][0:64, :], bank(GATE, 64, CH), ACT.Relu, bias=gb1[:, :])\
                        .then_inc(s_gh, 1)

            tiles = (slice(0, 4 * FIRST_CHUNKS), slice(4 * FIRST_CHUNKS, N_TILES))

            def router_exp(part):
                act.wait_ge(s_router, R_END * part + R_EXP)
                act.activation(rt[0][:, tiles[part], :], rt[1][:, tiles[part], :], ACT.Exp).then_inc(s_rexp, 1)

            def router_tanh(part):
                act.wait_ge(s_router, R_END * part + R_DIFF)
                act.activation(rs[:, 4, tiles[part]], rs[:, 3, tiles[part]], ACT.Tanh, scale=0.5).then_inc(s_rexp, 1)

            def gate_and_router(s, k4, live):
                gate(s, k4, live)
                if isinstance(s, int) and s == N_CH + 1:
                    router_exp(0)

            pipeline(act, N_CH, 6, gate_and_router, 4)
            router_tanh(0)
            router_exp(1)

            def gelu(n, e):
                wait(act, s_split, n - 1)
                for half in range(2):
                    act.wait_ge(s_up, 2 * n + half + 1)
                    act.activation(act_f[e % 2][:, half, :], bank(UP + 2 * (e % 2) + half, D, CH), ACT.Gelu,
                                   bias=be1[:, e, half:half + 1]).then_inc(s_gelu, 1)
                act.wait_ge(s_gelu, 2 * n + 2)
                wait(act, s_down, n - 1)
                act.activation(act_hi[e % 2][:, :, :], act_f[e % 2][:, :, :], ACT.Identity).then_inc(s_act_hi, 1)

            for k in range(2 * EXPERTS):
                if k == 10:
                    router_tanh(1)
                gelu(k, k % EXPERTS)
            with act.Fori(2, N_CH, 1) as c:
                for e in range(EXPERTS):
                    gelu(EXPERTS * c + e, e)

        @block.vector
        def _(dve):
            V = nc.vector
            count = {}

            def link(ins, s=s_prep):
                count[s] = count.get(s, 0) + 1
                ins.then_inc(s, 1)
                dve.wait_ge(s, count[s])

            def rsqrt_from_root(v, root, r, w, s):
                link(V.reciprocal(r, root), s)
                link(V.tensor_tensor(w, r, r, ALU.mult), s)
                link(V.scalar_tensor_tensor(w, w, -0.5, v, op0=ALU.mult, op1=ALU.mult), s)
                link(V.scalar_tensor_tensor(r, w, 1.5, r, op0=ALU.add, op1=ALU.mult), s)

            dve.wait_ge(s_weights, 16 * len(WEIGHTS))
            dve.wait_ge(s_pool_c, 2)
            dve.wait_ge(s_conv_in, 16 * 2)
            for w, n, c in ((wdq, Q_PROJ, 11), (wdkv, KV_PROJ, 13)):
                link(V.tensor_reduce(vecs[:, c:c + 1], w[:, 0:n], AX.X, ALU.add))
                link(V.tensor_scalar(vecs[:, c + 1:c + 2], vecs[:, c:c + 1], -1.0 / n, None, ALU.mult))
                link(V.tensor_scalar(w[:, 0:n], w[:, 0:n], vecs[:, c + 1:c + 2], None, ALU.add))
            for w, at in ((wq_raw, D), (wkr, 0)):
                a = w[:, at:at + ROT].rearrange("p (h r) -> p r h", r=R)
                r = w[:, at + ROT:at + 2 * ROT].rearrange("p (h r) -> p r h", r=R)
                link(V.tensor_scalar(r[:, 0], a[:, 1], -1.0, None, ALU.mult))
                link(V.tensor_copy(r[:, 1], a[:, 0]))
            link(V.tensor_scalar(wq_g[:, :], wq_raw[:, :], q_gb[:, 0:1], None, ALU.mult))
            link(V.tensor_scalar(wk_g[:, :], wk_raw[:, :], kv_gb[:, 0:1], None, ALU.mult))
            link(V.tensor_scalar(bq_wide[:, :], ones[0:Q_PROJ, :], q_gb[:, 1:2], None, ALU.mult))
            link(V.tensor_scalar(bkv_wide[:, :], ones[0:KV_PROJ, :], kv_gb[:, 1:2], None, ALU.mult))
            assert count[s_prep] == N_PREP
            for c in range(N_CH):
                dve.wait_ge(s_relu, c + 1)
                V.bn_stats(bn[:, c, :], h[:, c * CH:c * CH + CH]).then_inc(s_bn, 1)
                if c == FOLD_AT[0]:
                    dve.wait_ge(s_fold, 1)
                    link(V.tensor_copy(yq_t[:, :], bank(6, Q_PROJ, D)))
                    link(V.tensor_copy(yk_t[:, :], bank(6, KV_PROJ, D, D)))
                if c == FOLD_AT[1]:
                    dve.wait_ge(s_fold, 2)
                    V.tensor_copy(v_bias[:, :], bank(7, D, 1, 300)).then_inc(s_fold_lo, 1)
                    V.tensor_copy(bias_row[:, :], bank(7, TILE, 2 * D + 2 * ROT)).then_inc(s_fold_lo, 1)
                if c == FOLD_AT[2]:
                    dve.wait_ge(s_fold, 3)
                    V.tensor_copy(o_bias[:, :], bank(6, D, 1, 300)).then_inc(s_fold_lo, 1)
            V.tensor_copy(eye_r[:, :], eye[0:TILE, 0:TILE]).then_inc(s_fold_lo, 1)

            dve.wait_ge(s_fold_hi, 2)
            V.tensor_tensor(stat_lo[:, :], bank(4, D, STAT_W), stat_hi[:, :].bitcast(F32), ALU.subtract)\
                .then_inc(s_fold_lo, 1)
            V.tensor_tensor(proj_lo[:, :], bank(5, D, PROJ_W), proj_hi[:, :].bitcast(F32), ALU.subtract)\
                .then_inc(s_fold_lo, 1)
            dve.wait_ge(s_bn, N_CH)
            V.bn_aggr(bn_mv[:, :], bn[:, :, :].rearrange("p a b -> p (a b)")).then_inc(s_bn, 1)
            dve.wait_ge(s_bn, N_CH + 1)
            V.tensor_scalar(vecs[:, 3:4], bn_mv[:, 1:2], EPS, None, ALU.add).then_inc(s_bn, 1)
            dve.wait_ge(s_bn_sqrt, 1)
            rsqrt_from_root(vecs[:, 3:4], vecs[:, 4:5], vecs[:, 5:6], vecs[:, 6:7], s_prep)
            link(V.tensor_tensor(vecs[:, 8:9], vecs[:, 1:2], vecs[:, 5:6], ALU.mult))
            link(V.tensor_tensor(vecs[:, 9:10], bn_mv[:, 0:1], vecs[:, 8:9], ALU.mult))
            V.tensor_tensor(vecs[:, 10:11], vecs[:, 2:3], vecs[:, 9:10], ALU.subtract).then_inc(s_bn, 1)

            def stats(s, p, live):
                q = 1 - p
                if live(4):
                    c = s - 4
                    dve.wait_ge(s_square, c + 1)
                    for k, (at, n) in enumerate(((0, D), (D, Q_PROJ), (D + Q_PROJ, KV_PROJ))):
                        last = V.tensor_reduce(sums[:, k, bass.ds(4 * c, 4)], squares[p][:, :, at:at + n],
                                               AX.X, ALU.add)
                    last.then_inc(s_sums, 1)
                if live(1):
                    c = s - 1
                    dve.wait_ge(s_hs_hi, c + 1)
                    wait(dve, s_stat, c - 1)
                    V.tensor_tensor(hs_lo[q][:, :], h[:, bass.ds(c * CH, CH)], hs_hi[q][:, :].bitcast(F32),
                                    ALU.subtract).then_inc(s_hs_lo, 1)

            pipeline(dve, N_CH, 4, stats)
            def split_low(s, p):
                dve.wait_ge(s_hi, s + 1)
                wait(dve, s_proj, s - 1)
                V.tensor_tensor(hs_lo[p][:, 0:T], h[:, bass.ds(s * T, T)], hs_hi[p][:, 0:T].bitcast(F32),
                                ALU.subtract).then_inc(s_lo, 1)

            for b in range(2):
                split_low(b, b)
            dve.wait_ge(s_sums, N_CH)
            link(V.tensor_scalar(varis[:, 0, :], sums[:, 0, :], 1.0 / D, EPS, ALU.mult, ALU.add))
            link(V.tensor_scalar(rwork[:, 0, :], varis[:, 0, :], EPS, None, ALU.mult))
            link(V.scalar_tensor_tensor(varis[:, 1, :], sums[:, 1, :], 1.0 / Q_PROJ, rwork[:, 0, :],
                                        op0=ALU.mult, op1=ALU.add))
            V.scalar_tensor_tensor(varis[:, 2, :], sums[:, 2, :], 1.0 / KV_PROJ, rwork[:, 0, :],
                                   op0=ALU.mult, op1=ALU.add).then_inc(s_root, 1)
            dve.wait_ge(s_root, 2)
            rsqrt_from_root(varis[:, :, :], rstd[:, :, :], sums[:, :, :], rwork[:, :, :], s_prep)
            r_all = sums
            dve.wait_ge(s_wsplit, 6)

            def per_token(k, b, shape):
                v = r_all[:, k, bass.ds(2 * b, 2)]
                return (v.rearrange("p (t a) -> p t a", a=1) if len(shape) == 3 else
                        v.rearrange("p (t a c) -> p t a c", a=1, c=1)).to_broadcast(shape)

            def scale(b, q):
                dve.wait_ge(s_proj, b + 1)
                wait(dve, s_slot_hi, 3 * (b - 1))
                y = ps[0:TILE, Y:Y + 2, :]
                V.tensor_tensor(rope[q][:, :, 1, :, :].rearrange("p t a r -> p t (a r)"), y[:, :, 3 * D + 2 * ROT:PROJ_W],
                                per_token(0, b, [TILE, 2, 2 * ROT]), ALU.mult)
                for t in range(2):
                    r_q = r_all[:, 1, bass.ds(2 * b + t, 1)]
                    V.scalar_tensor_tensor(rope[q][:, t, 0, :, :].rearrange("p a r -> p (a r)"),
                                           y[:, t, 3 * D:3 * D + 2 * ROT], r_q, bias_row[:, 2 * D:],
                                           op0=ALU.mult, op1=ALU.add).then_inc(s_scaled, 1)
                for t in range(2):
                    r_q, r_kv = (r_all[:, k, bass.ds(2 * b + t, 1)] for k in (1, 2))
                    for side, r in ((0, r_q), (1, r_kv)):
                        V.scalar_tensor_tensor(x_tok[q][:, t, side, :, 0:DH],
                                               y[:, t, side * D:side * D + D].rearrange("p (h d) -> p h d", d=DH), r,
                                               bias_row[:, side * D:side * D + D].rearrange("p (h d) -> p h d", d=DH),
                                               op0=ALU.mult, op1=ALU.add)
                V.tensor_tensor(v_all[0:TILE, bass.ds(b, 1), :, :].rearrange("p b t d -> p (b t) d"),
                                y[:, :, 2 * D:3 * D], per_token(2, b, [TILE, 2, D]), ALU.mult).then_inc(s_v, 1)

            def neg_maximum(b, u, q):
                half, k = u % 2, u // 2
                dve.wait_ge(s_score, 6 * b + u + 1)
                if u == 0:
                    wait(dve, s_mt, b - 1)
                if k == 0:
                    dst, src = neg_max[q][:, 0, half, :], bank(S + half, TILE, 4 * TILE)
                else:
                    dst, src = neg_max[q][:, 1, half, 2 * k - 2:2 * k], bank(S + half, TILE, 2 * T)
                src = src.rearrange("p (a b) -> p a b", a=4 if k == 0 else 2)
                V.tensor_reduce(dst, src, AX.X, ALU.max, negate=True).then_inc(s_max, 1)

            def attention(s, p, live):
                q = 1 - p
                if live(3):
                    b = s - 3
                    for side in (1, 0):
                        dve.wait_ge(s_tr, 4 * b + 2 * (1 - side) + 2)
                        if side == 1:
                            wait(dve, s_st, 6 * (b - 1))
                        V.tensor_copy(stack[q][0:TW, side, :, TILE:],
                                      bank(TR[side] + 1, TW, 4 * TILE).rearrange("p (a b) -> p a b", a=4))\
                            .then_inc(s_tr_dve, 1)
                if live(4):
                    b = s - 4
                    dve.wait_ge(s_v, b + 1)
                    wait(dve, s_pv, b - 1)
                    V.tensor_copy(v_ones[p][:, :, :, 0:DH].rearrange("p t h d -> p (t h) d"),
                                  v_all[0:TILE, bass.ds(b, 1), :, :].rearrange("p b t (h d) -> p (b t h) d", d=DH))\
                        .then_inc(s_v_ones, 1)
                if live(2):
                    b = s - 2
                    dve.wait_ge(s_slot_hi, 3 * b + 1)
                    for side in range(2):
                        at = DQ * (2 - side)
                        V.tensor_tensor(slots[p][:, :, side, :, at:at + DQ], x_tok[p][:, :, side, :, :],
                                        slots[p][:, :, side, :, 0:DQ].bitcast(F32), ALU.subtract).then_inc(s_slot_lo, 1)
                if live(1):
                    scale(s - 1, q)
                if live(6):
                    b = s - 6
                    dve.wait_ge(s_wo, b + 1)
                    hb = h[:, bass.ds(b * T, T)]
                    V.scalar_tensor_tensor(hb, bank(M1, D, T), o_bias[:, :], hb, op0=ALU.add, op1=ALU.add)\
                        .then_inc(s_resid, 1)
                if live(3):
                    neg_maximum(s - 3, 0, q)
                    neg_maximum(s - 3, 1, q)
                if live(5):
                    b = s - 5
                    dve.wait_ge(s_ot, b + 1)
                    o = bank(M1, TILE, 512).rearrange("p (a c) -> p a c", c=32)
                    V.reciprocal(o_rec[q][:, :, :], o[:, :, DH:DH + 1]).then_inc(s_rec, 1)
                    dve.wait_ge(s_rec, b + 1)
                    wait(dve, s_nt, b - 1)
                    V.tensor_tensor(o_tok[q][:, :, :].rearrange("p t (a d) -> p (t a) d", d=DH), o[:, :, 0:DH],
                                    o_rec[q][:, :, :].to_broadcast([TILE, 16, DH]), ALU.mult).then_inc(s_o_norm, 1)
                if live(3):
                    neg_maximum(s - 3, 2, q)
                if live(3):
                    neg_maximum(s - 3, 3, q)
                if live(3):
                    neg_maximum(s - 3, 4, q)
                if live(3):
                    neg_maximum(s - 3, 5, q)
                if live(0) and not (isinstance(s, int) and s < 2):
                    split_low(s, p)

            pipeline(dve, B, 6, attention)

            def norm(s, k4, live):
                p, q = k4 % 2, 1 - k4 % 2
                if live(0):
                    if not isinstance(s, int) or s == 0:
                        dve.wait_ge(s_resid, B)
                    wait(dve, s_cen, s - 1)
                    V.tensor_copy(hn[p][:, :], h[:, bass.ds(s * CH, CH)]).then_inc(s_hn, 1)
                if live(3):
                    c = s - 3
                    dve.wait_ge(s_chain2, N_CHAIN * c + N_CHAIN)
                    wait(dve, s_xt, c - 1)
                    V.tensor_tensor(xn[q][:, :, :], bank(CEN[(k4 - 3) % 4], TILE, 4 * D).rearrange("p (a b) -> p a b", a=4),
                                    st2[q][:, 4, :].rearrange("p (a b) -> p a b", b=1).to_broadcast([TILE, 4, D]),
                                    ALU.mult).then_inc(s_xn, 1)
                if live(1):
                    c = s - 1
                    dve.wait_ge(s_sq2, c + 1)
                    V.tensor_reduce(st2[q][:, 0, :], sq2[q][:, :, :], AX.X, ALU.add).then_inc(s_var2, 1)
                if live(4):
                    c = s - 4
                    dve.wait_ge(s_xh, c + 1)
                    V.tensor_tensor(xl[:, bass.ds(c * CH, CH)], bank(XT + p, D, CH),
                                    xh[:, bass.ds(c * CH, CH)].bitcast(F32), ALU.subtract).then_inc(s_xl, 1)

            tiles = (slice(0, 4 * FIRST_CHUNKS), slice(4 * FIRST_CHUNKS, N_TILES))

            def router(part, ops):
                at = tiles[part]
                shape = [TILE, at.stop - at.start, EXPERTS]
                logits = bank(LOGIT, TILE, 512).rearrange("p (t e) -> p t e", e=EXPERTS)[:, at, :]
                t = [x[:, at, :] for x in rt]
                r = [rs[:, k, at] for k in range(6)]
                ranks = rank[:, :].rearrange("p (a e) -> p a e", a=1).to_broadcast(shape)

                def over(v):
                    return v.rearrange("p (t a) -> p t a", a=1).to_broadcast(shape)

                def first_largest(k, v, top, sel, tmp):
                    if k in ops:
                        link(V.tensor_reduce(top, v, AX.X, ALU.max), s_router)
                    if k + 1 in ops:
                        link(V.tensor_tensor(sel, v, over(top), ALU.is_equal), s_router)
                    if k + 2 in ops:
                        link(V.tensor_tensor(sel, sel, ranks, ALU.mult), s_router)
                    if k + 3 in ops:
                        link(V.tensor_reduce(tmp, sel, AX.X, ALU.max), s_router)
                    if k + 4 in ops:
                        link(V.tensor_tensor(sel, sel, over(tmp), ALU.is_equal), s_router)

                if 0 in ops:
                    link(V.tensor_reduce(r[0], logits, AX.X, ALU.max), s_router)
                if 1 in ops:
                    link(V.tensor_tensor(t[1], logits, over(r[0]), ALU.subtract), s_router)
                if 2 in ops:
                    dve.wait_ge(s_rexp, 1 if part == 0 else 3)
                    link(V.tensor_reduce(r[1], t[0], AX.X, ALU.add), s_router)
                if 3 in ops:
                    link(V.reciprocal(r[2], r[1]), s_router)
                if 4 in ops:
                    link(V.tensor_tensor(t[2], t[0], over(r[2]), ALU.mult), s_router)
                first_largest(5, t[2], r[0], t[3], r[1])
                if 10 in ops:
                    link(V.scalar_tensor_tensor(t[4], t[3], -2.0, t[2], op0=ALU.mult, op1=ALU.add), s_router)
                first_largest(11, t[4], r[2], t[5], r[1])
                if 16 in ops:
                    link(V.tensor_tensor(r[3], r[2], r[0], ALU.subtract), s_router)
                    assert count[s_router] == R_END * part + R_DIFF
                if 17 in ops:
                    dve.wait_ge(s_rexp, 2 if part == 0 else 4)
                    link(V.tensor_scalar(r[1], r[4], -0.5, 0.5, ALU.mult, ALU.add), s_router)
                if 18 in ops:
                    link(V.tensor_scalar(r[2], r[4], 0.5, 0.5, ALU.mult, ALU.add), s_router)
                if 19 in ops:
                    link(V.tensor_tensor(t[0], t[3], over(r[1]), ALU.mult), s_router)
                if 20 in ops:
                    link(V.tensor_tensor(t[1], t[5], over(r[2]), ALU.mult), s_router)
                if 21 in ops:
                    link(V.tensor_tensor(t[2], t[0], t[1], ALU.add), s_router)
                    assert count[s_router] == R_END * (part + 1)

            def norm_and_router(s, k4, live):
                norm(s, k4, live)
                if isinstance(s, int) and s == N_CH:
                    dve.wait_ge(s_logit, N_CH - 5)
                    router(0, range(0, R_EXP))
                if isinstance(s, int) and s == N_CH + 2:
                    router(0, range(R_EXP, 9))
                if isinstance(s, int) and s == N_CH + 3:
                    router(0, range(9, R_DIFF))

            pipeline(dve, N_CH, 6, norm_and_router, 4)
            router(0, range(R_DIFF, R_END))
            dve.wait_ge(s_logit, N_CH)
            router(1, range(0, R_EXP))
            dve.wait_ge(s_ct, 1)
            V.tensor_copy(comb_t[:, 0, :], bank(CT, 128, TILE)).then_inc(s_ct_out, 1)

            def split(n, e):
                dve.wait_ge(s_act_hi, n + 1)
                V.tensor_tensor(act_lo[e % 2][:, :, :], act_f[e % 2][:, :, :], act_hi[e % 2][:, :, :].bitcast(F32),
                                ALU.subtract).then_inc(s_split, 1)

            def weigh(n, e, c, p):
                dve.wait_ge(s_down, n + 1)
                wait(dve, s_total, n - 1)
                if e == 0:
                    dve.wait_ge(s_comb_in[p], 16 * (before(c, p) + 1))
                V.scalar_tensor_tensor(part[e % 2][:, :].rearrange("p (j i) -> p j i", j=4),
                                       bank(DOWN + e % 2, D, CH).rearrange("p (j i) -> p j i", j=4),
                                       be2[:, e:e + 1], comb[p][:, :, e, :], op0=ALU.add, op1=ALU.mult)\
                    .then_inc(s_part, 1)

            def unit(c, k, live):
                if live:
                    m = (k - LAG_W) % (2 * EXPERTS)
                    cc = c + (k - LAG_W) // EXPERTS
                    weigh(EXPERTS * c + k - LAG_W, m % EXPERTS, cc, m // EXPERTS)
                split(EXPERTS * c + k, k % EXPERTS)

            for k in range(2 * EXPERTS):
                unit(0, k, k >= LAG_W)
                if 1 <= k <= 8:
                    n = R_DIFF - R_EXP
                    router(1, range(R_EXP + n * (k - 1) // 8, R_EXP + n * k // 8))
                if 10 <= k <= 12:
                    router(1, range(R_DIFF, R_END - 2) if k == 10 else range(R_END - 13 + k, R_END - 12 + k))
            dve.wait_ge(s_ct, 2)
            V.tensor_copy(comb_t[:, 1:4, :], bank(CT, 128, 4 * TILE).rearrange("p (a b) -> p a b", a=4)[:, 1:4])\
                .then_inc(s_ct_out, 1)
            with dve.Fori(2, N_CH - 1, 2) as c:
                for k in range(2 * EXPERTS):
                    unit(c, k, True)
            for k in range(2 * EXPERTS - LAG_W, 2 * EXPERTS):
                weigh(EXPERTS * (N_CH - 2) + k, k % EXPERTS, N_CH - 1, 1)

        @block.tensor
        def _(pe):
            mm = nc.tensor.matmul

            def fold(stage):
                if stage == 0:
                    pe.wait_ge(s_weights, 16 * len(WEIGHTS))
                    pe.wait_ge(s_prep, N_PREP)
                    mm(bank(6, Q_PROJ, D), wdq[:, :], centre[:, :], start=True, stop=True)
                    mm(bank(6, KV_PROJ, D, D), wdkv[:, 0:KV_PROJ], centre[:, :], start=True, stop=True).then_inc(s_fold, 1)
                if stage == 1:
                    pe.wait_ge(s_prep, N_PREP + 2)
                    mm(bank(4, D, D), centre[:, :], eye[:, :], start=True, stop=True)
                    mm(bank(4, D, Q_PROJ, D), centre[:, :], wdq[:, :], start=True, stop=True)
                    mm(bank(4, D, KV_PROJ + 1, D + Q_PROJ), centre[:, :], wdkv[:, :], start=True, stop=True)
                    mm(bank(5, D, D), yq_t[:, :], wq_g[:, 0:D], start=True, stop=True)
                    mm(bank(5, D, 2 * D, D), yk_t[:, :], wk_g[:, :], start=True, stop=True)
                    mm(bank(5, D, 2 * ROT, 3 * D), yq_t[:, :], wq_g[:, D:], start=True, stop=True)
                    mm(bank(5, D, 2 * ROT, 3 * D + 2 * ROT), centre[:, :], wkr[:, :], start=True, stop=True)
                    mm(bank(7, TILE, D), bq_wide[:, :], wq_raw[:, 0:D], start=True, stop=True)
                    mm(bank(7, TILE, D, D), bkv_wide[:, :], wk_raw[:, 0:D], start=True, stop=True)
                    mm(bank(7, TILE, 2 * ROT, 2 * D), bq_wide[:, :], wq_raw[:, D:], start=True, stop=True)
                    mm(bank(7, D, 1, 300), wk_raw[:, D:], kv_gb[:, 1:2], start=True, stop=True).then_inc(s_fold, 1)
                if stage == 2:
                    pe.wait_ge(s_fold_lo, 1)
                    mm(bank(6, D, 1, 300), wo_t[:, :], v_bias[:, :], start=True, stop=True).then_inc(s_fold, 1)

            pe.wait_ge(s_conv_in, 16 * 2)

            def conv(c, k, wait_for):
                wait(pe, s_relu, wait_for)
                rhs = frames[:, bass.ds(c * 2 * T_IN, 2 * T_IN)].rearrange("p (b t) -> p b t", b=2)[:, :, 0:T]
                mm(bank(k, D, CH).rearrange("p (b t) -> p b t", b=2), conv_w[:, :], rhs, start=True, stop=True)\
                    .then_inc(s_conv, 1)

            chunks = N_CH // len(s_frames)
            for c in range(N_CH):
                if c % chunks == 0:
                    pe.wait_ge(s_frames[c // chunks], 16 * CTX)
                conv(c, c % 4, c - 3)
                if c in FOLD_AT:
                    fold(FOLD_AT.index(c))

            def three(dst, w_hi, w_lo, x_hi, x_lo, first=True, last=True):
                mm(dst, w_hi, x_hi, start=first, stop=False)
                mm(dst, w_hi, x_lo, start=False, stop=False)
                return mm(dst, w_lo, x_hi, start=False, stop=last)

            def stats(s, p, live):
                if live(2):
                    c = s - 2
                    pe.wait_ge(s_hs_lo, c + 1)
                    wait(pe, s_square, c - 1)
                    if isinstance(s, int) and c == 0:
                        pe.wait_ge(s_consts, 16 * len(CONSTS))
                        pe.wait_ge(s_fold_lo, 6)
                    for j in range(4):
                        t = slice(j * TILE, j * TILE + TILE)
                        last = three(bank(4 * p + j, TILE, STAT_W), hs_hi[p][:, t], hs_lo[p][:, t],
                                     stat_hi[:, :], stat_lo[:, :])
                    last.then_inc(s_stat, 1)

            pipeline(pe, N_CH, 4, stats)

            def score(b, u, p):
                half, k = u % 2, u // 2
                at, rows = SLOT * half, slice(SLOT * half, SLOT * half + STACK)
                wait(pe, s_max, 6 * b + u - 1)
                if k == 0:
                    dst = bank(S + half, TILE, 4 * TILE).rearrange("p (a b) -> p a b", a=4)
                    for j in range(4):
                        mm(dst[:, j], stack[p][rows, 0, j, 0:TILE], stack[p][rows, 1, j, 0:TILE],
                           start=j == 0, stop=False, skip_group_check=True)
                    mm(dst, eye_bf[:, :], mask[:, :, :], start=False, stop=True, skip_group_check=True)\
                        .then_inc(s_score, 1)
                else:
                    dst = bank(S + half, TILE, 2 * T).rearrange("p (a b) -> p a b", a=2)
                    for j in range(2):
                        m = 2 * k - 2 + j
                        mm(dst[:, j], stack[p][rows, 0, m, TILE:], stack[p][rows, 1, m, :],
                           start=j == 0, stop=False, skip_group_check=True)
                    mm(dst[:, :, TILE:], eye_bf[:, :], mask[:, 0:2, :], start=False, stop=True,
                       skip_group_check=True).then_inc(s_score, 1)

            def score_t(b, u, q):
                half, k = u % 2, u // 2
                rows = slice(SLOT * half, SLOT * half + STACK + 1)
                if u == 0:
                    pe.wait_ge(s_m_dma[q], 32 * (before(b, q) + 1))
                wait(pe, s_exp, 6 * b + u - 1)
                if k == 0:
                    dst = bank(P + half, TILE, 4 * TILE).rearrange("p (a b) -> p a b", a=4)
                    for j in range(4):
                        last = mm(dst[:, j], stack[q][rows, 1, j, TILE:], stack[q][rows, 0, j, TILE:],
                                  start=True, stop=True)
                else:
                    dst = bank(P + half, TILE, 2 * T).rearrange("p (a b) -> p a b", a=2)
                    for j in range(2):
                        m = 2 * k - 2 + j
                        last = mm(dst[:, j], stack[q][rows, 1, m, 0:TILE], stack[q][rows, 0, m, :],
                                  start=True, stop=True)
                last.then_inc(s_st, 1)

            def attention(s, p, live):
                q = 1 - p
                if live(3):
                    b = s - 3
                    pe.wait_ge(s_slot_hi, 3 * b + 3)
                    pe.wait_ge(s_slot_lo, 2 * b + 2)
                    wait(pe, s_o_out, b - 2)
                    wait(pe, s_o_norm, b - 2)
                    wait(pe, s_v, batches(b + 2, B))
                    for side in (1, 0):
                        for t in range(2):
                            for j in range(4):
                                src = slots[q][:, t, side, 2 * j:2 * j + 2, :].rearrange("p h d -> p (h d)")
                                last = mm(bank(TR[side] + t, D, TILE, j * TILE), src, eye_r[:, :], start=True, stop=True)
                            last.then_inc(s_tr, 1)
                if live(4):
                    b = s - 4
                    pe.wait_ge(s_max, 6 * b + 6)
                    for t in range(2):
                        last = nc.tensor.transpose(bank(S, HEADS, TILE, t * TILE),
                                                   neg_max[p][:, t, :, :].rearrange("p a b -> p (a b)"),
                                                   eye[0:TILE, 0:TILE])
                    last.then_inc(s_mt, 1)
                if live(6):
                    b = s - 6
                    pe.wait_ge(s_o_norm, b + 1)
                    for t in range(2):
                        last = nc.tensor.transpose(bank(S + 1, D, TILE, t * TILE), o_tok[p][:, t, :],
                                                   eye[0:TILE, 0:TILE])
                    last.then_inc(s_nt, 1)
                if live(1):
                    b = s - 1
                    pe.wait_ge(s_lo, b + 1)
                    if live(3):
                        pe.wait_ge(s_tr_act, 2 * (s - 3) + 1)
                        pe.wait_ge(s_tr_dve, 2 * (s - 3) + 1)
                    wait(pe, s_v, b)
                    for t in range(2):
                        tt = slice(t * TILE, t * TILE + TILE)
                        last = three(bank(Y + t, TILE, PROJ_W), hs_hi[q][:, tt], hs_lo[q][:, tt],
                                     proj_hi[:, :], proj_lo[:, :])
                    last.then_inc(s_proj, 1)
                if live(5):
                    b = s - 5
                    pe.wait_ge(s_masked, 2 * b + 2)
                    pe.wait_ge(s_v_ones, b + 1)
                    wait(pe, *((s_tr_act, 2 * (s - 3) + 2) if live(3) else (s_o_out, b)))
                    o = bank(M0, D, 2 * T).rearrange("p (g t) -> p g t", g=2)
                    for g in range(2):
                        for j in range(4):
                            mm(o[32 * j:32 * j + 32, g], v_ones[q][:, 0, 4 * g + j, :], p0[q][:, g, j, :],
                               start=g == 0, stop=False, skip_group_check=True)
                        for j in range(4):
                            last = mm(o[32 * j:32 * j + 32, g, TILE:], v_ones[q][:, 1, 4 * g + j, :],
                                      p1[q][:, g, j, :], start=False, stop=True, skip_group_check=True)
                    last.then_inc(s_pv, 1)
                if live(6):
                    b = s - 6
                    pe.wait_ge(s_nt_out, b + 1)
                    if live(3):
                        pe.wait_ge(s_tr_dve, 2 * (s - 3) + 2)
                    mm(bank(M1, D, T), wo_t[:, :], o_feat[p][:, :], start=True, stop=True).then_inc(s_wo, 1)
                if live(3):
                    pe.wait_ge(s_tr_act, 2 * (s - 3) + 2)
                    pe.wait_ge(s_tr_dve, 2 * (s - 3) + 2)
                    if live(4):
                        pe.wait_ge(s_mt_out, s - 3)
                    score(s - 3, 0, q)
                    if live(6):
                        pe.wait_ge(s_nt_out, s - 5)
                    score(s - 3, 1, q)
                for u in range(6):
                    if live(3) and u >= 2:
                        score(s - 3, u, q)
                    if live(4):
                        score_t(s - 4, u, p)
                    if u == 0 and live(5):
                        b = s - 5
                        pe.wait_ge(s_o_out, b + 1)
                        wait(pe, s_resid, b)
                        for t in range(2):
                            for g in range(2):
                                last = nc.tensor.transpose(bank(M1, TILE, D, (2 * t + g) * D),
                                                           o_sb[q][:, g, t * TILE:t * TILE + TILE], eye[:, :])
                        last.then_inc(s_ot, 1)

            pipeline(pe, B, 6, attention)

            def gate(s, k4, live):
                p, q = k4 % 2, 1 - k4 % 2
                if live(4):
                    c = s - 4
                    pe.wait_ge(s_xn, c + 1)
                    wait(pe, s_xl, c - 1)
                    for j in range(4):
                        last = nc.tensor.transpose(bank(XT + p, D, TILE, j * TILE), xn[p][:, j, :],
                                                   eye[0:TILE, 0:TILE])
                    last.then_inc(s_xt, 1)
                if live(5):
                    c = s - 5
                    pe.wait_ge(s_xl, c + 1)
                    wait(pe, s_gh, c)
                    three(bank(GATE, 64, CH), gw1_hi[:, :], gw1_lo[:, :], xh[:, bass.ds(c * CH, CH)],
                          xl[:, bass.ds(c * CH, CH)]).then_inc(s_gate, 1)
                if live(6):
                    c = s - 6
                    pe.wait_ge(s_gh, c + 1)
                    if not isinstance(s, int) or c < 2:
                        pe.wait_ge(s_pool_c, N_POOL_C)
                    if isinstance(s, int) and c == N_CH - 5:
                        pe.wait_ge(s_router, R_EXP)
                    for j in range(4):
                        last = mm(ps[0:TILE, LOGIT, bass.ds(4 * EXPERTS * c + EXPERTS * j, EXPERTS)],
                                  gh[p][:, j * TILE:j * TILE + TILE], gw2[:, :], start=True, stop=True)
                    last.then_inc(s_logit, 1)
                if live(0):
                    pe.wait_ge(s_hn, s + 1)
                    wait(pe, s_xn, s - 3)
                    for j in range(4):
                        last = mm(bank(CEN[k4], TILE, D, j * D), hn[p][:, j * TILE:j * TILE + TILE], centre[:, :],
                                  start=True, stop=True)
                    last.then_inc(s_cen, 1)

            pipeline(pe, N_CH, 6, gate, 4)

            def up(n, e, c):
                for half in range(2):
                    wait(pe, s_gelu, 2 * (n - 2) + half + 1)
                    cols = slice(half * D, half * D + D)
                    three(bank(UP + 2 * (e % 2) + half, D, CH), w1_hi[:, e, cols], w1_lo[:, e, cols],
                          xh[:, bass.ds(c * CH, CH)], xl[:, bass.ds(c * CH, CH)]).then_inc(s_up, 1)

            def down(n, e):
                wait(pe, s_part, n - 1)
                pe.wait_ge(s_split, n + 1)
                for half in range(2):
                    last = three(bank(DOWN + e % 2, D, CH), w2_hi[:, e, half, :], w2_lo[:, e, half, :],
                                 act_hi[e % 2][:, half, :], act_lo[e % 2][:, half, :], half == 0, half == 1)
                last.then_inc(s_down, 1)

            def unit(c, k, live):
                up(EXPERTS * c + k, k % EXPERTS, c + k // EXPERTS)
                if live:
                    down(EXPERTS * c + k - 2, (k - 2) % EXPERTS)

            def combine_t(part, blocks):
                pe.wait_ge(s_router, R_END * (part + 1))
                flat = rt[2][:, :, :].rearrange("p t e -> p (t e)")
                for j in blocks:
                    last = nc.tensor.transpose(bank(CT, 128, TILE, j * TILE), flat[:, 128 * j:128 * j + 128],
                                               eye[0:TILE, 0:TILE])
                last.then_inc(s_ct, 1)

            combine_t(0, range(0, 1))
            for k in range(2 * EXPERTS):
                unit(0, k, k >= 2)
                if k == 2 * EXPERTS - 1:
                    combine_t(1, range(1, 4))
            with pe.Fori(2, N_CH - 1, 2) as c:
                for k in range(2 * EXPERTS):
                    unit(c, k, True)
            for k in (EXPERTS - 2, EXPERTS - 1):
                down(EXPERTS * (N_CH - 1) + k, k)


def kernel(**inputs):
    import ml_dtypes
    import concourse.bacc as bacc
    from concourse.bass_utils import run_bass_kernel_spmd as run

    a = {n: np.asarray(v) for n, v in inputs.items()}
    t = {n[len("L0_attn_"):]: v for n, v in a.items() if n.startswith("L0_attn_")}
    f = {n[len("L0_ffn_"):]: v for n, v in a.items() if n.startswith("L0_ffn_")}
    pos = np.arange(T, dtype=np.float64).reshape(2, TILE).T[:, :, None]
    cos, sin = (np.broadcast_to(x, (TILE, 2, ROT)) for x in (np.cos(pos), np.sin(pos)))
    tri = np.where(np.arange(TILE)[None, :] <= np.arange(TILE)[:, None], 0.0, -3.0e38)
    arrays = {
        "x_t": a["x"].transpose(2, 0, 1).reshape(D_IN, B * T_IN),
        "conv_w": a["L0_tok_W"].T,
        "vecs": np.stack([a["L0_tok_b"], a["L0_tok_gamma"], a["L0_tok_beta"]], 1),
        "wdq": t["W_dq"], "wdkv": t["W_dkv"], "wuq": t["W_uq"], "wqr": t["W_qr"],
        "wukv": np.concatenate([t["W_ukv"][:, :D], t["W_ukv"][:, D:].reshape(KV_PROJ, 4, 2, DH)
                                .transpose(0, 2, 1, 3).reshape(KV_PROJ, D)], 1),
        "wkr": t["W_kr"],
        "wo_t": t["W_o"].T.reshape(4, 2, DH, D).transpose(1, 0, 2, 3).reshape(D, D),
        "q_gb": np.stack([t["q_ln_g"], t["q_ln_b"]], 1), "kv_gb": np.stack([t["kv_ln_g"], t["kv_ln_b"]], 1),
        "we1": f["we1"].transpose(1, 0, 2).reshape(D, EXPERTS * HID),
        "we2": f["we2"].reshape(EXPERTS, 2, D, D).transpose(2, 0, 1, 3).reshape(D, EXPERTS * HID),
        "be1": f["be1"].reshape(EXPERTS, 2, D).transpose(2, 0, 1), "be2": f["be2"].T,
        "gw1": f["gw1"], "gb1": f["gb1"][:, None], "gw2": np.concatenate([f["gw2"], f["gb2"][None]], 0),
        "eye": np.eye(128, dtype=np.float32),
        "centre": (np.eye(D) - 1.0 / D).astype(np.float32),
        "trig": np.concatenate([cos, sin, cos, sin], 2).astype(np.float32),
        "eye_bf": np.eye(TILE).astype(ml_dtypes.bfloat16),
        "mask": np.broadcast_to(tri[:, None, :], (TILE, 4, TILE)).astype(ml_dtypes.bfloat16),
        "rank": np.broadcast_to(np.arange(EXPERTS, 0, -1), (TILE, EXPERTS)).astype(np.float32),
    }
    nc = bacc.Bacc("TRN2", target_bir_lowering=False, num_devices=1)
    arrays = {f"in_{n}_dram": np.ascontiguousarray(v) for n, v in arrays.items()}
    aps = {n[3:-5]: nc.dram_tensor(n, v.shape, mybir.dt.from_np(v.dtype), kind="ExternalInput").ap()
           for n, v in arrays.items()}
    out = nc.dram_tensor("out_dram", (D, N_TOK), F32, kind="ExternalOutput").ap()
    build(nc, aps, out)
    r = run(nc, [arrays], core_ids=[0])
    return np.ascontiguousarray(np.asarray(r.results[0]["out_dram"]).T).reshape(B, T, D)
```
